# Optimizing a Trainium2 kernel written in Bass

```python
import numpy as np
import jax
import jax.numpy as jnp

def _softmax(x, axis=-1):
    return jax.nn.softmax(x, axis=axis)

def _gelu(x):
    return jax.nn.gelu(x, approximate=True)

def _silu(x):
    return jax.nn.silu(x)

def _sigmoid(x):
    return jax.nn.sigmoid(x)

def _layernorm(x, axis=-1, eps=1e-05):
    m = jnp.mean(x, axis=axis, keepdims=True)
    v = jnp.var(x, axis=axis, keepdims=True)
    return (x - m) / jnp.sqrt(v + eps)

def _scatter_add(tgt, idx, src, axis=0):
    return tgt.at[idx].add(src)

def _segment_sum(src, seg, n):
    return jax.ops.segment_sum(src, seg, n)
kernel_name = 'mk_lm_tower_d1_tok_ids512_r4_1b65d9'

def setup_inputs(seed: int=0):
    np.random.seed(seed)
    _w = jnp.asarray

    def _rec_inputs():
        import jax
        import jax.numpy as jnp
        _rk = jax.random.key(seed)
        x = jax.random.randint(jax.random.fold_in(_rk, 1), (16, 256), 0, 128, jnp.int32)
        return x
    x = _rec_inputs()

    def _L0_tok_setup():
        import jax, jax.numpy as jnp
        import numpy as np
        B, S, V, D, F = (8, 512, 128, 128, 512)

        def _pos_enc(seq_len, dim, dtype):
            pos = jnp.arange(seq_len, dtype=dtype)[:, None]
            i = jnp.arange(dim, dtype=dtype)[None, :]
            angle = pos / jnp.power(jnp.asarray(10000.0, dtype), 2.0 * i / dim)
            return jnp.where((jnp.arange(dim) % 2 == 0)[None, :], jnp.sin(angle), jnp.cos(angle))

        def _global_layernorm(t, gamma, beta):
            eps = 1e-09
            mean = jnp.mean(t)
            var = jnp.var(t, ddof=1)
            return gamma * ((t - mean) / (jnp.sqrt(var) + eps)) + beta
        key = jax.random.key(seed)
        ks = jax.random.split(key, 16)
        sc = 0.02
        return {'x': jax.random.randint(ks[0], (B, S), 0, V), 'emb': jax.random.normal(ks[1], (V, D), jnp.float32) * sc, 'Wq': jax.random.normal(ks[2], (D, D), jnp.float32) * sc, 'bq': jnp.zeros((D,), jnp.float32), 'Wk': jax.random.normal(ks[3], (D, D), jnp.float32) * sc, 'bk': jnp.zeros((D,), jnp.float32), 'Wv': jax.random.normal(ks[4], (D, D), jnp.float32) * sc, 'bv': jnp.zeros((D,), jnp.float32), 'Wo': jax.random.normal(ks[5], (D, D), jnp.float32) * sc, 'bo': jnp.zeros((D,), jnp.float32), 'W1': jax.random.normal(ks[6], (D, F), jnp.float32) * sc, 'b1': jnp.zeros((F,), jnp.float32), 'W2': jax.random.normal(ks[7], (F, D), jnp.float32) * sc, 'b2': jnp.zeros((D,), jnp.float32), 'gamma': jnp.ones((D,), jnp.float32), 'beta': jnp.zeros((D,), jnp.float32)}
    _L0_tok_all = _L0_tok_setup()
    _L0_tok_in = {k: v for k, v in _L0_tok_all.items() if k in ('emb', 'Wq', 'bq', 'Wk', 'bk', 'Wv', 'bv', 'Wo', 'bo', 'W1', 'b1', 'W2', 'b2', 'gamma', 'beta')}
    del _L0_tok_all

    def _L0_attn_setup():
        import jax, jax.numpy as jnp
        import numpy as np
        B, T, D, K, V = (4, 1024, 128, 128, 128)
        key = jax.random.key(seed)
        ks = jax.random.split(key, 7)
        w = lambda k, shp: jax.random.normal(k, shp, dtype=jnp.float32) * 0.02
        return {'minibatch': jax.random.normal(ks[0], (B, T, D), dtype=jnp.float32), 'Wk': w(ks[1], (D, K)), 'bk': jnp.zeros((K,), jnp.float32), 'Wq': w(ks[2], (D, K)), 'bq': jnp.zeros((K,), jnp.float32), 'Wv': w(ks[3], (D, V)), 'bv': jnp.zeros((V,), jnp.float32)}
    _L0_attn_all = _L0_attn_setup()
    _L0_attn_in = {k: v for k, v in _L0_attn_all.items() if k in ('Wk', 'bk', 'Wq', 'bq', 'Wv', 'bv')}
    del _L0_attn_all

    def _L0_ffn_setup():
        import jax, jax.numpy as jnp
        import numpy as np
        B, S, D, F, E = (8, 1024, 128, 512, 8)
        INIT_LAMBDA = 0.2
        LN_EPS = 1e-05
        LN_MERGE = 0.03
        key = jax.random.key(seed)
        ks = jax.random.split(key, 12)
        n = lambda k, shp, s=1.0: jax.random.normal(k, shp, dtype=jnp.float32) * s
        return {'hidden_states': n(ks[0], (B, S, D)), 'gfc1_w': n(ks[1], (D, D), 0.01), 'gfc1_b': jnp.zeros((D,), jnp.float32), 'gfc2_w': n(ks[2], (E, D), 0.01), 'gfc2_b': jnp.full((E,), INIT_LAMBDA, dtype=jnp.float32), 'W1': n(ks[3], (F, D), 0.02), 'b1': jnp.zeros((F,), jnp.float32), 'W2': n(ks[4], (D, F), 0.02), 'b2': jnp.zeros((D,), jnp.float32), 'ln_g': jnp.ones((D,), jnp.float32), 'ln_b': jnp.zeros((D,), jnp.float32), 'tv_W1': n(ks[5], (E, F, D), 0.02), 'tv_b1': n(ks[6], (E, F), 0.02), 'tv_W2': n(ks[7], (E, D, F), 0.02), 'tv_b2': n(ks[8], (E, D), 0.02), 'tv_ln_g': n(ks[9], (E, D), 0.02), 'tv_ln_b': n(ks[10], (E, D), 0.02)}
    _L0_ffn_all = _L0_ffn_setup()
    _L0_ffn_in = {k: v for k, v in _L0_ffn_all.items() if k in ('gfc1_w', 'gfc1_b', 'gfc2_w', 'gfc2_b', 'W1', 'b1', 'W2', 'b2', 'ln_g', 'ln_b', 'tv_W1', 'tv_b1', 'tv_W2', 'tv_b2', 'tv_ln_g', 'tv_ln_b')}
    del _L0_ffn_all
    return {'x': x, 'L0_tok_emb': _L0_tok_in['emb'], 'L0_tok_Wq': _L0_tok_in['Wq'], 'L0_tok_bq': _L0_tok_in['bq'], 'L0_tok_Wk': _L0_tok_in['Wk'], 'L0_tok_bk': _L0_tok_in['bk'], 'L0_tok_Wv': _L0_tok_in['Wv'], 'L0_tok_bv': _L0_tok_in['bv'], 'L0_tok_Wo': _L0_tok_in['Wo'], 'L0_tok_bo': _L0_tok_in['bo'], 'L0_tok_W1': _L0_tok_in['W1'], 'L0_tok_b1': _L0_tok_in['b1'], 'L0_tok_W2': _L0_tok_in['W2'], 'L0_tok_b2': _L0_tok_in['b2'], 'L0_tok_gamma': _L0_tok_in['gamma'], 'L0_tok_beta': _L0_tok_in['beta'], 'L0_attn_Wk': _L0_attn_in['Wk'], 'L0_attn_bk': _L0_attn_in['bk'], 'L0_attn_Wq': _L0_attn_in['Wq'], 'L0_attn_bq': _L0_attn_in['bq'], 'L0_attn_Wv': _L0_attn_in['Wv'], 'L0_attn_bv': _L0_attn_in['bv'], 'L0_ffn_gfc1_w': _L0_ffn_in['gfc1_w'], 'L0_ffn_gfc1_b': _L0_ffn_in['gfc1_b'], 'L0_ffn_gfc2_w': _L0_ffn_in['gfc2_w'], 'L0_ffn_gfc2_b': _L0_ffn_in['gfc2_b'], 'L0_ffn_W1': _L0_ffn_in['W1'], 'L0_ffn_b1': _L0_ffn_in['b1'], 'L0_ffn_W2': _L0_ffn_in['W2'], 'L0_ffn_b2': _L0_ffn_in['b2'], 'L0_ffn_ln_g': _L0_ffn_in['ln_g'], 'L0_ffn_ln_b': _L0_ffn_in['ln_b'], 'L0_ffn_tv_W1': _L0_ffn_in['tv_W1'], 'L0_ffn_tv_b1': _L0_ffn_in['tv_b1'], 'L0_ffn_tv_W2': _L0_ffn_in['tv_W2'], 'L0_ffn_tv_b2': _L0_ffn_in['tv_b2'], 'L0_ffn_tv_ln_g': _L0_ffn_in['tv_ln_g'], 'L0_ffn_tv_ln_b': _L0_ffn_in['tv_ln_b']}

def reference(x, L0_tok_emb, L0_tok_Wq, L0_tok_bq, L0_tok_Wk, L0_tok_bk, L0_tok_Wv, L0_tok_bv, L0_tok_Wo, L0_tok_bo, L0_tok_W1, L0_tok_b1, L0_tok_W2, L0_tok_b2, L0_tok_gamma, L0_tok_beta, L0_attn_Wk, L0_attn_bk, L0_attn_Wq, L0_attn_bq, L0_attn_Wv, L0_attn_bv, L0_ffn_gfc1_w, L0_ffn_gfc1_b, L0_ffn_gfc2_w, L0_ffn_gfc2_b, L0_ffn_W1, L0_ffn_b1, L0_ffn_W2, L0_ffn_b2, L0_ffn_ln_g, L0_ffn_ln_b, L0_ffn_tv_W1, L0_ffn_tv_b1, L0_ffn_tv_W2, L0_ffn_tv_b2, L0_ffn_tv_ln_g, L0_ffn_tv_ln_b):
    import jax
    import jax.numpy as jnp

    def _L0_tok_ref(x, emb, Wq, bq, Wk, bk, Wv, bv, Wo, bo, W1, b1, W2, b2, gamma, beta):
        import jax, jax.numpy as jnp
        import numpy as np
        B, S, V, D, F = (8, 512, 128, 128, 512)

        def _pos_enc(seq_len, dim, dtype):
            pos = jnp.arange(seq_len, dtype=dtype)[:, None]
            i = jnp.arange(dim, dtype=dtype)[None, :]
            angle = pos / jnp.power(jnp.asarray(10000.0, dtype), 2.0 * i / dim)
            return jnp.where((jnp.arange(dim) % 2 == 0)[None, :], jnp.sin(angle), jnp.cos(angle))

        def _global_layernorm(t, gamma, beta):
            eps = 1e-09
            mean = jnp.mean(t)
            var = jnp.var(t, ddof=1)
            return gamma * ((t - mean) / (jnp.sqrt(var) + eps)) + beta
        h = emb[x]
        x1 = h + _pos_enc(h.shape[1], h.shape[2], h.dtype)[None]
        q = x1 @ Wq + bq
        k = x1 @ Wk + bk
        v = x1 @ Wv + bv
        scores = jnp.einsum('bqd,bkd->bqk', q, k) / jnp.sqrt(jnp.asarray(512.0, h.dtype))
        attn = jax.nn.softmax(scores, axis=-1)
        x2 = jnp.einsum('bqk,bkd->bqd', attn, v) @ Wo + bo
        x3 = _global_layernorm(x1 + x2, gamma, beta)
        x4 = jax.nn.relu(x3 @ W1 + b1) @ W2 + b2
        return _global_layernorm(x3 + x4, gamma, beta)

    def _L0_attn_ref(minibatch, Wk, bk, Wq, bq, Wv, bv):
        import jax, jax.numpy as jnp
        import numpy as np
        B, T, D, K, V = (4, 1024, 128, 128, 128)
        keys = minibatch @ Wk + bk
        queries = minibatch @ Wq + bq
        values = minibatch @ Wv + bv
        logits = jnp.einsum('btk,bsk->bts', queries, keys)
        t = logits.shape[1]
        mask = jnp.triu(jnp.ones((t, t), dtype=bool), k=1)
        logits = jnp.where(mask[None, :, :], -jnp.inf, logits)
        sqrt_k = jnp.asarray(np.sqrt(K), dtype=logits.dtype)
        probs = jax.nn.softmax(logits, axis=1) / sqrt_k
        read = jnp.einsum('bts,bsv->btv', probs, values)
        return minibatch + read

    def _L0_ffn_ref(hidden_states, gfc1_w, gfc1_b, gfc2_w, gfc2_b, W1, b1, W2, b2, ln_g, ln_b, tv_W1, tv_b1, tv_W2, tv_b2, tv_ln_g, tv_ln_b):
        import jax, jax.numpy as jnp
        import numpy as np
        B, S, D, F, E = (8, 1024, 128, 512, 8)
        INIT_LAMBDA = 0.2
        LN_EPS = 1e-05
        LN_MERGE = 0.03
        x = hidden_states
        gh = jax.nn.relu(jnp.einsum('bsd,hd->bsh', x, gfc1_w) + gfc1_b)
        g = (jnp.einsum('bsh,eh->bse', gh, gfc2_w) + gfc2_b).mean(axis=1)
        W1m = W1 + jnp.einsum('be,efd->bfd', g, tv_W1)
        b1m = b1 + g @ tv_b1
        W2m = W2 + jnp.einsum('be,edf->bdf', g, tv_W2)
        b2m = b2 + g @ tv_b2
        lng = ln_g + LN_MERGE * (tv_ln_g - ln_g).sum(axis=0)
        lnb = ln_b + LN_MERGE * (tv_ln_b - ln_b).sum(axis=0)
        h = jax.nn.relu(jnp.einsum('bsd,bfd->bsf', x, W1m) + b1m[:, None, :])
        out = jnp.einsum('bsf,bdf->bsd', h, W2m) + b2m[:, None, :]
        res = x + out
        mu = res.mean(axis=-1, keepdims=True)
        var = res.var(axis=-1, keepdims=True)
        return (res - mu) * jax.lax.rsqrt(var + LN_EPS) * lng + lnb
    h = _L0_tok_ref(x, L0_tok_emb, L0_tok_Wq, L0_tok_bq, L0_tok_Wk, L0_tok_bk, L0_tok_Wv, L0_tok_bv, L0_tok_Wo, L0_tok_bo, L0_tok_W1, L0_tok_b1, L0_tok_W2, L0_tok_b2, L0_tok_gamma, L0_tok_beta)
    h = h + _L0_attn_ref(_layernorm(h, axis=-1), L0_attn_Wk, L0_attn_bk, L0_attn_Wq, L0_attn_bq, L0_attn_Wv, L0_attn_bv)
    h = h + _L0_ffn_ref(_layernorm(h, axis=-1), L0_ffn_gfc1_w, L0_ffn_gfc1_b, L0_ffn_gfc2_w, L0_ffn_gfc2_b, L0_ffn_W1, L0_ffn_b1, L0_ffn_W2, L0_ffn_b2, L0_ffn_ln_g, L0_ffn_ln_b, L0_ffn_tv_W1, L0_ffn_tv_b1, L0_ffn_tv_W2, L0_ffn_tv_b2, L0_ffn_tv_ln_g, L0_ffn_tv_ln_b)
    return h

_drawn_inputs = setup_inputs


def setup_inputs(seed=0):
    import zlib

    import numpy as np

    out = dict(_drawn_inputs(seed))
    spreads = {'L0_tok_bq': (0.0, 2.0),
     'L0_tok_bk': (0.0, 2.0),
     'L0_tok_bv': (0.0, 0.1),
     'L0_tok_bo': (0.0, 0.1),
     'L0_tok_b1': (0.0, 0.285),
     'L0_tok_b2': (0.0, 0.1),
     'L0_tok_gamma': (1.0, 0.2),
     'L0_tok_beta': (0.0, 0.1),
     'L0_attn_bk': (0.0, 0.8),
     'L0_attn_bq': (0.0, 2.0),
     'L0_attn_bv': (0.0, 0.8),
     'L0_ffn_gfc1_b': (0.0, 0.8),
     'L0_ffn_gfc2_b': (0.20000000298023224, 0.6),
     'L0_ffn_b1': (0.0, 0.8),
     'L0_ffn_b2': (0.0, 2.0),
     'L0_ffn_ln_g': (1.0, 0.2),
     'L0_ffn_ln_b': (0.0, 0.332)}
    factors = {'L0_tok_Wq': 64.0,
     'L0_tok_Wk': 64.0,
     'L0_attn_Wk': 8.0,
     'L0_attn_Wq': 8.0,
     'L0_attn_Wv': 5.065,
     'L0_ffn_gfc1_w': 8.0,
     'L0_ffn_gfc2_w': 8.0,
     'L0_ffn_W1': 2.835,
     'L0_ffn_tv_W1': 5.142,
     'L0_ffn_tv_b1': 8.0,
     'L0_ffn_tv_W2': 4.552,
     'L0_ffn_tv_b2': 42.59,
     'L0_ffn_tv_ln_g': 64.0,
     'L0_ffn_tv_ln_b': 64.0}
    for name, (base, spread) in spreads.items():
        noise = np.random.default_rng([zlib.crc32(name.encode()), seed]).standard_normal(out[name].shape)
        drawn = base * np.exp(spread * noise) if base else spread * noise
        out[name] = jnp.asarray(drawn.astype(out[name].dtype))
    for name, factor in factors.items():
        out[name] = (out[name] * factor).astype(out[name].dtype)
    return out
```

```python
import math
from contextlib import ExitStack

import numpy as np

import concourse.bass as bass
from concourse import mybir

F32 = mybir.dt.float32
F32R = mybir.dt.float32r
BF16 = mybir.dt.bfloat16
I32 = mybir.dt.int32
ALU = mybir.AluOpType
ACT = mybir.ActivationFunctionType
AX = mybir.AxisListType

P = 128
MASKED = -1.0e30

C_PE = 0
C_PET = 256
C_ID = 512
C_AVG = 640
C_DIAG = 768
C_IOTA = 784
C_MERGE = 785
C_COLS = 913


def shape_constants(tokens, features):
    pos = np.arange(tokens, dtype=np.float32)[:, None]
    i = np.arange(features, dtype=np.float32)[None, :]
    angle = pos / np.power(np.float32(10000.0), np.float32(2.0) * i / np.float32(features))
    pe = np.where((np.arange(features) % 2 == 0)[None, :], np.sin(angle), np.cos(angle))
    pe = pe.astype(np.float32)
    c = np.zeros((P, C_COLS), np.float32)
    c[:, C_PE:C_PE + 256] = pe.reshape(2, P, features).transpose(1, 0, 2).reshape(P, 256)
    c[:, C_PET:C_PET + 256] = pe.T
    c[:, C_ID:C_ID + P] = np.eye(P)
    c[:, C_AVG:C_AVG + P] = 1.0 / P
    c[:, C_DIAG:C_DIAG + 16] = np.arange(P)[:, None] % 16 == np.arange(16)[None, :]
    c[:, C_IOTA] = np.arange(P)
    c[:, C_MERGE:C_MERGE + P] = 0.03
    return c


def build(nc, a, out):
    NB, T = a["x"].shape
    V, D = a["L0_tok_emb"].shape
    FF = a["L0_tok_W1"].shape[1]
    E = a["L0_ffn_tv_W1"].shape[0]
    NT = NB * T
    FCH = FF // P
    X = P // E
    CH = 512
    NCH = NT // CH
    assert (D, V, T, NB, E, FF) == (P, P, 2 * P, 16, 8, 512)
    TOK_SCALE = 1.0 / math.sqrt(512.0)
    INV_SQRT_K = 1.0 / math.sqrt(float(D))
    LN_EPS = 1e-5
    STD_EPS = 1e-9
    COUNT = NT * D

    with ExitStack() as ctx:
        def sb(name, shape, dt=F32):
            return ctx.enter_context(nc.sbuf_tensor(name, shape, dt))

        def sem(name):
            return ctx.enter_context(nc.semaphore(name))

        cst = sb("cst", [P, C_COLS])
        z_all = sb("z_all", [P, NT])
        onehot = sb("onehot", [P, 2, T], F32R)
        x13 = sb("x13", [P, NB, T])
        res2 = sb("res2", [P, NB, T])
        mT = sb("mT", [P, NB, T])
        w1m = sb("w1m", [P, NB, FF])
        w2m = sb("w2m", [P, NB, FCH, D])
        tv1 = sb("tv1", [P, FF // X, D])
        tv2 = sb("tv2", [P, D // X, FF])
        xv_all = w1m
        early = res2[:].rearrange("p b t -> p (b t)")
        mats = lambda o, k: early[:, o * D:(o + k) * D].rearrange("p (k d) -> p k d", k=k)
        emb, embT, wvT, bvbc, bo_bc = (early[:, k * D:(k + 1) * D] for k in range(5))
        wtok = mats(5, 4)
        wpre = mats(9, 3)
        tab = mats(12, 4)
        w1s = early[:, 16 * D:20 * D]
        fw1 = mats(20, FCH)
        fw2 = early[:, 24 * D:28 * D]
        tvd, tvln = (early[0:E, o * D:(o + 2) * D].rearrange("e (k d) -> e k d", k=2) for o in (28, 30))
        early_b = mT[:].rearrange("p b t -> p (b t)")
        w2s = early_b[:, 0:FF].rearrange("p (c d) -> p c d", c=FCH)
        c_qk = early_b[:, 512:1024].rearrange("p (k t) -> p k t", k=2)
        c_xv = early_b[:, 1024:1536].rearrange("p (k j d) -> p k j d", k=2, j=2)
        gw1 = early_b[:, 1536:1664]
        lnp = early_b[:, 1664:1920].rearrange("p (k d) -> p k d", k=2)
        gw2 = early_b[0:E, 1920:2048]
        w1b = tv1[:, 0:8, :].rearrange("p (u c) d -> p u (c d)", u=2)
        free = w2m[:].rearrange("p b c d -> p (b c d)")
        two = lambda o, n: free[:, o:o + 2 * n].rearrange("p (k n) -> p k n", k=2)
        hid = free[:, 0:4 * 512].rearrange("p (f n) -> p f n", f=4)
        x3f = two(2048, 512)
        hT = two(3072, T)
        n_s = two(3584, T)
        nT = two(4096, T)
        v_s = two(4608, T)
        vp_s = two(5120, T)
        gjunk = free[:, 5632:5632 + T]
        probT = free[:, 6144:6144 + 4 * T].rearrange("p (u k t) -> p u k t", u=2, k=2)
        b2m = z_all[:, 0:NB * D].rearrange("p (b d) -> p b d", b=NB)
        gbc = z_all[0:E, NB * D:2 * NB * D].rearrange("p (b d) -> p b d", b=NB)
        hid2 = z_all[:, NB * D:2 * NB * D].rearrange("p (u f t) -> p u f t", u=2, f=4)

        tab_hi = sb("tab_hi", [P, 4, D], F32R)
        tab_lo = sb("tab_lo", [P, 4, D], F32R)
        tcol = sb("tcol", [P, 6])
        tb1 = sb("tb1", [P, FCH])
        w1_hi = sb("w1_hi", [P, FF], F32R)
        w1_lo = sb("w1_lo", [P, FF], F32R)
        aw = sb("aw", [P, 3, D])
        acol = sb("acol", [P, 2])
        abv = sb("abv", [P, 2, D])
        gw1T = sb("gw1T", [P, D])
        gw2T = sb("gw2T", [P, E])
        gw2x = sb("gw2x", [P, E, X])
        gcol = sb("gcol", [P, 2])
        gb2 = sb("gb2", [E, 1])
        fw1T = sb("fw1T", [P, FF])
        fw2T = sb("fw2T", [P, FCH, D])
        fb1 = sb("fb1", [P, FCH])
        fb2 = sb("fb2", [P, D])
        tvb1 = sb("tvb1", [E, FF])
        tvb2 = sb("tvb2", [E, D])
        lng = sb("lng", [P, 2, D])
        maskT = sb("maskT", [P, P], BF16)
        ident_b = sb("ident_b", [P, P], BF16)
        nhalf = sb("nhalf", [P, 4])

        qk_s = sb("qk_s", [P, 2, 2, T])
        prob = sb("prob", [P, 2, 2, T])
        x13_s = sb("x13_s", [P, 2, T])
        r_s = qk_s[:, :, 0, :]
        ln_s = qk_s[:, :, 1, :]
        o_s = prob[:, :, 0, :]
        nmax = sb("nmax", [P, 2, 2])
        rmax = sb("rmax", [P, 2, 2])
        psums = sb("psums", [P, 2, 2])
        rsum = sb("rsum", [P, 2, 2])
        stats = sb("stats", [P, NB, 6])
        gstat = sb("gstat", [P, 12])
        gaff = sb("gaff", [P, 4])

        x3_hi = sb("x3_hi", [P, 2, CH], F32R)
        x3_lo = sb("x3_lo", [P, 2, CH], F32R)

        bn1 = sb("bn1", [P, 2, 2, 6])
        mv1 = sb("mv1", [P, 2, 2, 2])
        ve1 = sb("ve1", [P, 2, 2])
        rs1 = sb("rs1", [P, 2, 2])
        nm1 = sb("nm1", [P, 2, 2])
        bn2 = sb("bn2", [P, 2, 2, 6])
        mv2 = sb("mv2", [P, 2, 2, 2])
        ve2 = sb("ve2", [P, 2, 2])
        rs2 = sb("rs2", [P, 2, 2])
        nm2 = sb("nm2", [P, 2, 2])
        ghsum = sb("ghsum", [P, NB])
        gT = sb("gT", [E, NB])
        grep = sb("grep", [P, NB])
        gdiag = sb("gdiag", [P, NB, X])
        b1m = sb("b1m", [P, FCH, NB])

        bank = [ctx.enter_context(nc.psum_tensor(f"bank{i}", [P, 512], F32)) for i in range(8)]

        ld_const, ld_ids, ld_tok, ld_ffn, ld_attn, ld_gate, ld_merge, ld_tv = (
            sem(n) for n in ("ld_const", "ld_ids", "ld_tok", "ld_ffn", "ld_attn", "ld_gate",
                             "ld_merge", "ld_tv"))
        prep_pe, prep_dve, prep_pool, onehot_ready = (
            sem(n) for n in ("prep_pe", "prep_dve", "prep_pool", "onehot_ready"))
        qk_gathered, xv_gathered, qk_copied, xv_copied = (
            sem(n) for n in ("qk_gathered", "xv_gathered", "qk_copied", "xv_copied"))
        scores_ready, rmax_ready, nmax_ready, probs_ready = (
            sem(n) for n in ("scores_ready", "rmax_ready", "nmax_ready", "probs_ready"))
        probs_turned, probT_ready, av_ready, rsum_ready, x13_ready = (
            sem(n) for n in ("probs_turned", "probT_ready", "av_ready", "rsum_ready", "x13_ready"))
        stat_dve, stat_own, stat_dve_bn, stat_pe, stat_pool, affine_ready, pool_const = (
            sem(n) for n in ("stat_dve", "stat_own", "bn_ready", "stat_pe", "stat_pool", "affine_ready",
                             "pool_const"))
        x13_turned, x13T_copied, x3_full, x3_hi_ready, x3_lo_ready = (
            sem(n) for n in ("x13_turned", "x13T_copied", "x3_full", "x3_hi_ready", "x3_lo_ready"))
        hid_ready, relu_act, relu_dve, x4_ready, z_ready = (
            sem(n) for n in ("hid_ready", "relu_act", "relu_dve", "x4_ready", "z_ready"))
        hT_ready, h_turned, bn1_ready, aggr1_ready, var1_ready, rstd1_ready = (
            sem(n) for n in ("hT_ready", "h_turned", "bn1_ready", "aggr1_ready", "var1_ready",
                             "rstd1_ready"))
        shift1_ready, n_ready, hn_ready, n_turned, nT_ready = (
            sem(n) for n in ("shift1_ready", "n_ready", "hn_ready", "n_turned", "nT_ready"))
        qkv_ready, qk2_copied, v_copied, logits_ready = (
            sem(n) for n in ("qkv_ready", "qk2_copied", "v_copied", "logits_ready"))
        cmax_ready, ncmax_ready, cprobs_ready, csum_ready, vp_ready, read_ready = (
            sem(n) for n in ("cmax_ready", "ncmax_ready", "cprobs_ready", "csum_ready", "vp_ready",
                             "read_ready"))
        h2_ready, bn2_ready, aggr2_ready, var2_ready, rstd2_ready, shift2_ready = (
            sem(n) for n in ("h2_ready", "bn2_ready", "aggr2_ready", "var2_ready", "rstd2_ready",
                             "shift2_ready"))
        m_ready, m_kept, m_turned, mT_ready, gate_ready, gate_summed = (
            sem(n) for n in ("m_ready", "m_kept", "m_turned", "mT_ready", "gate_ready", "gate_summed"))
        g_pe, g_dve, merged_pe, merged_dve = (
            sem(n) for n in ("g_pe", "g_dve", "merged_pe", "merged_dve"))
        hid2_ready, w1b_ready, relu2_act, relu2_dve, out_ready, mb_ready, hlb_ready = (
            sem(n) for n in ("hid2_ready", "w1b_ready", "relu2_act", "relu2_dve", "out_ready", "mb_ready",
                             "hlb_ready"))
        res_ready, bn3_ready, aggr3_ready, var3_ready, rstd3_ready, scaled_ready, o_ready = (
            sem(n) for n in ("res_ready", "bn3_ready", "aggr3_ready", "var3_ready", "rstd3_ready",
                             "scaled_ready", "o_ready"))
        stored = [sem("stored_even"), sem("stored_odd")]

        ident = cst[:, C_ID:C_ID + P]
        avg = cst[:, C_AVG:C_AVG + P]
        ids = z_all[:].bitcast(I32)
        IDQ = NT // 4

        def x13c(c):
            return x13[:].rearrange("p b t -> p (b t)")[:, bass.ds(c * CH, CH)]

        def pipeline(eng, step, n, lag, unroll):
            head = -(-(lag + 2) // unroll) * unroll
            for i in range(head):
                step(i, i % unroll)
            with eng.Fori(head // unroll, n // unroll) as trip:
                for j in range(unroll):
                    step(trip * unroll + j, j)
            for i in range(n, n + lag):
                step(i, i % unroll)

        def on(i, lag, n):
            return not isinstance(i, int) or 0 <= i - lag < n

        def after(eng, s, count):
            if not isinstance(count, int) or count > 0:
                eng.wait_ge(s, count)

        def held_until(eng, s, count):
            after(eng, s, count)
            eng.nop(nofuse=True)

        block = ctx.enter_context(nc.Block())

        @block.sync
        def _(sp):
            col = lambda v: v.rearrange("(p o) -> p o", o=1)
            row = lambda v, n=P: v.rearrange("(o d) -> o d", o=1).broadcast_to([n, v.shape[0]])
            idrow = a["x"].rearrange("b t -> (b t)")
            sp.dma_start(cst[:], a["constants"]).then_inc(ld_const, 16)
            sp.dma_start(emb, a["L0_tok_emb"]).then_inc(ld_tok, 16)
            for k, w in enumerate(("Wq", "Wk", "Wv", "Wo")):
                sp.dma_start(wtok[:, k, :], a[f"L0_tok_{w}"]).then_inc(ld_tok, 16)
            for k, w in enumerate(("bq", "bk", "bv", "b2", "gamma", "beta")):
                sp.dma_start(tcol[:, k:k + 1], col(a[f"L0_tok_{w}"])).then_inc(ld_tok, 16)
            sp.dma_start(bo_bc, row(a["L0_tok_bo"])).then_inc(ld_tok, 16)
            for k in range(4):
                sp.dma_start(ids[:, k * IDQ:(k + 1) * IDQ], row(idrow[k * IDQ:(k + 1) * IDQ]))\
                    .then_inc(ld_ids, 16)
            sp.dma_start(w1s, a["L0_tok_W1"]).then_inc(ld_ffn, 16)
            sp.dma_start(w2s, a["L0_tok_W2"].rearrange("(c p) d -> p c d", p=P)).then_inc(ld_ffn, 16)
            for c in range(FCH):
                sp.dma_start(tb1[:, c:c + 1], col(a["L0_tok_b1"][c * P:(c + 1) * P])).then_inc(ld_ffn, 16)
            for k, w in enumerate(("Wq", "Wk", "Wv")):
                sp.dma_start(aw[:, k, :], a[f"L0_attn_{w}"]).then_inc(ld_attn, 16)
            for k, w in enumerate(("bq", "bk")):
                sp.dma_start(acol[:, k:k + 1], col(a[f"L0_attn_{w}"])).then_inc(ld_attn, 16)
            for k in range(2):
                sp.dma_start(abv[:, k, :], row(a["L0_attn_bv"])).then_inc(ld_attn, 16)
            sp.dma_start(gw1, a["L0_ffn_gfc1_w"]).then_inc(ld_gate, 16)
            sp.dma_start(gw2, a["L0_ffn_gfc2_w"]).then_inc(ld_gate, 16)
            sp.dma_start(gcol[:, 0:1], col(a["L0_ffn_gfc1_b"])).then_inc(ld_gate, 16)
            sp.dma_start(gb2[:], col(a["L0_ffn_gfc2_b"])).then_inc(ld_gate, 16)
            for e in range(E):
                sp.dma_start(gcol[e * X:(e + 1) * X, 1:2],
                             a["L0_ffn_gfc2_b"][e:e + 1].rearrange("(o d) -> o d", o=1).broadcast_to([X, 1]))\
                    .then_inc(ld_gate, 16)
            sp.dma_start(fw1, a["L0_ffn_W1"].rearrange("(c p) d -> p c d", p=P)).then_inc(ld_merge, 16)
            sp.dma_start(fw2, a["L0_ffn_W2"]).then_inc(ld_merge, 16)
            for c in range(FCH):
                sp.dma_start(fb1[:, c:c + 1], col(a["L0_ffn_b1"][c * P:(c + 1) * P])).then_inc(ld_merge, 16)
            sp.dma_start(fb2[:], row(a["L0_ffn_b2"])).then_inc(ld_merge, 16)
            sp.dma_start(tvb1[:], a["L0_ffn_tv_b1"]).then_inc(ld_merge, 16)
            sp.dma_start(tvb2[:], a["L0_ffn_tv_b2"]).then_inc(ld_merge, 16)
            for k, w in enumerate(("g", "b")):
                sp.dma_start(lnp[:, k, :], row(a[f"L0_ffn_ln_{w}"])).then_inc(ld_merge, 16)
                sp.dma_start(tvln[:, k, :], a[f"L0_ffn_tv_ln_{w}"]).then_inc(ld_merge, 16)
            for e in range(E):
                sp.dma_start(tv1[e * X:(e + 1) * X, :, :],
                             a["L0_ffn_tv_W1"][e].rearrange("(c x) d -> x c d", x=X)).then_inc(ld_tv, 16)
                sp.dma_start(tv2[e * X:(e + 1) * X, :, :],
                             a["L0_ffn_tv_W2"][e].rearrange("(c x) f -> x c f", x=X)).then_inc(ld_tv, 16)

            def store(b, par):
                after(sp, o_ready, b + 1)
                sp.dma_start(out[b].rearrange("(k p) d -> p k d", p=P),
                             o_s[:, par, :].rearrange("p (k d) -> p k d", k=2)).then_inc(stored[par], 16)

            with sp.Fori(0, NB // 2) as pair:
                store(pair * 2, 0)
                store(pair * 2 + 1, 1)
            for par in range(2):
                sp.wait_ge(stored[par], 8 * NB)

        @block.tensor
        def _(pe):
            pe.wait_ge(ld_const, 16)
            pe.wait_ge(ld_tok, 16 * 12)
            pe.transpose(bank[0][:, 0:P], emb, ident)
            pe.transpose(bank[0][:, P:2 * P], wtok[:, 2, :], ident).then_inc(prep_pe, 1)
            pe.wait_ge(prep_dve, 1)
            pe.matmul(bank[1][:, 0:D], wvT, wtok[:, 3, :], start=True, stop=True).then_inc(prep_pe, 1)
            pe.wait_ge(prep_dve, 2)
            pe.matmul(bank[2][:, 0:3 * D], embT, wpre.rearrange("p k d -> p (k d)"),
                      start=True, stop=True).then_inc(prep_pe, 1)
            for k in range(2):
                mm = pe.matmul(bank[3][:, k * T:(k + 1) * T], wtok[:, k, :], cst[:, C_PET:C_PET + T],
                               start=True, stop=True)
            mm.then_inc(prep_pe, 1)
            for k in range(2):
                pe.matmul(bank[4][:, k * D:(k + 1) * D], cst[:, C_PET + k * P:C_PET + (k + 1) * P],
                          wpre[:, 2, :], start=True, stop=False)
                mm = pe.matmul(bank[4][:, k * D:(k + 1) * D], bvbc, wtok[:, 3, :],
                               start=False, stop=True)
            mm.then_inc(prep_pe, 1)
            pe.wait_ge(prep_dve, 6)

            qk_b, xv_b, s_b, t_b, av_b, xt_b = bank[0:2], bank[2], bank[4:6], bank[6], bank[7], bank[3]

            def step_a(i, par):
                if on(i, 1, NB):
                    b, pb = i - 1, (par + 1) % 2
                    after(pe, onehot_ready, b + 1)
                    oh = onehot[:, pb, :]
                    after(pe, qk_copied, b - 1)
                    for k in range(2):
                        pe.matmul(qk_b[pb][:, k * T:(k + 1) * T], tab_hi[:, k, :], oh, start=True, stop=False)
                        mm = pe.matmul(qk_b[pb][:, k * T:(k + 1) * T], tab_lo[:, k, :], oh,
                                       start=False, stop=True)
                    mm.then_inc(qk_gathered, 1)
                    after(pe, xv_copied, b)
                    for k in range(2):
                        ohk = onehot[:, pb, k * P:(k + 1) * P]
                        pe.matmul(xv_b[:, k * T:(k + 1) * T], ohk,
                                  tab_hi[:, 2:4, :].rearrange("p k d -> p (k d)"), start=True, stop=False)
                        mm = pe.matmul(xv_b[:, k * T:(k + 1) * T], ohk,
                                       tab_lo[:, 2:4, :].rearrange("p k d -> p (k d)"), start=False, stop=True)
                    mm.then_inc(xv_gathered, 1)
                if on(i, 2, NB):
                    b, pb = i - 2, par
                    after(pe, qk_copied, b + 1)
                    after(pe, probs_ready, b - 1)
                    for q in range(2):
                        mm = pe.matmul(s_b[pb][:, q * T:(q + 1) * T], qk_s[:, pb, 0, q * P:(q + 1) * P],
                                       qk_s[:, pb, 1, :], start=True, stop=True)
                    mm.then_inc(scores_ready, 1)
                if on(i, 3, NB):
                    b, pb = i - 3, (par + 1) % 2
                    after(pe, probs_ready, b + 1)
                    after(pe, probT_ready, b)
                    for k in range(2):
                        for q in range(2):
                            mm = pe.transpose(t_b[:, (2 * k + q) * P:(2 * k + q + 1) * P],
                                              prob[:, pb, q, k * P:(k + 1) * P], ident)
                    mm.then_inc(probs_turned, 1)
                if on(i, 4, NB):
                    b, pb = i - 4, par
                    after(pe, probT_ready, b + 1)
                    after(pe, x13_ready, b)
                    for q in range(2):
                        for k in range(2):
                            mm = pe.matmul(av_b[:, q * P:(q + 1) * P], probT[:, pb, k, q * P:(q + 1) * P],
                                           xv_all[:, b, k * T + P:k * T + 2 * P],
                                           start=(k == 0), stop=(k == 1))
                    mm.then_inc(av_ready, 1)
                if on(i, 5, NB):
                    b, pb = i - 5, (par + 1) % 2
                    after(pe, x13_ready, b + 1)
                    after(pe, x13T_copied, b)
                    for k in range(2):
                        mm = pe.transpose(xt_b[:, k * P:(k + 1) * P], x13_s[:, pb, k * P:(k + 1) * P], ident)
                    mm.then_inc(x13_turned, 1)

            pipeline(pe, step_a, NB, 5, 2)

            def global_mean(r):
                pe.wait_ge(stat_dve, 3 * r + 1)
                pe.matmul(bank[7][:, 0:1], avg, gstat[:, 0:1], start=True, stop=True).then_inc(stat_pe, 1)
                pe.wait_ge(stat_dve, 3 * r + 2)
                pe.matmul(bank[7][:, 1:2], avg, gstat[:, 4:5], start=True, stop=True).then_inc(stat_pe, 1)

            global_mean(0)

            h_b, x4_b = bank[2:6], bank[6:8]

            def step_b(c, par):
                pe.wait_ge(x3_hi_ready, c + 1)
                pe.wait_ge(x3_lo_ready, c + 1)
                for f in range(FCH):
                    after(pe, (relu_act, relu_dve)[f % 2], 2 * c - 1 + f // 2)
                    w = slice(f * P, (f + 1) * P)
                    pe.matmul(h_b[f][:], w1_hi[:, w], x3_hi[:, par, :], start=True, stop=False)
                    pe.matmul(h_b[f][:], w1_lo[:, w], x3_hi[:, par, :], start=False, stop=False)
                    pe.matmul(h_b[f][:], w1_hi[:, w], x3_lo[:, par, :], start=False, stop=True)\
                        .then_inc(hid_ready, 1)
                after(pe, z_ready, c - 1)
                for f in range(FCH):
                    after(pe, (relu_act, relu_dve)[f % 2], 2 * c + 1 + f // 2)
                    mm = pe.matmul(x4_b[par][:], w2s[:, f, :], hid[:, f, :],
                                   start=(f == 0), stop=(f == FCH - 1))
                mm.then_inc(x4_ready, 1)

            pe.wait_ge(prep_pool, 2)
            pe.wait_ge(ld_ffn, 16 * 6)
            for c in range(2):
                step_b(c, c)
            with pe.Fori(1, NCH // 2 - 1) as pair:
                step_b(pair * 2, 0)
                step_b(pair * 2 + 1, 1)
            for c in range(NCH - 2, NCH):
                step_b(c, c % 2)
            global_mean(1)

            pe.wait_ge(ld_gate, 16 * (4 + E))
            pe.wait_ge(ld_merge, 16 * 13)
            pe.transpose(bank[0][:, 0:P], gw1, ident)
            pe.transpose(bank[0][:, P:P + E], gw2, cst[0:E, C_ID:C_ID + E])
            for c in range(FCH):
                pe.transpose(bank[1][:, c * P:(c + 1) * P], fw1[:, c, :], ident)
                mm = pe.transpose(bank[2][:, c * P:(c + 1) * P], fw2[:, c * P:(c + 1) * P], ident)
            mm.then_inc(prep_pe, 1)
            pe.wait_ge(prep_dve, 7)
            pe.matmul(bank[3][:, 0:2 * D], cst[0:E, C_MERGE:C_MERGE + P],
                      tvd.rearrange("e k d -> e (k d)"), start=True, stop=True).then_inc(prep_pe, 1)
            pe.wait_ge(prep_dve, 8)
            pe.wait_ge(ld_attn, 16 * 7)

            h_b, t2_b, t3_b, qk_b, v_b, l_b, r_b, g_b = bank

            def step_c(i, par):
                other = (par + 1) % 2
                if on(i, 0, NB):
                    after(pe, hT_ready, i + 1)
                    after(pe, hn_ready, i)
                    for k in range(2):
                        mm = pe.transpose(h_b[:, k * P:(k + 1) * P], hT[:, par, k * P:(k + 1) * P], ident)
                    mm.then_inc(h_turned, 1)
                if on(i, 1, NB):
                    b = i - 1
                    after(pe, n_ready, b + 1)
                    after(pe, nT_ready, b)
                    for k in range(2):
                        mm = pe.transpose(t2_b[:, k * P:(k + 1) * P], n_s[:, other, k * P:(k + 1) * P], ident)
                    mm.then_inc(n_turned, 1)
                if on(i, 3, NB):
                    b, pb = i - 3, other
                    after(pe, vp_ready, b + 1)
                    after(pe, h2_ready, b)
                    pr = prob[:, pb].rearrange("p k t -> p (k t)")
                    pe.matmul(r_b[:, 0:P], pr[:, 0:P], vp_s[:, pb, 0:P], start=True, stop=True)
                    pe.matmul(r_b[:, P:T], pr[:, P:T], vp_s[:, pb, 0:P], start=True, stop=False)
                    pe.matmul(r_b[:, P:T], pr[:, T:T + P], vp_s[:, pb, P:T], start=False, stop=True)\
                        .then_inc(read_ready, 1)
                if on(i, 4, NB):
                    b = i - 4
                    after(pe, m_ready, b + 1)
                    after(pe, mT_ready, b)
                    for k in range(2):
                        mm = pe.transpose(t3_b[:, k * P:(k + 1) * P], x13_s[:, par, k * P:(k + 1) * P], ident)
                    mm.then_inc(m_turned, 1)
                if on(i, 2, NB):
                    b, pb = i - 2, par
                    after(pe, qk2_copied, b + 1)
                    after(pe, cprobs_ready, b)
                    pe.matmul(l_b[:, 0:T], qk_s[:, pb, 1, 0:P], qk_s[:, pb, 0, :], start=True, stop=False,
                              skip_group_check=True)
                    pe.matmul(l_b[:, T:T + P], qk_s[:, pb, 1, P:T], qk_s[:, pb, 0, P:T],
                              start=False, stop=False, skip_group_check=True)
                    pe.matmul(l_b[:, 0:P], ident_b[:], maskT[:], start=False, stop=False,
                              skip_group_check=True)
                    pe.matmul(l_b[:, T:T + P], ident_b[:], maskT[:], start=False, stop=True,
                              skip_group_check=True).then_inc(logits_ready, 1)
                if on(i, 1, NB):
                    b, pb = i - 1, other
                    after(pe, nT_ready, b + 1)
                    after(pe, qk2_copied, b)
                    after(pe, v_copied, b)
                    for k in range(2):
                        pe.matmul(qk_b[:, k * T:(k + 1) * T], aw[:, k, :], nT[:, pb, :], start=True, stop=True)
                    for k in range(2):
                        mm = pe.matmul(v_b[:, k * P:(k + 1) * P], nT[:, pb, k * P:(k + 1) * P], aw[:, 2, :],
                                       start=True, stop=True)
                    mm.then_inc(qkv_ready, 1)
                if on(i, 4, NB):
                    b = i - 4
                    after(pe, mT_ready, b + 1)
                    after(pe, gate_summed, b)
                    pe.matmul(g_b[:, 0:T], gw1T[:], mT[:, b, :], start=True, stop=True).then_inc(gate_ready, 1)

            pipeline(pe, step_c, NB, 4, 2)

            pe.wait_ge(gate_summed, NB)
            pe.matmul(bank[7][:, 0:NB], gw2x[:].rearrange("p e x -> p (e x)"), ghsum[:], start=True, stop=True)
            pe.matmul(bank[7][0:E, NB:2 * NB], gw2T[:], ghsum[:], start=True, stop=True).then_inc(g_pe, 1)
            pe.wait_ge(g_dve, 2)
            pe.wait_ge(ld_tv, 16 * 2 * E)

            def merge(p, bk, count):
                after(pe, merged_dve, count - 3)
                for j in range(2):
                    blk = 2 * p + j
                    if bk == "w1":
                        lhsT = tv1[:, blk, :]
                    else:
                        lhsT = tv2[:, blk // FCH, (blk % FCH) * P:(blk % FCH + 1) * P]
                    mm = pe.matmul(bank[count % 4][:, j * T:(j + 1) * T], lhsT,
                                   gdiag[:].rearrange("p b x -> p (b x)"), start=True, stop=True)
                mm.then_inc(merged_pe, 1)

            for p in range(16):
                merge(p, "w1", p)
            pe.wait_ge(g_dve, 3)
            for c in range(FCH):
                mm = pe.matmul(bank[6][:, c * NB:(c + 1) * NB], tvb1[:, c * P:(c + 1) * P], gT[:],
                               start=True, stop=True)
            mm.then_inc(g_pe, 1)
            for q in range(4):
                after(pe, g_dve, 4 + q - 1 if q > 1 else 0)
                for b in range(4):
                    mm = pe.matmul(bank[4 + q % 2][:, b * P:(b + 1) * P], gbc[:, 4 * q + b, :], tvb2[:],
                                   start=True, stop=True)
                mm.then_inc(g_pe, 1)
            for p in range(16):
                merge(p, "w2", 16 + p)

            h_b, o_b = bank[0:4], bank[6:8]
            pe.wait_ge(merged_dve, 32)
            pe.wait_ge(g_dve, 8)

            def step_d(i, par):
                other = (par + 1) % 2
                if on(i, 0, NB):
                    after(pe, w1b_ready, i + 1)
                    for f in range(FCH):
                        after(pe, (relu2_act, relu2_dve)[f // 2], 2 * (i - 1))
                        mm = pe.matmul(h_b[2 * par + f // 2][:, (f % 2) * T:(f % 2 + 1) * T],
                                       w1b[:, par, f * P:(f + 1) * P], mT[:, i, :], start=True, stop=True)
                        if f % 2 == 1:
                            mm.then_inc(hid2_ready, 1)
                if on(i, 1, NB):
                    b, pb = i - 1, other
                    after(pe, res_ready, b - 1)
                    after(pe, relu2_act, 2 * (b + 1))
                    after(pe, relu2_dve, 2 * (b + 1))
                    for k in range(2):
                        for f in range(FCH):
                            mm = pe.matmul(o_b[pb][:, k * P:(k + 1) * P], hid2[:, pb, f, k * P:(k + 1) * P],
                                           w2m[:, b, f, :], start=(f == 0), stop=(f == FCH - 1))
                    mm.then_inc(out_ready, 1)

            pipeline(pe, step_d, NB, 1, 2)

        @block.scalar
        def _(act):
            def step_a(i, par):
                if on(i, 2, NB):
                    b, pb = i - 2, par
                    after(act, nmax_ready, b + 1)
                    after(act, probs_turned, b - 1)
                    for q in range(2):
                        ins = act.activation(prob[:, pb, q, :], bank[4 + pb][:, q * T:(q + 1) * T], ACT.Exp,
                                             bias=nmax[:, pb, q:q + 1], scale=TOK_SCALE,
                                             accum_out=psums[:, pb, q:q + 1])
                    ins.then_inc(probs_ready, 1)
                if on(i, 3, NB):
                    b, pb = i - 3, (par + 1) % 2
                    after(act, probs_turned, b + 1)
                    after(act, av_ready, b - 1)
                    act.activation(probT[:, pb].rearrange("p k q -> p (k q)"), bank[6][:], ACT.Copy)\
                        .then_inc(probT_ready, 1)
                if on(i, 5, NB):
                    b = i - 5
                    after(act, x13_turned, b + 1)
                    act.activation(x13[:, b, :], bank[3][:, 0:T], ACT.Copy).then_inc(x13T_copied, 1)

            pipeline(act, step_a, NB, 5, 2)

            def norm_hi(c, par):
                after(act, hid_ready, 4 * (c - 1))
                act.activation(x3_hi[:, par, :], x13c(c), ACT.Identity, bias=gaff[:, 1:2],
                               scale=gaff[:, 0:1]).then_inc(x3_hi_ready, 1)

            def step_b(c, par):
                for f in (0, 2):
                    after(act, hid_ready, 4 * c + f + 1)
                    after(act, x4_ready, c)
                    act.activation(hid[:, f, :], bank[2 + f][:], ACT.Relu, bias=tb1[:, f:f + 1])\
                        .then_inc(relu_act, 1)
                if on(c, 0, NCH - 1):
                    norm_hi(c + 1, (par + 1) % 2)

            act.wait_ge(affine_ready, 1)
            act.wait_ge(ld_ffn, 16 * 6)
            norm_hi(0, 0)
            for c in range(2):
                step_b(c, c)
            with act.Fori(1, NCH // 2 - 1) as pair:
                step_b(pair * 2, 0)
                step_b(pair * 2 + 1, 1)
            for c in range(NCH - 2, NCH):
                step_b(c, c % 2)

            act.wait_ge(affine_ready, 2)
            act.wait_ge(ld_attn, 16 * 7)
            act.wait_ge(ld_gate, 16 * (4 + E))
            h_b, t2_b, t3_b, qk_b, v_b, l_b, r_b, g_b = bank

            def step_c(i, par):
                other = (par + 1) % 2
                if on(i, 0, NB):
                    after(act, h_turned, i - 1)
                    act.activation(hT[:, par, :], z_all[:, bass.ds(i * T, T)], ACT.Identity,
                                   bias=gaff[:, 3:4], scale=gaff[:, 2:3]).then_inc(hT_ready, 1)
                if on(i, 1, NB):
                    b, pb = i - 1, other
                    after(act, n_turned, b + 1)
                    after(act, qkv_ready, b - 1)
                    act.activation(nT[:, pb, :], t2_b[:, 0:T], ACT.Copy).then_inc(nT_ready, 1)
                if on(i, 4, NB):
                    b = i - 4
                    after(act, m_turned, b + 1)
                    act.activation(mT[:, b, :], t3_b[:, 0:T], ACT.Copy).then_inc(mT_ready, 1)
                if on(i, 2, NB):
                    b, pb = i - 2, par
                    after(act, ncmax_ready, b + 1)
                    after(act, read_ready, b - 1)
                    pr = prob[:, pb].rearrange("p k t -> p (k t)")
                    act.activation(pr[:, 0:T], l_b[:, 0:T], ACT.Exp, bias=nmax[:, pb, 0:1],
                                   accum_out=psums[:, pb, 0:1])
                    act.activation(pr[:, T:T + P], l_b[:, T:T + P], ACT.Exp, bias=nmax[:, pb, 1:2],
                                   accum_out=psums[:, pb, 1:2]).then_inc(cprobs_ready, 1)
                if on(i, 0, NB):
                    after(act, shift1_ready, i + 1)
                    after(act, n_turned, i - 1)
                    for k in range(2):
                        ins = act.activation(n_s[:, par, k * P:(k + 1) * P], h_b[:, k * P:(k + 1) * P],
                                             ACT.Identity, bias=nm1[:, par, k:k + 1], scale=rs1[:, par, k:k + 1])
                    ins.then_inc(n_ready, 1)
                if on(i, 1, NB):
                    b, pb = i - 1, other
                    after(act, qkv_ready, b + 1)
                    after(act, logits_ready, b - 1)
                    for k in range(2):
                        ins = act.activation(qk_s[:, pb, k, :], qk_b[:, k * T:(k + 1) * T], ACT.Identity,
                                             bias=acol[:, k:k + 1])
                    ins.then_inc(qk2_copied, 1)
                if on(i, 3, NB):
                    b, pb = i - 3, other
                    after(act, shift2_ready, b + 1)
                    after(act, m_turned, b - 1)
                    after(act, m_kept, b - 1)
                    for k in range(2):
                        ins = act.activation(x13_s[:, pb, k * P:(k + 1) * P], res2[:, b, k * P:(k + 1) * P],
                                             ACT.Identity, bias=nm2[:, pb, k:k + 1], scale=rs2[:, pb, k:k + 1])
                    ins.then_inc(m_ready, 1)
                if on(i, 4, NB):
                    b = i - 4
                    after(act, gate_ready, b + 1)
                    act.activation(gjunk, g_b[:, 0:T], ACT.Relu, bias=gcol[:, 0:1],
                                   accum_out=ghsum[:, bass.ds(b, 1)]).then_inc(gate_summed, 1)

            pipeline(act, step_c, NB, 4, 2)

            act.wait_ge(g_dve, 4)

            def load_w1(b, par):
                after(act, hid2_ready, 2 * (b - 1))
                act.activation(w1b[:, par, :], w1m[:, b, :], ACT.Copy).then_inc(w1b_ready, 1)

            act.wait_ge(merged_dve, 32)
            load_w1(0, 0)

            def step_d(i, par):
                if on(i, 0, NB - 1):
                    load_w1(i + 1, (par + 1) % 2)
                for f in range(2):
                    after(act, hid2_ready, 2 * i + 1)
                    after(act, out_ready, i - 1)
                    act.activation(hid2[:, par, f, :], bank[2 * par][:, f * T:(f + 1) * T], ACT.Relu,
                                   bias=b1m[:, f, bass.ds(i, 1)]).then_inc(relu2_act, 1)

            for i in range(2):
                step_d(i, i)
            with act.Fori(1, NB // 2 - 1) as pair:
                step_d(pair * 2, 0)
                step_d(pair * 2 + 1, 1)
            for i in range(NB - 2, NB):
                step_d(i, i % 2)

        @block.vector
        def _(dve):
            add, mult, sub = ALU.add, ALU.mult, ALU.subtract
            flat = lambda t: t.rearrange("p k d -> p (k d)")
            dve.wait_ge(ld_const, 16)
            dve.wait_ge(ld_tok, 16 * 12)
            dve.wait_ge(prep_pe, 1)
            dve.tensor_copy(embT, bank[0][:, 0:P])
            dve.tensor_copy(wvT, bank[0][:, P:2 * P]).then_inc(prep_dve, 1)
            dve.tensor_copy(bvbc, tcol[:, 2:3].to_broadcast([P, P]))
            dve.tensor_copy(wpre[:, 0:2, :], wtok[:, 0:2, :])
            dve.wait_ge(prep_pe, 2)
            dve.tensor_copy(wpre[:, 2, :], bank[1][:, 0:D]).then_inc(prep_dve, 1)
            dve.tensor_copy(tab[:, 2, :], emb)
            dve.wait_ge(prep_pe, 3)
            dve.tensor_copy(tab[:, 0:2, :], bank[2][:, 0:2 * D].rearrange("p (k d) -> p k d", k=2))
            dve.tensor_copy(tab[:, 3, :], bank[2][:, 2 * D:3 * D]).then_inc(prep_dve, 1)
            dve.wait_ge(prep_dve, 3)
            dve.tensor_copy(tab_hi[:], tab).then_inc(prep_dve, 1)
            dve.wait_ge(prep_dve, 4)
            dve.tensor_tensor(tab_lo[:], tab, tab_hi[:].bitcast(F32), sub).then_inc(prep_dve, 1)
            dve.wait_ge(prep_pe, 4)
            for k in range(2):
                dve.tensor_scalar(c_qk[:, k, :], bank[3][:, k * T:(k + 1) * T], tcol[:, k:k + 1], None, add)
            dve.wait_ge(prep_pe, 5)
            for k in range(2):
                dve.tensor_tensor(c_xv[:, k, 0, :], cst[:, C_PE + k * P:C_PE + (k + 1) * P], bo_bc, add)
                ins = dve.tensor_copy(c_xv[:, k, 1, :], bank[4][:, k * D:(k + 1) * D])
            ins.then_inc(prep_dve, 1)
            dve.wait_ge(ld_ids, 16 * 4)

            dve.wait_ge(prep_dve, 6)

            def step_a(i, par):
                other = (par + 1) % 2
                if on(i, 4, NB):
                    b, pb = i - 4, par
                    after(dve, probs_ready, b + 1)
                    dve.reciprocal(rsum[:, pb, :], psums[:, pb, :]).then_inc(rsum_ready, 1)
                if on(i, 0, NB):
                    after(dve, xv_gathered, i - 1)
                    dve.tensor_scalar(onehot[:, par, :], ids[:, bass.ds(i * T, T)],
                                      cst[:, C_IOTA:C_IOTA + 1], None, ALU.is_equal).then_inc(onehot_ready, 1)
                if on(i, 1, NB):
                    b, pb = i - 1, other
                    after(dve, qk_gathered, b + 1)
                    after(dve, scores_ready, b - 1)
                    dve.tensor_tensor(qk_s[:, pb].rearrange("p k t -> p (k t)"), bank[pb][:],
                                      flat(c_qk), add).then_inc(qk_copied, 1)
                    after(dve, xv_gathered, b + 1)
                    dve.tensor_tensor(xv_all[:, b, :], bank[2][:],
                                      c_xv.rearrange("p k j d -> p (k j d)"), add).then_inc(xv_copied, 1)
                if on(i, 2, NB):
                    b, pb = i - 2, par
                    after(dve, scores_ready, b + 1)
                    after(dve, nmax_ready, b - 1)
                    dve.tensor_reduce(rmax[:, pb, :], bank[4 + pb][:].rearrange("p (q k) -> p q k", q=2),
                                      AX.X, ALU.max).then_inc(rmax_ready, 1)
                    after(dve, rmax_ready, b + 1)
                    after(dve, probs_ready, b - 1)
                    dve.tensor_scalar(nmax[:, pb, :], rmax[:, pb, :], -TOK_SCALE, None, mult)\
                        .then_inc(nmax_ready, 1)
                if on(i, 4, NB):
                    b, pb = i - 4, par
                    after(dve, rsum_ready, b + 1)
                    after(dve, xv_copied, b + 1)
                    after(dve, av_ready, b + 1)
                    after(dve, x13_turned, b - 1)
                    for q in range(2):
                        ins = dve.scalar_tensor_tensor(x13_s[:, pb, q * P:(q + 1) * P], bank[7][:, q * P:(q + 1) * P],
                                                       rsum[:, pb, q:q + 1], xv_all[:, b, q * T:q * T + P],
                                                       mult, add)
                    ins.then_inc(x13_ready, 1)
                    held_until(dve, x13_ready, b + 1)
                    dve.bn_stats(stats[:, b, :], x13_s[:, pb, :]).then_inc(stat_dve_bn, 1)

            def global_affine(r, n, gcols):
                s = gaff[:, 2 * r:2 * r + 1]
                bn_base = NB * (1 if r else 0)
                dve.wait_ge(stat_dve_bn, bn_base + n)
                dve.bn_aggr(gstat[:, 0:2], stats[:, 0:n, :].rearrange("p b s -> p (b s)")).then_inc(stat_dve, 1)
                dve.wait_ge(stat_pe, 2 * r + 1)
                dve.tensor_copy(gstat[:, 2:3], bank[7][:, 0:1]).then_inc(stat_own, 1)
                dve.wait_ge(stat_dve, 3 * r + 1)
                dve.wait_ge(stat_own, 6 * r + 1)
                dve.tensor_tensor(gstat[:, 3:4], gstat[:, 0:1], gstat[:, 2:3], sub).then_inc(stat_own, 1)
                dve.wait_ge(stat_own, 6 * r + 2)
                dve.scalar_tensor_tensor(gstat[:, 4:5], gstat[:, 3:4], gstat[:, 3:4], gstat[:, 1:2], mult, add)\
                    .then_inc(stat_dve, 1)
                dve.wait_ge(stat_pe, 2 * r + 2)
                dve.tensor_scalar(gstat[:, 5:6], bank[7][:, 1:2], COUNT / (COUNT - 1.0), None, mult)\
                    .then_inc(stat_dve, 1)
                dve.wait_ge(stat_pool, r + 1)
                dve.tensor_scalar(gstat[:, 7:8], gstat[:, 6:7], STD_EPS, None, add).then_inc(stat_own, 1)
                dve.wait_ge(stat_own, 6 * r + 3)
                dve.reciprocal(gstat[:, 8:9], gstat[:, 7:8]).then_inc(stat_own, 1)
                dve.wait_ge(stat_own, 6 * r + 4)
                dve.tensor_scalar(s, tcol[:, 4:5], gstat[:, 8:9], None, mult).then_inc(stat_own, 1)
                dve.wait_ge(stat_own, 6 * r + 5)
                dve.tensor_scalar(gstat[:, 9:10], gstat[:, 2:3], -1.0, None, mult).then_inc(stat_own, 1)
                dve.wait_ge(stat_own, 6 * r + 6)
                dve.scalar_tensor_tensor(gaff[:, 2 * r + 1:2 * r + 2], gstat[:, 9:10], s, tcol[:, 5:6], mult, add)\
                    .then_inc(affine_ready, 1)
                dve.wait_ge(affine_ready, r + 1)

            pipeline(dve, step_a, NB, 4, 2)
            global_affine(0, NB, None)

            def norm_full(c, par):
                after(dve, x3_lo_ready, c - 1)
                dve.tensor_scalar(x3f[:, par, :], x13c(c), gaff[:, 0:1], gaff[:, 1:2], mult, add)\
                    .then_inc(x3_full, 1)

            def step_b(c, par):
                for f in (1, 3):
                    after(dve, hid_ready, 4 * c + f + 1)
                    after(dve, x4_ready, c)
                    dve.tensor_scalar(hid[:, f, :], bank[2 + f][:], tb1[:, f:f + 1], 0.0, add, ALU.max)\
                        .then_inc(relu_dve, 1)
                if on(c, 0, NCH - 1):
                    norm_full(c + 1, (par + 1) % 2)
                after(dve, x4_ready, c + 1)
                zc = z_all[:, bass.ds(c * CH, CH)]
                dve.scalar_tensor_tensor(zc, bank[6 + par][:], tcol[:, 3:4], x3f[:, par, :], add, add)\
                    .then_inc(z_ready, 1)
                held_until(dve, z_ready, c + 1)
                dve.bn_stats(stats[:, c, :], zc).then_inc(stat_dve_bn, 1)

            dve.wait_ge(ld_ffn, 16 * 6)
            dve.wait_ge(x13T_copied, NB)
            norm_full(0, 0)
            for c in range(2):
                step_b(c, c)
            with dve.Fori(1, NCH // 2 - 1) as pair:
                step_b(pair * 2, 0)
                step_b(pair * 2 + 1, 1)
            for c in range(NCH - 2, NCH):
                step_b(c, c % 2)
            global_affine(1, NCH, None)

            dve.wait_ge(ld_merge, 16 * 13)
            dve.tensor_tensor(tvd, tvln, lnp[0:E, :, :], sub).then_inc(prep_dve, 1)
            dve.wait_ge(prep_pe, 6)
            dve.tensor_copy(gw1T[:], bank[0][:, 0:P])
            dve.tensor_copy(gw2T[:], bank[0][:, P:P + E])
            dve.tensor_copy(gw2x[:], bank[0][:, P:P + E].unsqueeze(2).to_broadcast([P, E, X]))
            dve.tensor_copy(fw1T[:], bank[1][:])
            dve.tensor_copy(fw2T[:].rearrange("p c d -> p (c d)"), bank[2][:])
            dve.wait_ge(prep_pe, 7)
            dve.tensor_tensor(flat(lng), flat(lnp), bank[3][:, 0:2 * D], add).then_inc(prep_dve, 1)

            dve.wait_ge(ld_attn, 16 * 7)
            h_b, t2_b, t3_b, qk_b, v_b, l_b, r_b, g_b = bank

            def row_stats(src, bn, mv, ve, par, b, bn_s, aggr_s, var_s, pool_done):
                dve.nop(nofuse=True)
                for k in range(2):
                    ins = dve.bn_stats(bn[:, par, k, :], src[k])
                ins.then_inc(bn_s, 1)
                held_until(dve, bn_s, b + 1)
                for k in range(2):
                    ins = dve.bn_aggr(mv[:, par, k, :], bn[:, par, k, :])
                ins.then_inc(aggr_s, 1)
                after(dve, aggr_s, b + 1)
                after(dve, pool_done, b - 1)
                dve.tensor_scalar(ve[:, par, :], mv[:, par, :, 1], LN_EPS, None, add).then_inc(var_s, 1)

            def step_c(i, par):
                other = (par + 1) % 2
                if on(i, 0, NB):
                    after(dve, h_turned, i + 1)
                    after(dve, n_ready, i - 1)
                    row_stats([h_b[:, 0:P], h_b[:, P:T]], bn1, mv1, ve1, par, i, bn1_ready, aggr1_ready,
                              var1_ready, rstd1_ready)
                if on(i, 3, NB):
                    b, pb = i - 3, other
                    after(dve, read_ready, b + 1)
                    after(dve, hn_ready, b + 1)
                    dve.tensor_tensor(res2[:, b, :], r_b[:, 0:T], res2[:, b, :], add).then_inc(h2_ready, 1)
                    after(dve, h2_ready, b + 1)
                    row_stats([res2[:, b, 0:P], res2[:, b, P:T]], bn2, mv2, ve2, pb, b, bn2_ready,
                              aggr2_ready, var2_ready, rstd2_ready)
                if on(i, 2, NB):
                    b, pb = i - 2, par
                    after(dve, logits_ready, b + 1)
                    dve.tensor_reduce(rmax[:, pb, 0:1], l_b[:, 0:T], AX.X, ALU.max)
                    dve.tensor_reduce(rmax[:, pb, 1:2], l_b[:, T:T + P], AX.X, ALU.max).then_inc(cmax_ready, 1)
                    after(dve, cmax_ready, b + 1)
                    after(dve, cprobs_ready, b - 1)
                    dve.tensor_scalar(nmax[:, pb, :], rmax[:, pb, :], -1.0, None, mult).then_inc(ncmax_ready, 1)
                if on(i, 0, NB):
                    after(dve, rstd1_ready, i + 1)
                    dve.scalar_tensor_tensor(nm1[:, par, :], mv1[:, par, :, 0], -1.0, rs1[:, par, :],
                                             mult, mult).then_inc(shift1_ready, 1)
                if on(i, 1, NB):
                    b, pb = i - 1, other
                    after(dve, qkv_ready, b + 1)
                    dve.tensor_tensor(v_s[:, pb, :], v_b[:, 0:T], flat(abv), add).then_inc(v_copied, 1)
                if on(i, 3, NB):
                    b, pb = i - 3, other
                    after(dve, rstd2_ready, b + 1)
                    after(dve, m_ready, b - 1)
                    dve.scalar_tensor_tensor(nm2[:, pb, :], mv2[:, pb, :, 0], -1.0, rs2[:, pb, :],
                                             mult, mult).then_inc(shift2_ready, 1)
                if on(i, 2, NB):
                    b, pb = i - 2, par
                    after(dve, cprobs_ready, b + 1)
                    dve.reciprocal(rsum[:, pb, :], psums[:, pb, :]).then_inc(csum_ready, 1)
                    after(dve, csum_ready, b + 1)
                    after(dve, v_copied, b + 1)
                    after(dve, read_ready, b - 1)
                    for k in range(2):
                        ins = dve.tensor_scalar(vp_s[:, pb, k * P:(k + 1) * P], v_s[:, pb, k * P:(k + 1) * P],
                                                rsum[:, pb, k:k + 1], INV_SQRT_K, mult, mult)
                    ins.then_inc(vp_ready, 1)
                if on(i, 0, NB):
                    after(dve, n_ready, i + 1)
                    dve.tensor_tensor(res2[:, i, :], h_b[:, 0:T], n_s[:, par, :], add).then_inc(hn_ready, 1)

            pipeline(dve, step_c, NB, 4, 2)

            dve.wait_ge(g_pe, 1)
            dve.tensor_scalar(grep[:], bank[7][:, 0:NB], 1.0 / T, gcol[:, 1:2], mult, add)
            dve.tensor_scalar(gT[:], bank[7][0:E, NB:2 * NB], 1.0 / T, gb2[:, 0:1], mult, add).then_inc(g_dve, 1)
            dve.wait_ge(g_dve, 1)
            dve.tensor_tensor(gdiag[:], grep[:].unsqueeze(2).to_broadcast([P, NB, X]),
                              cst[:, C_DIAG:C_DIAG + X].unsqueeze(1).to_broadcast([P, NB, X]), mult)\
                .then_inc(g_dve, 1)
            dve.tensor_copy(gbc, gT[:].unsqueeze(2).to_broadcast([E, NB, P])).then_inc(g_dve, 1)

            def merged(p, count):
                dve.wait_ge(merged_pe, count + 1)
                src = bank[count % 4][:].rearrange("p (j b x) -> p j b x", j=2, b=NB)
                f0 = 2 * p * X
                if count < 16:
                    dst = w1m[:, :, f0:f0 + 2 * X].rearrange("p b (j x) -> p j b x", j=2)
                    base = fw1T[:, f0:f0 + 2 * X].rearrange("p (j x) -> p j x", j=2)
                else:
                    dc, c = 2 * p // FCH, 2 * p % FCH
                    dst = w2m[:, :, c:c + 2, dc * X:(dc + 1) * X].rearrange("p b j x -> p j b x")
                    base = fw2T[:, c:c + 2, dc * X:(dc + 1) * X]
                dve.tensor_tensor(dst, src, base.unsqueeze(2).to_broadcast([P, 2, NB, X]), add)\
                    .then_inc(merged_dve, 1)

            for p in range(16):
                merged(p, p)
            dve.wait_ge(g_pe, 2)
            dve.tensor_tensor(b1m[:], bank[6][:, 0:FCH * NB].rearrange("p (c b) -> p c b", c=FCH),
                              fb1[:].unsqueeze(2).to_broadcast([P, FCH, NB]), add).then_inc(g_dve, 1)
            for q in range(4):
                dve.wait_ge(g_pe, 3 + q)
                dve.tensor_tensor(b2m[:, 4 * q:4 * q + 4, :], bank[4 + q % 2][:].rearrange("p (b d) -> p b d", b=4),
                                  fb2[:].unsqueeze(1).to_broadcast([P, 4, D]), add).then_inc(g_dve, 1)
            for p in range(16):
                merged(p, 16 + p)

            def step_d(i, par):
                other = (par + 1) % 2
                if on(i, 0, NB):
                    for f in range(2, 4):
                        after(dve, hid2_ready, 2 * i + 2)
                        after(dve, out_ready, i - 1)
                        dve.tensor_scalar(hid2[:, par, f, :], bank[2 * par + 1][:, (f - 2) * T:(f - 1) * T],
                                          b1m[:, f, bass.ds(i, 1)], 0.0, add, ALU.max).then_inc(relu2_dve, 1)
                if on(i, 1, NB):
                    b, pb = i - 1, other
                    after(dve, out_ready, b + 1)
                    after(dve, mb_ready, b + 1)
                    dve.tensor_tensor(r_s[:, pb, :], bank[6 + pb][:, 0:T], x13[:, b, :], add)\
                        .then_inc(res_ready, 1)
                    after(dve, res_ready, b + 1)
                    row_stats([r_s[:, pb, 0:P], r_s[:, pb, P:T]], bn1, mv1, ve1, pb, b, bn3_ready,
                              aggr3_ready, var3_ready, rstd3_ready)
                if on(i, 2, NB):
                    b, pb = i - 2, par
                    for k in range(2):
                        ins = dve.scalar_tensor_tensor(ln_s[:, pb, k * P:(k + 1) * P], r_s[:, pb, k * P:(k + 1) * P],
                                                       mv1[:, pb, k, 0:1], lng[:, 0, :], sub, mult)
                    ins.then_inc(scaled_ready, 1)
                    after(dve, scaled_ready, b + 1)
                    after(dve, rstd3_ready, b + 1)
                    after(dve, hlb_ready, b + 1)
                    after(dve, stored[pb], 8 * (b - pb))
                    for k in range(2):
                        ins = dve.scalar_tensor_tensor(o_s[:, pb, k * P:(k + 1) * P], ln_s[:, pb, k * P:(k + 1) * P],
                                                       rs1[:, pb, k:k + 1], res2[:, b, k * P:(k + 1) * P],
                                                       mult, add)
                    ins.then_inc(o_ready, 1)

            pipeline(dve, step_d, NB, 2, 2)

        @block.gpsimd
        def _(pool):
            pool.memset(nhalf[:, 0:2], -0.5)
            pool.memset(nhalf[:, 2:4], 0.5).then_inc(pool_const, 1)
            pool.wait_ge(ld_ffn, 16 * 6)
            pool.tensor_copy(w1_hi[:], w1s).then_inc(prep_pool, 1)
            pool.wait_ge(prep_pool, 1)
            pool.tensor_tensor(w1_lo[:], w1s, w1_hi[:].bitcast(F32), ALU.subtract).then_inc(prep_pool, 1)
            pool.wait_ge(ld_const, 16)
            pool.tensor_copy(ident_b[:], ident)
            pool.memset(maskT[:], 0.0).then_inc(pool_const, 1)
            pool.wait_ge(pool_const, 2)
            pool.affine_select(out=maskT[:], in_=maskT[:], compare_op=ALU.is_ge, fill=MASKED, base=0,
                               pattern=[[1, P]], channel_multiplier=-1).then_inc(pool_const, 1)

            def root(r):
                pool.wait_ge(stat_dve, 3 * r + 3)
                pool.tensor_tensor(gstat[:, 6:7], gstat[:, 5:6], nhalf[:, 2:3], ALU.pow).then_inc(stat_pool, 1)

            root(0)

            def step_b(c, par):
                pool.wait_ge(x3_hi_ready, c + 1)
                pool.wait_ge(x3_full, c + 1)
                after(pool, hid_ready, 4 * (c - 1))
                pool.tensor_tensor(x3_lo[:, par, :], x3f[:, par, :], x3_hi[:, par, :].bitcast(F32),
                                   ALU.subtract).then_inc(x3_lo_ready, 1)

            for c in range(2):
                step_b(c, c)
            with pool.Fori(1, NCH // 2) as pair:
                step_b(pair * 2, 0)
                step_b(pair * 2 + 1, 1)
            root(1)

            def step_c(i, par):
                other = (par + 1) % 2
                if on(i, 0, NB):
                    after(pool, var1_ready, i + 1)
                    after(pool, n_ready, i - 1)
                    pool.tensor_tensor(rs1[:, par, :], ve1[:, par, :], nhalf[:, 0:2], ALU.pow)\
                        .then_inc(rstd1_ready, 1)
                if on(i, 3, NB):
                    b, pb = i - 3, other
                    after(pool, var2_ready, b + 1)
                    after(pool, m_ready, b - 1)
                    pool.tensor_tensor(rs2[:, pb, :], ve2[:, pb, :], nhalf[:, 0:2], ALU.pow)\
                        .then_inc(rstd2_ready, 1)
                if on(i, 4, NB):
                    b = i - 4
                    after(pool, m_ready, b + 1)
                    pool.tensor_copy(x13[:, b, :], x13_s[:, par, :]).then_inc(m_kept, 1)

            pipeline(pool, step_c, NB, 4, 2)

            def step_d(i, par):
                if on(i, 0, NB):
                    if isinstance(i, int) and i == 0:
                        pool.wait_ge(m_kept, NB)
                        pool.wait_ge(g_dve, 8)
                        pool.wait_ge(prep_dve, 8)
                    for k in range(2):
                        ins = pool.tensor_tensor(x13[:, i, k * P:(k + 1) * P], x13[:, i, k * P:(k + 1) * P],
                                                 b2m[:, i, :], ALU.add)
                    ins.then_inc(mb_ready, 1)
                    for k in range(2):
                        ins = pool.tensor_tensor(res2[:, i, k * P:(k + 1) * P], res2[:, i, k * P:(k + 1) * P],
                                                 lng[:, 1, :], ALU.add)
                    ins.then_inc(hlb_ready, 1)
                if on(i, 1, NB):
                    b, pb = i - 1, (par + 1) % 2
                    after(pool, var3_ready, b + 1)
                    after(pool, o_ready, b - 1)
                    pool.tensor_tensor(rs1[:, pb, :], ve1[:, pb, :], nhalf[:, 0:2], ALU.pow)\
                        .then_inc(rstd3_ready, 1)

            pipeline(pool, step_d, NB, 1, 2)


_NAMES = ["x"] + [f"L0_tok_{n}" for n in ("emb", "Wq", "bq", "Wk", "bk", "Wv", "bv", "Wo", "bo", "W1", "b1",
                                          "W2", "b2", "gamma", "beta")]
_NAMES += [f"L0_attn_{n}" for n in ("Wk", "bk", "Wq", "bq", "Wv", "bv")]
_NAMES += [f"L0_ffn_{n}" for n in ("gfc1_w", "gfc1_b", "gfc2_w", "gfc2_b", "W1", "b1", "W2", "b2", "ln_g",
                                   "ln_b", "tv_W1", "tv_b1", "tv_W2", "tv_b2", "tv_ln_g", "tv_ln_b")]


def kernel(**inputs):
    import concourse.bacc as bacc
    from concourse.bass_utils import run_bass_kernel_spmd

    nc = bacc.Bacc("TRN2", target_bir_lowering=False, num_devices=1)
    tokens, features = inputs["x"].shape[1], inputs["L0_tok_emb"].shape[1]
    arrays = {n: np.ascontiguousarray(inputs[n]) for n in _NAMES}
    arrays["constants"] = shape_constants(tokens, features)
    args = {n: nc.dram_tensor(f"in_{n}", v.shape, mybir.dt.from_np(v.dtype), kind="ExternalInput").ap()
            for n, v in arrays.items()}
    out = nc.dram_tensor("out", (*inputs["x"].shape, features), F32, kind="ExternalOutput").ap()
    build(nc, args, out)
    r = run_bass_kernel_spmd(nc, [{f"in_{n}": v for n, v in arrays.items()}], core_ids=[0])
    return r.results[0]["out"]
```

```python
import math
from contextlib import ExitStack

import numpy as np

import concourse.bass as bass
from concourse import mybir

F32 = mybir.dt.float32
F32R = mybir.dt.float32r
BF16 = mybir.dt.bfloat16
I32 = mybir.dt.int32
ALU = mybir.AluOpType
ACT = mybir.ActivationFunctionType
AX = mybir.AxisListType

P = 128
MASKED = -1.0e30
C_LAGS = (1, 2, 3, 4, 5, 6, 7, 8, 9, 10)

C_PE = 0
C_PET = 256
C_ID = 512
C_AVG = 640
C_DIAG = 768
C_IOTA = 784
C_MERGE = 785
C_COLS = 913


def shape_constants(tokens, features):
    pos = np.arange(tokens, dtype=np.float32)[:, None]
    i = np.arange(features, dtype=np.float32)[None, :]
    angle = pos / np.power(np.float32(10000.0), np.float32(2.0) * i / np.float32(features))
    pe = np.where((np.arange(features) % 2 == 0)[None, :], np.sin(angle), np.cos(angle))
    pe = pe.astype(np.float32)
    c = np.zeros((P, C_COLS), np.float32)
    c[:, C_PE:C_PE + 256] = pe.reshape(2, P, features).transpose(1, 0, 2).reshape(P, 256)
    c[:, C_PET:C_PET + 256] = pe.T
    c[:, C_ID:C_ID + P] = np.eye(P)
    c[:, C_AVG:C_AVG + P] = 1.0 / P
    c[:, C_DIAG:C_DIAG + 16] = np.arange(P)[:, None] % 16 == np.arange(16)[None, :]
    c[:, C_IOTA] = np.arange(P)
    c[:, C_MERGE:C_MERGE + P] = 0.03
    return c


def build(nc, a, out):
    NB, T = a["x"].shape
    V, D = a["L0_tok_emb"].shape
    FF = a["L0_tok_W1"].shape[1]
    E = a["L0_ffn_tv_W1"].shape[0]
    NT = NB * T
    FCH = FF // P
    X = P // E
    CH = 512
    NCH = NT // CH
    assert (D, V, T, NB, E, FF) == (P, P, 2 * P, 16, 8, 512)
    TOK_SCALE = 1.0 / math.sqrt(512.0)
    INV_SQRT_K = 1.0 / math.sqrt(float(D))
    LN_EPS = 1e-5
    STD_EPS = 1e-9
    COUNT = NT * D

    L_TH, L_N, L_TN, L_QKV, L_LOG, L_READ, L_H2, L_M, L_TM, L_GATE = C_LAGS

    with ExitStack() as ctx:
        def sb(name, shape, dt=F32):
            return ctx.enter_context(nc.sbuf_tensor(name, shape, dt))

        def sem(name):
            return ctx.enter_context(nc.semaphore(name))

        cst = sb("cst", [P, C_COLS])
        z_all = sb("z_all", [P, NT])
        onehot = sb("onehot", [P, 2, T], F32R)
        x13 = sb("x13", [P, NB, T])
        res2 = sb("res2", [P, NB, T])
        mT = sb("mT", [P, NB, T])
        w1m = sb("w1m", [P, NB, FF])
        w2m = sb("w2m", [P, NB, FCH, D])
        tv1 = sb("tv1", [P, FF // X, D])
        tv2 = sb("tv2", [P, D // X, FF])
        xv_all = w1m
        early = res2[:].rearrange("p b t -> p (b t)")
        mats = lambda o, k: early[:, o * D:(o + k) * D].rearrange("p (k d) -> p k d", k=k)
        emb, embT, wvT, bvbc, bo_bc = (early[:, k * D:(k + 1) * D] for k in range(5))
        wtok = mats(5, 4)
        wpre = mats(9, 3)
        tab = mats(12, 4)
        w1s = early[:, 16 * D:20 * D]
        fw1 = mats(20, FCH)
        fw2 = early[:, 24 * D:28 * D]
        tvd, tvln = (early[0:E, o * D:(o + 2) * D].rearrange("e (k d) -> e k d", k=2) for o in (28, 30))
        early_b = mT[:].rearrange("p b t -> p (b t)")
        w2s = early_b[:, 0:FF].rearrange("p (c d) -> p c d", c=FCH)
        c_qk = early_b[:, 512:1024].rearrange("p (k t) -> p k t", k=2)
        c_xv = early_b[:, 1024:1536].rearrange("p (k j d) -> p k j d", k=2, j=2)
        gw1 = early_b[:, 1536:1664]
        lnp = early_b[:, 1664:1920].rearrange("p (k d) -> p k d", k=2)
        gw2 = early_b[0:E, 1920:2048]
        w1b = tv1[:, 0:8, :].rearrange("p (u c) d -> p u (c d)", u=2)
        free = w2m[:].rearrange("p b c d -> p (b c d)")
        two = lambda o, n: free[:, o:o + 2 * n].rearrange("p (k n) -> p k n", k=2)
        hid = free[:, 0:4 * 512].rearrange("p (f n) -> p f n", f=4)
        x3f = two(2048, 512)
        hT = two(3072, T)
        n_s = two(3584, T)
        nT = two(4096, T)
        v_s = two(4608, T)
        vp_s = two(5120, T)
        gjunk = free[:, 5632:5632 + T]
        probT = free[:, 6144:6144 + 4 * T].rearrange("p (u k t) -> p u k t", u=2, k=2)
        b2m = z_all[:, 0:NB * D].rearrange("p (b d) -> p b d", b=NB)
        gbc = z_all[0:E, NB * D:2 * NB * D].rearrange("p (b d) -> p b d", b=NB)
        hid2 = z_all[:, NB * D:2 * NB * D].rearrange("p (u f t) -> p u f t", u=2, f=4)

        tab_hi = sb("tab_hi", [P, 4, D], F32R)
        tab_lo = sb("tab_lo", [P, 4, D], F32R)
        tcol = sb("tcol", [P, 6])
        tb1 = sb("tb1", [P, FCH])
        w1_hi = sb("w1_hi", [P, FF], F32R)
        w1_lo = sb("w1_lo", [P, FF], F32R)
        aw = sb("aw", [P, 3, D])
        acol = sb("acol", [P, 2])
        abv = sb("abv", [P, 2, D])
        gw1T = sb("gw1T", [P, D])
        gw2T = sb("gw2T", [P, E])
        gw2x = sb("gw2x", [P, E, X])
        gcol = sb("gcol", [P, 2])
        gb2 = sb("gb2", [E, 1])
        fw1T = sb("fw1T", [P, FF])
        fw2T = sb("fw2T", [P, FCH, D])
        fb1 = sb("fb1", [P, FCH])
        fb2 = sb("fb2", [P, D])
        tvb1 = sb("tvb1", [E, FF])
        tvb2 = sb("tvb2", [E, D])
        lng = sb("lng", [P, 2, D])
        maskT = sb("maskT", [P, P], BF16)
        ident_b = sb("ident_b", [P, P], BF16)
        nhalf = sb("nhalf", [P, 4])

        qk_s = sb("qk_s", [P, 2, 2, T])
        prob = sb("prob", [P, 2, 2, T])
        x13_s = sb("x13_s", [P, 2, T])
        r_s = qk_s[:, :, 0, :]
        ln_s = qk_s[:, :, 1, :]
        o_s = prob[:, :, 0, :]
        nmax = sb("nmax", [P, 2, 2])
        rmax = sb("rmax", [P, 2, 2])
        psums = sb("psums", [P, 2, 2])
        rsum = sb("rsum", [P, 2, 2])
        stats = sb("stats", [P, NB, 6])
        gstat = sb("gstat", [P, 12])
        gaff = sb("gaff", [P, 4])

        x3_hi = sb("x3_hi", [P, 2, CH], F32R)
        x3_lo = sb("x3_lo", [P, 2, CH], F32R)

        bn1 = sb("bn1", [P, 2, 2, 6])
        mv1 = sb("mv1", [P, 2, 2, 2])
        ve1 = sb("ve1", [P, 2, 2])
        rs1 = sb("rs1", [P, 2, 2])
        nm1 = sb("nm1", [P, 2, 2])
        bn2 = sb("bn2", [P, 2, 2, 6])
        mv2 = sb("mv2", [P, 2, 2, 2])
        ve2 = sb("ve2", [P, 2, 2])
        rs2 = sb("rs2", [P, 2, 2])
        ghsum = sb("ghsum", [P, NB])
        gT = sb("gT", [E, NB])
        grep = sb("grep", [P, NB])
        gdiag = sb("gdiag", [P, NB, X])
        b1m = sb("b1m", [P, FCH, NB])

        bank = [ctx.enter_context(nc.psum_tensor(f"bank{i}", [P, 512], F32)) for i in range(8)]

        ld_const, ld_ids, ld_tok, ld_ffn, ld_attn, ld_gate, ld_merge, ld_tv = (
            sem(n) for n in ("ld_const", "ld_ids", "ld_tok", "ld_ffn", "ld_attn", "ld_gate",
                             "ld_merge", "ld_tv"))
        prep_pe, prep_dve, prep_pool, onehot_ready = (
            sem(n) for n in ("prep_pe", "prep_dve", "prep_pool", "onehot_ready"))
        qk_gathered, xv_gathered, qk_copied, xv_copied = (
            sem(n) for n in ("qk_gathered", "xv_gathered", "qk_copied", "xv_copied"))
        scores_ready, rmax_ready, nmax_ready, probs_ready = (
            sem(n) for n in ("scores_ready", "rmax_ready", "nmax_ready", "probs_ready"))
        probs_turned, probT_ready, av_ready, rsum_ready, x13_ready = (
            sem(n) for n in ("probs_turned", "probT_ready", "av_ready", "rsum_ready", "x13_ready"))
        stat_dve, stat_own, stat_dve_bn, stat_pe, stat_pool, affine_ready, pool_const = (
            sem(n) for n in ("stat_dve", "stat_own", "bn_ready", "stat_pe", "stat_pool", "affine_ready",
                             "pool_const"))
        x13_turned, x13T_copied, x3_full, x3_hi_ready, x3_lo_ready = (
            sem(n) for n in ("x13_turned", "x13T_copied", "x3_full", "x3_hi_ready", "x3_lo_ready"))
        hid_ready, relu_act, relu_dve, x4_ready, z_ready = (
            sem(n) for n in ("hid_ready", "relu_act", "relu_dve", "x4_ready", "z_ready"))
        hT_ready, h_turned, bn1_ready, aggr1_ready, var1_ready, rstd1_ready = (
            sem(n) for n in ("hT_ready", "h_turned", "bn1_ready", "aggr1_ready", "var1_ready",
                             "rstd1_ready"))
        shift1_ready, n_ready, hn_ready, n_turned, nT_ready = (
            sem(n) for n in ("shift1_ready", "n_ready", "hn_ready", "n_turned", "nT_ready"))
        qkv_ready, qk2_copied, v_copied, logits_ready = (
            sem(n) for n in ("qkv_ready", "qk2_copied", "v_copied", "logits_ready"))
        cmax_ready, ncmax_ready, cprobs_ready, csum_ready, vp_ready, read_ready = (
            sem(n) for n in ("cmax_ready", "ncmax_ready", "cprobs_ready", "csum_ready", "vp_ready",
                             "read_ready"))
        h2_ready, bn2_ready, aggr2_ready, var2_ready, rstd2_ready = (
            sem(n) for n in ("h2_ready", "bn2_ready", "aggr2_ready", "var2_ready", "rstd2_ready"))
        m_ready, m_kept, m_turned, mT_ready, gate_ready, gate_summed = (
            sem(n) for n in ("m_ready", "m_kept", "m_turned", "mT_ready", "gate_ready", "gate_summed"))
        g_pe, g_dve, merged_pe, merged_dve = (
            sem(n) for n in ("g_pe", "g_dve", "merged_pe", "merged_dve"))
        hid2_ready, w1b_ready, relu2_act, relu2_dve, out_ready, mb_ready, hlb_ready = (
            sem(n) for n in ("hid2_ready", "w1b_ready", "relu2_act", "relu2_dve", "out_ready", "mb_ready",
                             "hlb_ready"))
        res_ready, bn3_ready, aggr3_ready, var3_ready, rstd3_ready, scaled_ready, o_ready = (
            sem(n) for n in ("res_ready", "bn3_ready", "aggr3_ready", "var3_ready", "rstd3_ready",
                             "scaled_ready", "o_ready"))
        stored = [sem("stored_even"), sem("stored_odd")]

        ident = cst[:, C_ID:C_ID + P]
        avg = cst[:, C_AVG:C_AVG + P]
        ids = z_all[:].bitcast(I32)
        IDQ = NT // 4

        def x13c(c):
            return x13[:].rearrange("p b t -> p (b t)")[:, bass.ds(c * CH, CH)]

        def pipeline(eng, stages, n):
            depth = max(lag for _, lag in stages)
            head = -(-(depth + 2) // 2) * 2

            def edge(i):
                for stage, lag in stages:
                    if 0 <= i - lag < n:
                        stage(i - lag, (i - lag) % 2)

            for i in range(head):
                edge(i)
            if head < n:
                with eng.Fori(head // 2, n // 2) as pair:
                    for j in range(2):
                        for stage, lag in stages:
                            stage(pair * 2 + (j - lag), (j - lag) % 2)
            for i in range(max(head, n), n + depth):
                edge(i)

        def after(eng, s, count):
            if not isinstance(count, int) or count > 0:
                eng.wait_ge(s, count)

        def held_until(eng, s, count):
            after(eng, s, count)
            eng.nop(nofuse=True)

        block = ctx.enter_context(nc.Block())

        @block.sync
        def _(sp):
            col = lambda v: v.rearrange("(p o) -> p o", o=1)
            row = lambda v, n=P: v.rearrange("(o d) -> o d", o=1).broadcast_to([n, v.shape[0]])
            idrow = a["x"].rearrange("b t -> (b t)")
            sp.dma_start(cst[:], a["constants"]).then_inc(ld_const, 16)
            sp.dma_start(emb, a["L0_tok_emb"]).then_inc(ld_tok, 16)
            for k, w in enumerate(("Wq", "Wk", "Wv", "Wo")):
                sp.dma_start(wtok[:, k, :], a[f"L0_tok_{w}"]).then_inc(ld_tok, 16)
            for k, w in enumerate(("bq", "bk", "bv", "b2", "gamma", "beta")):
                sp.dma_start(tcol[:, k:k + 1], col(a[f"L0_tok_{w}"])).then_inc(ld_tok, 16)
            sp.dma_start(bo_bc, row(a["L0_tok_bo"])).then_inc(ld_tok, 16)
            for k in range(4):
                sp.dma_start(ids[:, k * IDQ:(k + 1) * IDQ], row(idrow[k * IDQ:(k + 1) * IDQ]))\
                    .then_inc(ld_ids, 16)
            sp.dma_start(w1s, a["L0_tok_W1"]).then_inc(ld_ffn, 16)
            sp.dma_start(w2s, a["L0_tok_W2"].rearrange("(c p) d -> p c d", p=P)).then_inc(ld_ffn, 16)
            for c in range(FCH):
                sp.dma_start(tb1[:, c:c + 1], col(a["L0_tok_b1"][c * P:(c + 1) * P])).then_inc(ld_ffn, 16)
            for k, w in enumerate(("Wq", "Wk", "Wv")):
                sp.dma_start(aw[:, k, :], a[f"L0_attn_{w}"]).then_inc(ld_attn, 16)
            for k, w in enumerate(("bq", "bk")):
                sp.dma_start(acol[:, k:k + 1], col(a[f"L0_attn_{w}"])).then_inc(ld_attn, 16)
            for k in range(2):
                sp.dma_start(abv[:, k, :], row(a["L0_attn_bv"])).then_inc(ld_attn, 16)
            sp.dma_start(gw1, a["L0_ffn_gfc1_w"]).then_inc(ld_gate, 16)
            sp.dma_start(gw2, a["L0_ffn_gfc2_w"]).then_inc(ld_gate, 16)
            sp.dma_start(gcol[:, 0:1], col(a["L0_ffn_gfc1_b"])).then_inc(ld_gate, 16)
            sp.dma_start(gb2[:], col(a["L0_ffn_gfc2_b"])).then_inc(ld_gate, 16)
            for e in range(E):
                sp.dma_start(gcol[e * X:(e + 1) * X, 1:2],
                             a["L0_ffn_gfc2_b"][e:e + 1].rearrange("(o d) -> o d", o=1).broadcast_to([X, 1]))\
                    .then_inc(ld_gate, 16)
            sp.dma_start(fw1, a["L0_ffn_W1"].rearrange("(c p) d -> p c d", p=P)).then_inc(ld_merge, 16)
            sp.dma_start(fw2, a["L0_ffn_W2"]).then_inc(ld_merge, 16)
            for c in range(FCH):
                sp.dma_start(fb1[:, c:c + 1], col(a["L0_ffn_b1"][c * P:(c + 1) * P])).then_inc(ld_merge, 16)
            sp.dma_start(fb2[:], row(a["L0_ffn_b2"])).then_inc(ld_merge, 16)
            sp.dma_start(tvb1[:], a["L0_ffn_tv_b1"]).then_inc(ld_merge, 16)
            sp.dma_start(tvb2[:], a["L0_ffn_tv_b2"]).then_inc(ld_merge, 16)
            for k, w in enumerate(("g", "b")):
                sp.dma_start(lnp[:, k, :], row(a[f"L0_ffn_ln_{w}"])).then_inc(ld_merge, 16)
                sp.dma_start(tvln[:, k, :], a[f"L0_ffn_tv_ln_{w}"]).then_inc(ld_merge, 16)
            for e in range(E):
                sp.dma_start(tv1[e * X:(e + 1) * X, :, :],
                             a["L0_ffn_tv_W1"][e].rearrange("(c x) d -> x c d", x=X)).then_inc(ld_tv, 16)
                sp.dma_start(tv2[e * X:(e + 1) * X, :, :],
                             a["L0_ffn_tv_W2"][e].rearrange("(c x) f -> x c f", x=X)).then_inc(ld_tv, 16)

            def store(b, par):
                after(sp, o_ready, b + 1)
                sp.dma_start(out[b].rearrange("(k p) d -> p k d", p=P),
                             o_s[:, par, :].rearrange("p (k d) -> p k d", k=2)).then_inc(stored[par], 16)

            with sp.Fori(0, NB // 2) as pair:
                store(pair * 2, 0)
                store(pair * 2 + 1, 1)
            for par in range(2):
                sp.wait_ge(stored[par], 8 * NB)

        @block.tensor
        def _(pe):
            pe.wait_ge(ld_const, 16)
            pe.wait_ge(ld_tok, 16 * 12)
            pe.transpose(bank[0][:, 0:P], emb, ident)
            pe.transpose(bank[0][:, P:2 * P], wtok[:, 2, :], ident).then_inc(prep_pe, 1)
            pe.wait_ge(prep_dve, 1)
            pe.matmul(bank[1][:, 0:D], wvT, wtok[:, 3, :], start=True, stop=True).then_inc(prep_pe, 1)
            pe.wait_ge(prep_dve, 2)
            pe.matmul(bank[2][:, 0:3 * D], embT, wpre.rearrange("p k d -> p (k d)"),
                      start=True, stop=True).then_inc(prep_pe, 1)
            for k in range(2):
                mm = pe.matmul(bank[3][:, k * T:(k + 1) * T], wtok[:, k, :], cst[:, C_PET:C_PET + T],
                               start=True, stop=True)
            mm.then_inc(prep_pe, 1)
            for k in range(2):
                pe.matmul(bank[4][:, k * D:(k + 1) * D], cst[:, C_PET + k * P:C_PET + (k + 1) * P],
                          wpre[:, 2, :], start=True, stop=False)
                mm = pe.matmul(bank[4][:, k * D:(k + 1) * D], bvbc, wtok[:, 3, :],
                               start=False, stop=True)
            mm.then_inc(prep_pe, 1)
            pe.wait_ge(prep_dve, 6)

            qk_b, xv_b, s_b, t_b, av_b, xt_b = bank[0:2], bank[2], bank[4:6], bank[6], bank[7], bank[3]

            def gather(b, u):
                after(pe, onehot_ready, b + 1)
                after(pe, qk_copied, b - 1)
                for k in range(2):
                    pe.matmul(qk_b[u][:, k * T:(k + 1) * T], tab_hi[:, k, :], onehot[:, u, :],
                              start=True, stop=False)
                    mm = pe.matmul(qk_b[u][:, k * T:(k + 1) * T], tab_lo[:, k, :], onehot[:, u, :],
                                   start=False, stop=True)
                mm.then_inc(qk_gathered, 1)
                after(pe, xv_copied, b)
                for k in range(2):
                    for part in (tab_hi, tab_lo):
                        mm = pe.matmul(xv_b[:, k * T:(k + 1) * T], onehot[:, u, k * P:(k + 1) * P],
                                       part[:, 2:4, :].rearrange("p k d -> p (k d)"),
                                       start=(part is tab_hi), stop=(part is tab_lo))
                mm.then_inc(xv_gathered, 1)

            def scores(b, u):
                after(pe, qk_copied, b + 1)
                after(pe, probs_ready, b - 1)
                for q in range(2):
                    mm = pe.matmul(s_b[u][:, q * T:(q + 1) * T], qk_s[:, u, 0, q * P:(q + 1) * P],
                                   qk_s[:, u, 1, :], start=True, stop=True)
                mm.then_inc(scores_ready, 1)

            def turn_probs(b, u):
                after(pe, probs_ready, b + 1)
                after(pe, probT_ready, b)
                for k in range(2):
                    for q in range(2):
                        mm = pe.transpose(t_b[:, (2 * k + q) * P:(2 * k + q + 1) * P],
                                          prob[:, u, q, k * P:(k + 1) * P], ident)
                mm.then_inc(probs_turned, 1)

            def probs_by_values(b, u):
                after(pe, probT_ready, b + 1)
                after(pe, x13_ready, b)
                for q in range(2):
                    for k in range(2):
                        mm = pe.matmul(av_b[:, q * P:(q + 1) * P], probT[:, u, k, q * P:(q + 1) * P],
                                       xv_all[:, b, k * T + P:k * T + 2 * P], start=(k == 0), stop=(k == 1))
                mm.then_inc(av_ready, 1)

            def turn_x13(b, u):
                after(pe, x13_ready, b + 1)
                after(pe, x13T_copied, b)
                for k in range(2):
                    mm = pe.transpose(xt_b[:, k * P:(k + 1) * P], x13_s[:, u, k * P:(k + 1) * P], ident)
                mm.then_inc(x13_turned, 1)

            pipeline(pe, [(scores, 2), (turn_probs, 3), (gather, 1), (probs_by_values, 4), (turn_x13, 5)], NB)

            def global_mean(r):
                pe.wait_ge(stat_dve, 3 * r + 1)
                pe.matmul(bank[7][:, 0:1], avg, gstat[:, 0:1], start=True, stop=True).then_inc(stat_pe, 1)
                pe.wait_ge(stat_dve, 3 * r + 2)
                pe.matmul(bank[7][:, 1:2], avg, gstat[:, 4:5], start=True, stop=True).then_inc(stat_pe, 1)

            global_mean(0)

            h_b, x4_b = bank[2:6], bank[6:8]

            def step_b(c, par):
                pe.wait_ge(x3_hi_ready, c + 1)
                pe.wait_ge(x3_lo_ready, c + 1)
                for f in range(FCH):
                    after(pe, (relu_act, relu_dve)[f % 2], 2 * c - 1 + f // 2)
                    w = slice(f * P, (f + 1) * P)
                    pe.matmul(h_b[f][:], w1_hi[:, w], x3_hi[:, par, :], start=True, stop=False)
                    pe.matmul(h_b[f][:], w1_lo[:, w], x3_hi[:, par, :], start=False, stop=False)
                    pe.matmul(h_b[f][:], w1_hi[:, w], x3_lo[:, par, :], start=False, stop=True)\
                        .then_inc(hid_ready, 1)
                after(pe, z_ready, c - 1)
                for f in range(FCH):
                    after(pe, (relu_act, relu_dve)[f % 2], 2 * c + 1 + f // 2)
                    mm = pe.matmul(x4_b[par][:], w2s[:, f, :], hid[:, f, :],
                                   start=(f == 0), stop=(f == FCH - 1))
                mm.then_inc(x4_ready, 1)

            pe.wait_ge(prep_pool, 2)
            pe.wait_ge(ld_ffn, 16 * 6)
            for c in range(2):
                step_b(c, c)
            with pe.Fori(1, NCH // 2 - 1) as pair:
                step_b(pair * 2, 0)
                step_b(pair * 2 + 1, 1)
            for c in range(NCH - 2, NCH):
                step_b(c, c % 2)
            global_mean(1)

            pe.wait_ge(ld_gate, 16 * (4 + E))
            pe.wait_ge(ld_merge, 16 * 13)
            pe.transpose(bank[0][:, 0:P], gw1, ident)
            pe.transpose(bank[0][:, P:P + E], gw2, cst[0:E, C_ID:C_ID + E])
            for c in range(FCH):
                pe.transpose(bank[1][:, c * P:(c + 1) * P], fw1[:, c, :], ident)
                mm = pe.transpose(bank[2][:, c * P:(c + 1) * P], fw2[:, c * P:(c + 1) * P], ident)
            mm.then_inc(prep_pe, 1)
            pe.wait_ge(prep_dve, 7)
            pe.matmul(bank[3][:, 0:2 * D], cst[0:E, C_MERGE:C_MERGE + P],
                      tvd.rearrange("e k d -> e (k d)"), start=True, stop=True).then_inc(prep_pe, 1)
            pe.wait_ge(prep_dve, 8)
            pe.wait_ge(ld_attn, 16 * 7)

            h_b, t_b, qk_b, v_b, l_b, r_b, g_b = bank[0:2], bank[2], bank[3], bank[4], bank[5], bank[6], bank[7]

            def turn_h(b, u):
                after(pe, hT_ready, b + 1)
                after(pe, hn_ready, b - 1)
                for k in range(2):
                    mm = pe.transpose(h_b[u][:, k * P:(k + 1) * P], hT[:, u, k * P:(k + 1) * P], ident)
                mm.then_inc(h_turned, 1)

            def turn_n(b, u):
                after(pe, n_ready, b + 1)
                after(pe, nT_ready, b)
                after(pe, mT_ready, b - (L_TM - L_TN))
                for k in range(2):
                    mm = pe.transpose(t_b[:, k * P:(k + 1) * P], n_s[:, u, k * P:(k + 1) * P], ident)
                mm.then_inc(n_turned, 1)

            def turn_m(b, u):
                after(pe, m_ready, b + 1)
                after(pe, mT_ready, b)
                for k in range(2):
                    mm = pe.transpose(t_b[:, T + k * P:T + (k + 1) * P], x13_s[:, u, k * P:(k + 1) * P], ident)
                mm.then_inc(m_turned, 1)

            def project(b, u):
                after(pe, nT_ready, b + 1)
                after(pe, qk2_copied, b)
                after(pe, v_copied, b)
                for k in range(2):
                    pe.matmul(qk_b[:, k * T:(k + 1) * T], aw[:, k, :], nT[:, u, :], start=True, stop=True)
                for k in range(2):
                    mm = pe.matmul(v_b[:, k * P:(k + 1) * P], nT[:, u, k * P:(k + 1) * P], aw[:, 2, :],
                                   start=True, stop=True)
                mm.then_inc(qkv_ready, 1)

            def logits(b, u):
                after(pe, qk2_copied, b + 1)
                after(pe, cprobs_ready, b)
                pe.matmul(l_b[:, 0:T], qk_s[:, u, 1, 0:P], qk_s[:, u, 0, :], start=True, stop=False,
                          skip_group_check=True)
                pe.matmul(l_b[:, T:T + P], qk_s[:, u, 1, P:T], qk_s[:, u, 0, P:T],
                          start=False, stop=False, skip_group_check=True)
                pe.matmul(l_b[:, 0:P], ident_b[:], maskT[:], start=False, stop=False,
                          skip_group_check=True)
                pe.matmul(l_b[:, T:T + P], ident_b[:], maskT[:], start=False, stop=True,
                          skip_group_check=True).then_inc(logits_ready, 1)

            def read(b, u):
                after(pe, vp_ready, b + 1)
                after(pe, h2_ready, b)
                pr = prob[:, u].rearrange("p k t -> p (k t)")
                pe.matmul(r_b[:, 0:P], pr[:, 0:P], vp_s[:, u, 0:P], start=True, stop=True)
                pe.matmul(r_b[:, P:T], pr[:, P:T], vp_s[:, u, 0:P], start=True, stop=False)
                pe.matmul(r_b[:, P:T], pr[:, T:T + P], vp_s[:, u, P:T], start=False, stop=True)\
                    .then_inc(read_ready, 1)

            def gate(b, u):
                after(pe, mT_ready, b + 1)
                after(pe, gate_summed, b)
                pe.matmul(g_b[:, 0:T], gw1T[:], mT[:, b, :], start=True, stop=True).then_inc(gate_ready, 1)

            pipeline(pe, [(turn_h, L_TH), (turn_n, L_TN), (turn_m, L_TM), (logits, L_LOG), (read, L_READ),
                          (project, L_QKV), (gate, L_GATE)], NB)

            pe.wait_ge(gate_summed, NB)
            pe.matmul(bank[7][:, 0:NB], gw2x[:].rearrange("p e x -> p (e x)"), ghsum[:], start=True, stop=True)
            pe.matmul(bank[7][0:E, NB:2 * NB], gw2T[:], ghsum[:], start=True, stop=True).then_inc(g_pe, 1)
            pe.wait_ge(g_dve, 2)
            pe.wait_ge(ld_tv, 16 * 2 * E)

            def merge(p, bk, count):
                after(pe, merged_dve, count - 3)
                for j in range(2):
                    blk = 2 * p + j
                    if bk == "w1":
                        lhsT = tv1[:, blk, :]
                    else:
                        lhsT = tv2[:, blk // FCH, (blk % FCH) * P:(blk % FCH + 1) * P]
                    mm = pe.matmul(bank[count % 4][:, j * T:(j + 1) * T], lhsT,
                                   gdiag[:].rearrange("p b x -> p (b x)"), start=True, stop=True)
                mm.then_inc(merged_pe, 1)

            for p in range(16):
                merge(p, "w1", p)
            pe.wait_ge(g_dve, 3)
            for c in range(FCH):
                mm = pe.matmul(bank[6][:, c * NB:(c + 1) * NB], tvb1[:, c * P:(c + 1) * P], gT[:],
                               start=True, stop=True)
            mm.then_inc(g_pe, 1)
            for q in range(4):
                after(pe, g_dve, 4 + q - 1 if q > 1 else 0)
                for b in range(4):
                    mm = pe.matmul(bank[4 + q % 2][:, b * P:(b + 1) * P], gbc[:, 4 * q + b, :], tvb2[:],
                                   start=True, stop=True)
                mm.then_inc(g_pe, 1)
            for p in range(16):
                merge(p, "w2", 16 + p)

            h_b, o_b = bank[0:4], bank[6:8]
            pe.wait_ge(merged_dve, 32)
            pe.wait_ge(g_dve, 8)

            def hidden(b, u):
                after(pe, w1b_ready, b + 1)
                for f in range(FCH):
                    after(pe, (relu2_act, relu2_dve)[f // 2], 2 * (b - 1))
                    mm = pe.matmul(h_b[2 * u + f // 2][:, (f % 2) * T:(f % 2 + 1) * T],
                                   w1b[:, u, f * P:(f + 1) * P], mT[:, b, :], start=True, stop=True)
                    if f % 2 == 1:
                        mm.then_inc(hid2_ready, 1)

            def project_out(b, u):
                after(pe, res_ready, b - 1)
                after(pe, relu2_act, 2 * (b + 1))
                after(pe, relu2_dve, 2 * (b + 1))
                for k in range(2):
                    for f in range(FCH):
                        mm = pe.matmul(o_b[u][:, k * P:(k + 1) * P], hid2[:, u, f, k * P:(k + 1) * P],
                                       w2m[:, b, f, :], start=(f == 0), stop=(f == FCH - 1))
                mm.then_inc(out_ready, 1)

            pipeline(pe, [(hidden, 0), (project_out, 1)], NB)

        @block.scalar
        def _(act):
            def exponentials(b, u):
                after(act, nmax_ready, b + 1)
                after(act, probs_turned, b - 1)
                for q in range(2):
                    ins = act.activation(prob[:, u, q, :], bank[4 + u][:, q * T:(q + 1) * T], ACT.Exp,
                                         bias=nmax[:, u, q:q + 1], scale=TOK_SCALE,
                                         accum_out=psums[:, u, q:q + 1])
                ins.then_inc(probs_ready, 1)

            def copy_probT(b, u):
                after(act, probs_turned, b + 1)
                after(act, av_ready, b - 1)
                act.activation(probT[:, u].rearrange("p k q -> p (k q)"), bank[6][:], ACT.Copy)\
                    .then_inc(probT_ready, 1)

            def copy_x13T(b, u):
                after(act, x13_turned, b + 1)
                act.activation(x13[:, b, :], bank[3][:, 0:T], ACT.Copy).then_inc(x13T_copied, 1)

            pipeline(act, [(copy_x13T, 6), (copy_probT, 3), (exponentials, 2)], NB)

            def norm_hi(c, par):
                after(act, hid_ready, 4 * (c - 1))
                act.activation(x3_hi[:, par, :], x13c(c), ACT.Identity, bias=gaff[:, 1:2],
                               scale=gaff[:, 0:1]).then_inc(x3_hi_ready, 1)

            def step_b(c, par):
                for f in (0, 2):
                    after(act, hid_ready, 4 * c + f + 1)
                    after(act, x4_ready, c)
                    act.activation(hid[:, f, :], bank[2 + f][:], ACT.Relu, bias=tb1[:, f:f + 1])\
                        .then_inc(relu_act, 1)
                if not isinstance(c, int) or c < NCH - 1:
                    norm_hi(c + 1, (par + 1) % 2)

            act.wait_ge(affine_ready, 1)
            act.wait_ge(ld_ffn, 16 * 6)
            norm_hi(0, 0)
            for c in range(2):
                step_b(c, c)
            with act.Fori(1, NCH // 2 - 1) as pair:
                step_b(pair * 2, 0)
                step_b(pair * 2 + 1, 1)
            for c in range(NCH - 2, NCH):
                step_b(c, c % 2)

            act.wait_ge(affine_ready, 2)
            act.wait_ge(ld_attn, 16 * 7)
            act.wait_ge(ld_gate, 16 * (4 + E))
            h_b, t_b, qk_b, v_b, l_b, r_b, g_b = bank[0:2], bank[2], bank[3], bank[4], bank[5], bank[6], bank[7]

            def norm_h(b, u):
                after(act, h_turned, b - 1)
                act.activation(hT[:, u, :], z_all[:, bass.ds(b * T, T)], ACT.Identity,
                               bias=gaff[:, 3:4], scale=gaff[:, 2:3]).then_inc(hT_ready, 1)

            def norm_n(b, u):
                after(act, shift1_ready, b + 1)
                after(act, n_turned, b - 1)
                for k in range(2):
                    ins = act.activation(n_s[:, u, k * P:(k + 1) * P], h_b[u][:, k * P:(k + 1) * P],
                                         ACT.Identity, bias=nm1[:, u, k:k + 1], scale=rs1[:, u, k:k + 1])
                ins.then_inc(n_ready, 1)

            def copy_nT(b, u):
                after(act, n_turned, b + 1)
                after(act, m_turned, b + 1 - (L_TM - L_TN))
                after(act, qkv_ready, b - 1)
                act.activation(nT[:, u, :], t_b[:, 0:T], ACT.Copy).then_inc(nT_ready, 1)

            def bias_qk(b, u):
                after(act, qkv_ready, b + 1)
                after(act, logits_ready, b - 1)
                for k in range(2):
                    ins = act.activation(qk_s[:, u, k, :], qk_b[:, k * T:(k + 1) * T], ACT.Identity,
                                         bias=acol[:, k:k + 1])
                ins.then_inc(qk2_copied, 1)

            def exponentials_c(b, u):
                after(act, ncmax_ready, b + 1)
                after(act, read_ready, b - 1)
                pr = prob[:, u].rearrange("p k t -> p (k t)")
                act.activation(pr[:, 0:T], l_b[:, 0:T], ACT.Exp, bias=nmax[:, u, 0:1],
                               accum_out=psums[:, u, 0:1])
                act.activation(pr[:, T:T + P], l_b[:, T:T + P], ACT.Exp, bias=nmax[:, u, 1:2],
                               accum_out=psums[:, u, 1:2]).then_inc(cprobs_ready, 1)

            def copy_mT(b, u):
                after(act, m_turned, b + 1)
                act.activation(mT[:, b, :], t_b[:, T:2 * T], ACT.Copy).then_inc(mT_ready, 1)

            def relu_gate(b, u):
                after(act, gate_ready, b + 1)
                act.activation(gjunk, g_b[:, 0:T], ACT.Relu, bias=gcol[:, 0:1],
                               accum_out=ghsum[:, bass.ds(b, 1)]).then_inc(gate_summed, 1)

            pipeline(act, [(norm_h, 0), (norm_n, L_N), (copy_nT, L_TN), (copy_mT, L_TM),
                           (exponentials_c, L_LOG), (bias_qk, L_QKV), (relu_gate, L_GATE)], NB)

            act.wait_ge(g_dve, 4)

            def load_w1(b, u):
                after(act, hid2_ready, 2 * (b - 1))
                act.activation(w1b[:, u, :], w1m[:, b, :], ACT.Copy).then_inc(w1b_ready, 1)

            def relu_d(b, u):
                for f in range(2):
                    after(act, hid2_ready, 2 * b + 1)
                    after(act, out_ready, b - 1)
                    act.activation(hid2[:, u, f, :], bank[2 * u][:, f * T:(f + 1) * T], ACT.Relu,
                                   bias=b1m[:, f, bass.ds(b, 1)]).then_inc(relu2_act, 1)

            act.wait_ge(merged_dve, 32)
            pipeline(act, [(load_w1, 0), (relu_d, 1)], NB)

        @block.vector
        def _(dve):
            add, mult, sub = ALU.add, ALU.mult, ALU.subtract
            flat = lambda t: t.rearrange("p k d -> p (k d)")
            dve.wait_ge(ld_const, 16)
            dve.wait_ge(ld_tok, 16 * 12)
            dve.wait_ge(prep_pe, 1)
            dve.tensor_copy(embT, bank[0][:, 0:P])
            dve.tensor_copy(wvT, bank[0][:, P:2 * P]).then_inc(prep_dve, 1)
            dve.tensor_copy(bvbc, tcol[:, 2:3].to_broadcast([P, P]))
            dve.tensor_copy(wpre[:, 0:2, :], wtok[:, 0:2, :])
            dve.wait_ge(prep_pe, 2)
            dve.tensor_copy(wpre[:, 2, :], bank[1][:, 0:D]).then_inc(prep_dve, 1)
            dve.tensor_copy(tab[:, 2, :], emb)
            dve.wait_ge(prep_pe, 3)
            dve.tensor_copy(tab[:, 0:2, :], bank[2][:, 0:2 * D].rearrange("p (k d) -> p k d", k=2))
            dve.tensor_copy(tab[:, 3, :], bank[2][:, 2 * D:3 * D]).then_inc(prep_dve, 1)
            dve.wait_ge(prep_dve, 3)
            dve.tensor_copy(tab_hi[:], tab).then_inc(prep_dve, 1)
            dve.wait_ge(prep_dve, 4)
            dve.tensor_tensor(tab_lo[:], tab, tab_hi[:].bitcast(F32), sub).then_inc(prep_dve, 1)
            dve.wait_ge(prep_pe, 4)
            for k in range(2):
                dve.tensor_scalar(c_qk[:, k, :], bank[3][:, k * T:(k + 1) * T], tcol[:, k:k + 1], None, add)
            dve.wait_ge(prep_pe, 5)
            for k in range(2):
                dve.tensor_tensor(c_xv[:, k, 0, :], cst[:, C_PE + k * P:C_PE + (k + 1) * P], bo_bc, add)
                ins = dve.tensor_copy(c_xv[:, k, 1, :], bank[4][:, k * D:(k + 1) * D])
            ins.then_inc(prep_dve, 1)

            dve.wait_ge(prep_dve, 6)

            def copy_qk(b, u):
                after(dve, qk_gathered, b + 1)
                after(dve, scores_ready, b - 1)
                dve.tensor_tensor(qk_s[:, u].rearrange("p k t -> p (k t)"), bank[u][:],
                                  flat(c_qk), add).then_inc(qk_copied, 1)

            def copy_xv(b, u):
                after(dve, xv_gathered, b + 1)
                dve.tensor_tensor(xv_all[:, b, :], bank[2][:],
                                  c_xv.rearrange("p k j d -> p (k j d)"), add).then_inc(xv_copied, 1)

            def row_max(b, u):
                after(dve, scores_ready, b + 1)
                after(dve, nmax_ready, b - 1)
                dve.tensor_reduce(rmax[:, u, :], bank[4 + u][:].rearrange("p (q k) -> p q k", q=2),
                                  AX.X, ALU.max).then_inc(rmax_ready, 1)

            def scaled_max(b, u):
                after(dve, rmax_ready, b + 1)
                after(dve, probs_ready, b - 1)
                dve.tensor_scalar(nmax[:, u, :], rmax[:, u, :], -TOK_SCALE, None, mult)\
                    .then_inc(nmax_ready, 1)

            def invert_sums(b, u):
                after(dve, probs_ready, b + 1)
                dve.reciprocal(rsum[:, u, :], psums[:, u, :]).then_inc(rsum_ready, 1)

            def residual_a(b, u):
                after(dve, rsum_ready, b + 1)
                after(dve, xv_copied, b + 1)
                after(dve, av_ready, b + 1)
                after(dve, x13_turned, b - 1)
                for q in range(2):
                    ins = dve.scalar_tensor_tensor(x13_s[:, u, q * P:(q + 1) * P], bank[7][:, q * P:(q + 1) * P],
                                                   rsum[:, u, q:q + 1], xv_all[:, b, q * T:q * T + P],
                                                   mult, add)
                ins.then_inc(x13_ready, 1)

            def stats_a(b, u):
                held_until(dve, x13_ready, b + 1)
                dve.bn_stats(stats[:, b, :], x13_s[:, u, :]).then_inc(stat_dve_bn, 1)

            def global_affine(r, n, gcols):
                s = gaff[:, 2 * r:2 * r + 1]
                bn_base = NB * (1 if r else 0)
                dve.wait_ge(stat_dve_bn, bn_base + n)
                dve.bn_aggr(gstat[:, 0:2], stats[:, 0:n, :].rearrange("p b s -> p (b s)")).then_inc(stat_dve, 1)
                dve.wait_ge(stat_pe, 2 * r + 1)
                dve.tensor_copy(gstat[:, 2:3], bank[7][:, 0:1]).then_inc(stat_own, 1)
                dve.wait_ge(stat_dve, 3 * r + 1)
                dve.wait_ge(stat_own, 6 * r + 1)
                dve.tensor_tensor(gstat[:, 3:4], gstat[:, 0:1], gstat[:, 2:3], sub).then_inc(stat_own, 1)
                dve.wait_ge(stat_own, 6 * r + 2)
                dve.scalar_tensor_tensor(gstat[:, 4:5], gstat[:, 3:4], gstat[:, 3:4], gstat[:, 1:2], mult, add)\
                    .then_inc(stat_dve, 1)
                dve.wait_ge(stat_pe, 2 * r + 2)
                dve.tensor_scalar(gstat[:, 5:6], bank[7][:, 1:2], COUNT / (COUNT - 1.0), None, mult)\
                    .then_inc(stat_dve, 1)
                dve.wait_ge(stat_pool, r + 1)
                dve.tensor_scalar(gstat[:, 7:8], gstat[:, 6:7], STD_EPS, None, add).then_inc(stat_own, 1)
                dve.wait_ge(stat_own, 6 * r + 3)
                dve.reciprocal(gstat[:, 8:9], gstat[:, 7:8]).then_inc(stat_own, 1)
                dve.wait_ge(stat_own, 6 * r + 4)
                dve.tensor_scalar(s, tcol[:, 4:5], gstat[:, 8:9], None, mult).then_inc(stat_own, 1)
                dve.wait_ge(stat_own, 6 * r + 5)
                dve.tensor_scalar(gstat[:, 9:10], gstat[:, 2:3], -1.0, None, mult).then_inc(stat_own, 1)
                dve.wait_ge(stat_own, 6 * r + 6)
                dve.scalar_tensor_tensor(gaff[:, 2 * r + 1:2 * r + 2], gstat[:, 9:10], s, tcol[:, 5:6], mult, add)\
                    .then_inc(affine_ready, 1)
                dve.wait_ge(affine_ready, r + 1)

            pipeline(dve, [(row_max, 2), (invert_sums, 4), (scaled_max, 2), (copy_qk, 1), (copy_xv, 1),
                           (stats_a, 5), (residual_a, 4)], NB)
            global_affine(0, NB, None)

            def norm_full(c, par):
                after(dve, x3_lo_ready, c - 1)
                dve.tensor_scalar(x3f[:, par, :], x13c(c), gaff[:, 0:1], gaff[:, 1:2], mult, add)\
                    .then_inc(x3_full, 1)

            def step_b(c, par):
                for f in (1, 3):
                    after(dve, hid_ready, 4 * c + f + 1)
                    after(dve, x4_ready, c)
                    dve.tensor_scalar(hid[:, f, :], bank[2 + f][:], tb1[:, f:f + 1], 0.0, add, ALU.max)\
                        .then_inc(relu_dve, 1)
                if not isinstance(c, int) or c < NCH - 1:
                    norm_full(c + 1, (par + 1) % 2)
                after(dve, x4_ready, c + 1)
                zc = z_all[:, bass.ds(c * CH, CH)]
                dve.scalar_tensor_tensor(zc, bank[6 + par][:], tcol[:, 3:4], x3f[:, par, :], add, add)\
                    .then_inc(z_ready, 1)
                held_until(dve, z_ready, c + 1)
                dve.bn_stats(stats[:, c, :], zc).then_inc(stat_dve_bn, 1)

            dve.wait_ge(ld_ffn, 16 * 6)
            dve.wait_ge(x13T_copied, NB)
            norm_full(0, 0)
            for c in range(2):
                step_b(c, c)
            with dve.Fori(1, NCH // 2 - 1) as pair:
                step_b(pair * 2, 0)
                step_b(pair * 2 + 1, 1)
            for c in range(NCH - 2, NCH):
                step_b(c, c % 2)
            global_affine(1, NCH, None)

            dve.wait_ge(ld_merge, 16 * 13)
            dve.tensor_tensor(tvd, tvln, lnp[0:E, :, :], sub).then_inc(prep_dve, 1)
            dve.wait_ge(prep_pe, 6)
            dve.tensor_copy(gw1T[:], bank[0][:, 0:P])
            dve.tensor_copy(gw2T[:], bank[0][:, P:P + E])
            dve.tensor_copy(gw2x[:], bank[0][:, P:P + E].unsqueeze(2).to_broadcast([P, E, X]))
            dve.tensor_copy(fw1T[:], bank[1][:])
            dve.tensor_copy(fw2T[:].rearrange("p c d -> p (c d)"), bank[2][:])
            dve.wait_ge(prep_pe, 7)
            dve.tensor_tensor(flat(lng), flat(lnp), bank[3][:, 0:2 * D], add).then_inc(prep_dve, 1)

            dve.wait_ge(ld_attn, 16 * 7)
            h_b, t_b, qk_b, v_b, l_b, r_b, g_b = bank[0:2], bank[2], bank[3], bank[4], bank[5], bank[6], bank[7]

            def row_stats(src, bn, u, done):
                dve.nop(nofuse=True)
                for k in range(2):
                    ins = dve.bn_stats(bn[:, u, k, :], src[k])
                ins.then_inc(done, 1)

            def row_aggregate(bn, mv, u, b, started, done):
                held_until(dve, started, b + 1)
                for k in range(2):
                    ins = dve.bn_aggr(mv[:, u, k, :], bn[:, u, k, :])
                ins.then_inc(done, 1)

            def stats_h(b, u):
                after(dve, h_turned, b + 1)
                row_stats([h_b[u][:, 0:P], h_b[u][:, P:T]], bn1, u, bn1_ready)

            def aggregate_h(b, u):
                after(dve, shift1_ready, b - 1)
                row_aggregate(bn1, mv1, u, b, bn1_ready, aggr1_ready)

            def variance_h(b, u):
                after(dve, aggr1_ready, b + 1)
                after(dve, rstd1_ready, b - 1)
                dve.tensor_scalar(ve1[:, u, :], mv1[:, u, :, 1], LN_EPS, None, add).then_inc(var1_ready, 1)

            def shift_h(b, u):
                after(dve, rstd1_ready, b + 1)
                after(dve, n_ready, b - 1)
                dve.scalar_tensor_tensor(nm1[:, u, :], mv1[:, u, :, 0], -1.0, rs1[:, u, :],
                                         mult, mult).then_inc(shift1_ready, 1)

            def add_hn(b, u):
                after(dve, n_ready, b + 1)
                dve.tensor_tensor(res2[:, b, :], h_b[u][:, 0:T], n_s[:, u, :], add).then_inc(hn_ready, 1)

            def bias_v(b, u):
                after(dve, qkv_ready, b + 1)
                after(dve, vp_ready, b - 1)
                dve.tensor_tensor(v_s[:, u, :], v_b[:, 0:T], flat(abv[:]), add).then_inc(v_copied, 1)

            def column_max(b, u):
                after(dve, logits_ready, b + 1)
                after(dve, ncmax_ready, b - 1)
                dve.tensor_reduce(rmax[:, u, 0:1], l_b[:, 0:T], AX.X, ALU.max)
                dve.tensor_reduce(rmax[:, u, 1:2], l_b[:, T:T + P], AX.X, ALU.max).then_inc(cmax_ready, 1)

            def negate_max(b, u):
                after(dve, cmax_ready, b + 1)
                after(dve, cprobs_ready, b - 1)
                dve.tensor_scalar(nmax[:, u, :], rmax[:, u, :], -1.0, None, mult).then_inc(ncmax_ready, 1)

            def invert_sums_c(b, u):
                after(dve, cprobs_ready, b + 1)
                after(dve, vp_ready, b - 1)
                dve.reciprocal(rsum[:, u, :], psums[:, u, :]).then_inc(csum_ready, 1)

            def scale_v(b, u):
                after(dve, csum_ready, b + 1)
                after(dve, v_copied, b + 1)
                after(dve, read_ready, b - 1)
                for k in range(2):
                    ins = dve.tensor_scalar(vp_s[:, u, k * P:(k + 1) * P], v_s[:, u, k * P:(k + 1) * P],
                                            rsum[:, u, k:k + 1], INV_SQRT_K, mult, mult)
                ins.then_inc(vp_ready, 1)

            def residual_c(b, u):
                after(dve, read_ready, b + 1)
                after(dve, hn_ready, b + 1)
                dve.tensor_tensor(res2[:, b, :], r_b[:, 0:T], res2[:, b, :], add).then_inc(h2_ready, 1)

            def stats_h2(b, u):
                after(dve, h2_ready, b + 1)
                row_stats([res2[:, b, 0:P], res2[:, b, P:T]], bn2, u, bn2_ready)

            def aggregate_h2(b, u):
                row_aggregate(bn2, mv2, u, b, bn2_ready, aggr2_ready)

            def variance_h2(b, u):
                after(dve, aggr2_ready, b + 1)
                after(dve, rstd2_ready, b - 1)
                dve.tensor_scalar(ve2[:, u, :], mv2[:, u, :, 1], LN_EPS, None, add).then_inc(var2_ready, 1)

            def norm_m(b, u):
                after(dve, rstd2_ready, b + 1)
                after(dve, m_turned, b - 1)
                after(dve, m_kept, b - 1)
                for k in range(2):
                    ins = dve.tensor_scalar(x13_s[:, u, k * P:(k + 1) * P], res2[:, b, k * P:(k + 1) * P],
                                            mv2[:, u, k, 0:1], rs2[:, u, k:k + 1], sub, mult)
                ins.then_inc(m_ready, 1)

            pipeline(dve, [(shift_h, L_N), (invert_sums_c, L_READ), (stats_h, L_TH), (scale_v, L_READ),
                           (aggregate_h, L_TH), (residual_c, L_H2), (variance_h, L_TH), (column_max, L_LOG),
                           (stats_h2, L_H2), (negate_max, L_LOG), (aggregate_h2, L_H2), (add_hn, L_N),
                           (variance_h2, L_H2), (norm_m, L_M), (bias_v, L_QKV)], NB)

            dve.wait_ge(g_pe, 1)
            dve.tensor_scalar(grep[:], bank[7][:, 0:NB], 1.0 / T, gcol[:, 1:2], mult, add)
            dve.tensor_scalar(gT[:], bank[7][0:E, NB:2 * NB], 1.0 / T, gb2[:, 0:1], mult, add).then_inc(g_dve, 1)
            dve.wait_ge(g_dve, 1)
            dve.tensor_tensor(gdiag[:], grep[:].unsqueeze(2).to_broadcast([P, NB, X]),
                              cst[:, C_DIAG:C_DIAG + X].unsqueeze(1).to_broadcast([P, NB, X]), mult)\
                .then_inc(g_dve, 1)
            dve.tensor_copy(gbc, gT[:].unsqueeze(2).to_broadcast([E, NB, P])).then_inc(g_dve, 1)

            def merged(p, count):
                dve.wait_ge(merged_pe, count + 1)
                src = bank[count % 4][:].rearrange("p (j b x) -> p j b x", j=2, b=NB)
                f0 = 2 * p * X
                if count < 16:
                    dst = w1m[:, :, f0:f0 + 2 * X].rearrange("p b (j x) -> p j b x", j=2)
                    base = fw1T[:, f0:f0 + 2 * X].rearrange("p (j x) -> p j x", j=2)
                else:
                    dc, c = 2 * p // FCH, 2 * p % FCH
                    dst = w2m[:, :, c:c + 2, dc * X:(dc + 1) * X].rearrange("p b j x -> p j b x")
                    base = fw2T[:, c:c + 2, dc * X:(dc + 1) * X]
                dve.tensor_tensor(dst, src, base.unsqueeze(2).to_broadcast([P, 2, NB, X]), add)\
                    .then_inc(merged_dve, 1)

            for p in range(16):
                merged(p, p)
            dve.wait_ge(g_pe, 2)
            dve.tensor_tensor(b1m[:], bank[6][:, 0:FCH * NB].rearrange("p (c b) -> p c b", c=FCH),
                              fb1[:].unsqueeze(2).to_broadcast([P, FCH, NB]), add).then_inc(g_dve, 1)
            for q in range(4):
                dve.wait_ge(g_pe, 3 + q)
                dve.tensor_tensor(b2m[:, 4 * q:4 * q + 4, :], bank[4 + q % 2][:].rearrange("p (b d) -> p b d", b=4),
                                  fb2[:].unsqueeze(1).to_broadcast([P, 4, D]), add).then_inc(g_dve, 1)
            for p in range(16):
                merged(p, 16 + p)

            def relu_d(b, u):
                for f in range(2, 4):
                    after(dve, hid2_ready, 2 * b + 2)
                    after(dve, out_ready, b - 1)
                    dve.tensor_scalar(hid2[:, u, f, :], bank[2 * u + 1][:, (f - 2) * T:(f - 1) * T],
                                      b1m[:, f, bass.ds(b, 1)], 0.0, add, ALU.max).then_inc(relu2_dve, 1)

            def residual_d(b, u):
                after(dve, out_ready, b + 1)
                after(dve, mb_ready, b + 1)
                dve.tensor_tensor(r_s[:, u, :], bank[6 + u][:, 0:T], x13[:, b, :], add).then_inc(res_ready, 1)

            def stats_d(b, u):
                after(dve, res_ready, b + 1)
                row_stats([r_s[:, u, 0:P], r_s[:, u, P:T]], bn1, u, bn3_ready)

            def aggregate_d(b, u):
                row_aggregate(bn1, mv1, u, b, bn3_ready, aggr3_ready)

            def variance_d(b, u):
                after(dve, aggr3_ready, b + 1)
                after(dve, rstd3_ready, b - 1)
                dve.tensor_scalar(ve1[:, u, :], mv1[:, u, :, 1], LN_EPS, None, add).then_inc(var3_ready, 1)

            def center(b, u):
                for k in range(2):
                    ins = dve.scalar_tensor_tensor(ln_s[:, u, k * P:(k + 1) * P], r_s[:, u, k * P:(k + 1) * P],
                                                   mv1[:, u, k, 0:1], lng[:, 0, :], sub, mult)
                ins.then_inc(scaled_ready, 1)

            def finish(b, u):
                after(dve, scaled_ready, b + 1)
                after(dve, rstd3_ready, b + 1)
                after(dve, hlb_ready, b + 1)
                after(dve, stored[u], 8 * (b - u))
                for k in range(2):
                    ins = dve.scalar_tensor_tensor(o_s[:, u, k * P:(k + 1) * P], ln_s[:, u, k * P:(k + 1) * P],
                                                   rs1[:, u, k:k + 1], res2[:, b, k * P:(k + 1) * P],
                                                   mult, add)
                ins.then_inc(o_ready, 1)

            pipeline(dve, [(residual_d, 1), (relu_d, 0), (stats_d, 1), (center, 2), (aggregate_d, 1),
                           (finish, 2), (variance_d, 1)], NB)

        @block.gpsimd
        def _(pool):
            pool.memset(nhalf[:, 0:2], -0.5)
            pool.memset(nhalf[:, 2:4], 0.5).then_inc(pool_const, 1)
            pool.wait_ge(ld_const, 16)
            pool.wait_ge(ld_ids, 16 * 4)

            def one_hot(b, u):
                after(pool, xv_gathered, b - 1)
                pool.tensor_scalar(onehot[:, u, :], ids[:, b * T:(b + 1) * T],
                                   cst[:, C_IOTA:C_IOTA + 1], None, ALU.is_equal).then_inc(onehot_ready, 1)

            for b in range(NB):
                one_hot(b, b % 2)
            pool.wait_ge(ld_ffn, 16 * 6)
            pool.tensor_copy(w1_hi[:], w1s).then_inc(prep_pool, 1)
            pool.wait_ge(prep_pool, 1)
            pool.tensor_tensor(w1_lo[:], w1s, w1_hi[:].bitcast(F32), ALU.subtract).then_inc(prep_pool, 1)
            pool.wait_ge(ld_const, 16)
            pool.tensor_copy(ident_b[:], ident)
            pool.memset(maskT[:], 0.0).then_inc(pool_const, 1)
            pool.wait_ge(pool_const, 2)
            pool.affine_select(out=maskT[:], in_=maskT[:], compare_op=ALU.is_ge, fill=MASKED, base=0,
                               pattern=[[1, P]], channel_multiplier=-1).then_inc(pool_const, 1)

            def root(r):
                pool.wait_ge(stat_dve, 3 * r + 3)
                pool.tensor_tensor(gstat[:, 6:7], gstat[:, 5:6], nhalf[:, 2:3], ALU.pow).then_inc(stat_pool, 1)

            root(0)

            def step_b(c, par):
                pool.wait_ge(x3_hi_ready, c + 1)
                pool.wait_ge(x3_full, c + 1)
                after(pool, hid_ready, 4 * (c - 1))
                pool.tensor_tensor(x3_lo[:, par, :], x3f[:, par, :], x3_hi[:, par, :].bitcast(F32),
                                   ALU.subtract).then_inc(x3_lo_ready, 1)

            for c in range(2):
                step_b(c, c)
            with pool.Fori(1, NCH // 2) as pair:
                step_b(pair * 2, 0)
                step_b(pair * 2 + 1, 1)
            root(1)

            def rstd_h(b, u):
                after(pool, var1_ready, b + 1)
                after(pool, n_ready, b - 1)
                pool.tensor_tensor(rs1[:, u, :], ve1[:, u, :], nhalf[:, 0:2], ALU.pow).then_inc(rstd1_ready, 1)

            def rstd_h2(b, u):
                after(pool, var2_ready, b + 1)
                after(pool, m_ready, b - 1)
                pool.tensor_tensor(rs2[:, u, :], ve2[:, u, :], nhalf[:, 0:2], ALU.pow).then_inc(rstd2_ready, 1)

            def keep_m(b, u):
                after(pool, m_ready, b + 1)
                pool.tensor_copy(x13[:, b, :], x13_s[:, u, :]).then_inc(m_kept, 1)

            pipeline(pool, [(rstd_h, L_TH), (rstd_h2, L_H2), (keep_m, L_M)], NB)

            def add_biases(b, u):
                for k in range(2):
                    ins = pool.tensor_tensor(x13[:, b, k * P:(k + 1) * P], x13[:, b, k * P:(k + 1) * P],
                                             b2m[:, b, :], ALU.add)
                ins.then_inc(mb_ready, 1)
                for k in range(2):
                    ins = pool.tensor_tensor(res2[:, b, k * P:(k + 1) * P], res2[:, b, k * P:(k + 1) * P],
                                             lng[:, 1, :], ALU.add)
                ins.then_inc(hlb_ready, 1)

            def rstd_d(b, u):
                after(pool, var3_ready, b + 1)
                after(pool, o_ready, b - 1)
                pool.tensor_tensor(rs1[:, u, :], ve1[:, u, :], nhalf[:, 0:2], ALU.pow).then_inc(rstd3_ready, 1)

            pool.wait_ge(m_kept, NB)
            pool.wait_ge(g_dve, 8)
            pool.wait_ge(prep_dve, 8)
            pipeline(pool, [(add_biases, 0), (rstd_d, 1)], NB)


_NAMES = ["x"] + [f"L0_tok_{n}" for n in ("emb", "Wq", "bq", "Wk", "bk", "Wv", "bv", "Wo", "bo", "W1", "b1",
                                          "W2", "b2", "gamma", "beta")]
_NAMES += [f"L0_attn_{n}" for n in ("Wk", "bk", "Wq", "bq", "Wv", "bv")]
_NAMES += [f"L0_ffn_{n}" for n in ("gfc1_w", "gfc1_b", "gfc2_w", "gfc2_b", "W1", "b1", "W2", "b2", "ln_g",
                                   "ln_b", "tv_W1", "tv_b1", "tv_W2", "tv_b2", "tv_ln_g", "tv_ln_b")]


def kernel(**inputs):
    import concourse.bacc as bacc
    from concourse.bass_utils import run_bass_kernel_spmd

    nc = bacc.Bacc("TRN2", target_bir_lowering=False, num_devices=1)
    tokens, features = inputs["x"].shape[1], inputs["L0_tok_emb"].shape[1]
    arrays = {n: np.ascontiguousarray(inputs[n]) for n in _NAMES}
    arrays["constants"] = shape_constants(tokens, features)
    args = {n: nc.dram_tensor(f"in_{n}", v.shape, mybir.dt.from_np(v.dtype), kind="ExternalInput").ap()
            for n, v in arrays.items()}
    out = nc.dram_tensor("out", (*inputs["x"].shape, features), F32, kind="ExternalOutput").ap()
    build(nc, args, out)
    r = run_bass_kernel_spmd(nc, [{f"in_{n}": v for n, v in arrays.items()}], core_ids=[0])
    return r.results[0]["out"]
```

```python
import math
from contextlib import ExitStack

import numpy as np

import concourse.bass as bass
from concourse import mybir

F32 = mybir.dt.float32
F32R = mybir.dt.float32r
BF16 = mybir.dt.bfloat16
I32 = mybir.dt.int32
ALU = mybir.AluOpType
ACT = mybir.ActivationFunctionType
AX = mybir.AxisListType

P = 128
MASKED = -1.0e30
LN_MERGE = 0.03

PACKS = {
    "tables": (("WvT", 128), ("Wo", 128), ("embT", 128), ("Wq", 128), ("Wk", 128), ("emb", 128),
               ("bq", 1), ("bk", 1), ("bv", 1), ("b2", 1), ("gamma", 1), ("beta", 1), ("b1", 4), ("iota", 1)),
    "const": (("pe", 256),
              ("peT", 256),
              ("ident", 128), ("avg", 128),
              ("diag", 16),
              ("merge", 128)),
    "ffn": (("W1", 512), ("W2", 512)),
    "attn": (("aWq", 128), ("aWk", 128), ("aWv", 128), ("abq", 1), ("abk", 1)),
    "later": (("gw1T", 128), ("gw2T", 8), ("gw2x", 128), ("gb1", 1), ("gb2x", 1),
              ("fw1T", 512), ("fw2T", 512), ("fb1", 4)),
    "rows_early": (("bo", 128), ("ln_g", 128), ("ln_b", 128)),
    "rows_late": (("abv", 256), ("fb2", 128)),
    "tasks": (("tvb1", 512), ("tvb2", 128), ("gb2", 1), ("tv_ln_g", 128), ("tv_ln_b", 128)),
}


def width(pack):
    return sum(w for _, w in PACKS[pack])


def columns(tile, pack, first, last=None):
    names = [n for n, _ in PACKS[pack]]
    start = lambda k: sum(w for _, w in PACKS[pack][:k])
    return tile[:, start(names.index(first)):start(names.index(last or first) + 1)]


def shape_constants(tokens, features):
    pos = np.arange(tokens, dtype=np.float32)[:, None]
    i = np.arange(features, dtype=np.float32)[None, :]
    angle = pos / np.power(np.float32(10000.0), np.float32(2.0) * i / np.float32(features))
    pe = np.where((np.arange(features) % 2 == 0)[None, :], np.sin(angle), np.cos(angle))
    pe = pe.astype(np.float32)
    index = np.arange(P, dtype=np.float32)[:, None]
    return {"pe": pe.reshape(2, P, features).transpose(1, 0, 2).reshape(P, 2 * features), "peT": pe.T,
            "ident": np.eye(P, dtype=np.float32), "avg": np.full((P, P), 1.0 / P, np.float32),
            "diag": (index % 16 == index[:16].T).astype(np.float32),
            "merge": np.full((P, P), LN_MERGE, np.float32), "iota": index}


def lay_out(inputs):
    tok = {n[7:]: v for n, v in inputs.items() if n.startswith("L0_tok_")}
    attn = {n[8:]: v for n, v in inputs.items() if n.startswith("L0_attn_")}
    ffn = {n[7:]: v for n, v in inputs.items() if n.startswith("L0_ffn_")}
    column = lambda v: v.reshape(-1, P).T
    X = P // ffn["tv_W1"].shape[0]
    blocks = dict(shape_constants(inputs["x"].shape[1], tok["emb"].shape[1]))
    blocks.update({n: tok[n] for n in ("Wo", "Wq", "Wk", "emb", "W1")})
    blocks.update({n: column(tok[n]) for n in ("bq", "bk", "bv", "b2", "gamma", "beta", "b1")})
    blocks.update({
        "WvT": tok["Wv"].T, "embT": tok["emb"].T,
        "W2": tok["W2"].reshape(-1, P, P).transpose(1, 0, 2).reshape(P, -1),
        "aWq": attn["Wq"], "aWk": attn["Wk"], "aWv": attn["Wv"],
        "abq": column(attn["bq"]), "abk": column(attn["bk"]),
        "gw1T": ffn["gfc1_w"].T, "gw2T": ffn["gfc2_w"].T, "gw2x": np.repeat(ffn["gfc2_w"].T, X, axis=1),
        "gb1": column(ffn["gfc1_b"]), "gb2x": np.repeat(ffn["gfc2_b"], X)[:, None],
        "fw1T": ffn["W1"].T, "fb1": column(ffn["b1"]),
        "fw2T": ffn["W2"].T.reshape(-1, P, P).transpose(1, 0, 2).reshape(P, -1),
        "bo": tok["bo"][None], "ln_g": ffn["ln_g"][None], "ln_b": ffn["ln_b"][None],
        "abv": np.concatenate([attn["bv"], attn["bv"]])[None], "fb2": ffn["b2"][None],
        "tvb1": ffn["tv_b1"], "tvb2": ffn["tv_b2"], "gb2": ffn["gfc2_b"][:, None],
        "tv_ln_g": ffn["tv_ln_g"], "tv_ln_b": ffn["tv_ln_b"]})
    arrays = {pack: np.concatenate([blocks[n] for n, _ in PACKS[pack]], axis=1)
              for pack in PACKS}
    spread = lambda w: np.ascontiguousarray(
        w.reshape(w.shape[0], -1, X, w.shape[2]).transpose(0, 2, 1, 3).reshape(P, -1, w.shape[2]))
    arrays.update({"x": np.ascontiguousarray(inputs["x"]), "tv_W1": spread(ffn["tv_W1"]),
                   "tv_W2": spread(ffn["tv_W2"])})
    return arrays


def build(nc, a, out):
    NB, T = a["x"].shape
    E = a["tasks"].shape[0]
    FF = a["tv_W2"].shape[2]
    V = D = a["tv_W1"].shape[2]
    NT = NB * T
    FCH = FF // P
    X = P // E
    CH = 512
    NCH = NT // CH
    assert (D, V, T, NB, E, FF) == (P, P, 2 * P, 16, 8, 512)
    TOK_SCALE = 1.0 / math.sqrt(512.0)
    INV_SQRT_K = 1.0 / math.sqrt(float(D))
    LN_EPS = 1e-5
    STD_EPS = 1e-9
    COUNT = NT * D

    L_TN, L_TM, L_GATE = 3, 9, 10

    with ExitStack() as ctx:
        def sb(name, shape, dt=F32):
            return ctx.enter_context(nc.sbuf_tensor(name, shape, dt))

        def sem(name):
            return ctx.enter_context(nc.semaphore(name))

        cst = sb("cst", [P, width("const")])
        z_all = sb("z_all", [P, NT])
        onehot = sb("onehot", [P, 2, T], F32R)
        x13 = sb("x13", [P, NB, T])
        res2 = sb("res2", [P, NB, T])
        mT = sb("mT", [P, NB, T])
        w1m = sb("w1m", [P, NB, FF])
        with ExitStack() as place:
            here = lambda name, shape, dt=F32: place.enter_context(nc.sbuf_tensor(name, shape, dt))
            hid_hi = here("hid_hi", [P, FCH, CH], F32R)
            hid_lo = here("hid_lo", [P, FCH, CH], F32R)
            hid_act = here("hid_act", [P, 2, CH])
            probT = here("probT", [P, 2, 2, T])
            w2_hi, w2_lo = (here(n, [P, FF], F32R) for n in ("w2_hi", "w2_lo"))
        with ExitStack() as place:
            hT = here("hT", [P, 2, T])
            n_s = here("n_s", [P, 2, T])
            nT = here("nT", [P, 2, T])
            v_s = here("v_s", [P, 2, T])
            vp_s = here("vp_s", [P, 2, T])
            gjunk = here("gjunk", [P, T])
        w2m = sb("w2m", [P, NB, FCH, D])
        tv1 = sb("tv1", [P, FF // X, D])
        with ExitStack() as place:
            tv2_lo = here("tv2_lo", [P, D // X, FF], F32R)
        tv2 = sb("tv2", [P, D // X, FF])
        xv_all = w1m
        early = res2[:].rearrange("p b t -> p (b t)")
        o = [0]
        def early_cols(n):
            o[0] += n
            return early[:, o[0] - n:o[0]]
        tables_in, ffn_in, rows_early = (early_cols(width(p)) for p in ("tables", "ffn", "rows_early"))
        of_tables = lambda first, last=None: columns(tables_in, "tables", first, last)
        emb, embT, wvT, wo = (of_tables(n) for n in ("emb", "embT", "WvT", "Wo"))
        tcol = of_tables("bq", "beta")
        tb1 = of_tables("b1")
        w1s = columns(ffn_in, "ffn", "W1")
        w2f = columns(ffn_in, "ffn", "W2")
        w2s = w2f.rearrange("p (c d) -> p c d", c=FCH)
        bo_bc = columns(rows_early, "rows_early", "bo")
        lnp = columns(rows_early, "rows_early", "ln_g", "ln_b").rearrange("p (k d) -> p k d", k=2)
        wvo = early_cols(D)
        bvbc = early_cols(P)
        c_qk = early_cols(2 * T).rearrange("p (k t) -> p k t", k=2)
        c_xv = early_cols(4 * D).rearrange("p (k j d) -> p k j d", k=2, j=2)
        tvd = early_cols(2 * D)[0:E, :].rearrange("e (k d) -> e k d", k=2)
        b2m = z_all[:, 0:NB * D].rearrange("p (b d) -> p b d", b=NB)
        gbc = z_all[0:E, NB * D:2 * NB * D].rearrange("p (b d) -> p b d", b=NB)
        hid2 = z_all[:, NB * D:2 * NB * D].rearrange("p (u f t) -> p u f t", u=2, f=4)

        tab_hi = sb("tab_hi", [P, 4, D], F32R)
        tab_lo = sb("tab_lo", [P, 4, D], F32R)
        w1_hi = sb("w1_hi", [P, FF], F32R)
        w1_lo = sb("w1_lo", [P, FF], F32R)
        attn_in = sb("attn_in", [P, width("attn")])
        aw = columns(attn_in, "attn", "aWq", "aWv").rearrange("p (k d) -> p k d", k=3)
        acol = columns(attn_in, "attn", "abq", "abk")
        later_in = sb("later_in", [P, width("later")])
        of_later = lambda first, last=None: columns(later_in, "later", first, last)
        gw1T, gw2T, fw1T, fb1 = (of_later(n) for n in ("gw1T", "gw2T", "fw1T", "fb1"))
        gw2x = of_later("gw2x")
        gcol = of_later("gb1", "gb2x")
        fw2T = of_later("fw2T").rearrange("p (c d) -> p c d", c=FCH)
        rows_late = sb("rows_late", [P, width("rows_late")])
        abv = columns(rows_late, "rows_late", "abv")
        fb2 = columns(rows_late, "rows_late", "fb2")
        tasks_in = sb("tasks_in", [E, width("tasks")])
        tvb1, tvb2, gb2 = (columns(tasks_in, "tasks", n) for n in ("tvb1", "tvb2", "gb2"))
        tvln = columns(tasks_in, "tasks", "tv_ln_g", "tv_ln_b").rearrange("e (k d) -> e k d", k=2)
        lng = sb("lng", [P, 2, D])
        maskT = sb("maskT", [P, P], BF16)
        ident_b = sb("ident_b", [P, P], BF16)
        nhalf = sb("nhalf", [P, 4])

        qk_s = sb("qk_s", [P, 2, 2, T])
        prob = sb("prob", [P, 2, 2, T])
        x13_s = sb("x13_s", [P, 2, T])
        r_s = qk_s[:, :, 0, :]
        ln_s = qk_s[:, :, 1, :]
        o_s = prob[:, :, 0, :]
        nmax = sb("nmax", [P, 2, 2])
        rmax = sb("rmax", [P, 2, 2])
        psums = sb("psums", [P, 2, 2])
        rsum = sb("rsum", [P, 2, 2])
        stats = sb("stats", [P, NB, 6])
        gstat = sb("gstat", [P, 12])
        gaff = sb("gaff", [P, 3])
        bparts = sb("bparts", [P, 2, FCH + 1])
        bvec = sb("bvec", [P, FCH + 1])
        nbvec = sb("nbvec", [P, FCH])
        obase = sb("obase", [P, 2])

        x_hi = sb("x_hi", [P, 2, CH], F32R)
        x_lo = sb("x_lo", [P, 2, CH], F32R)
        tv2_hi = (x_hi[:, 0, :], x_lo[:, 0, :], w1_hi[:], w1_lo[:], x_hi[:, 1, :], x_lo[:, 1, :],
                  tab_hi[:].rearrange("p k d -> p (k d)"), tab_lo[:].rearrange("p k d -> p (k d)"))

        w1b_hi, w1b_lo = x_hi, x_lo
        mTb_hi, mTb_lo = (t[:].rearrange("p (u t) -> p u t", u=2) for t in (w1_hi, w1_lo))

        bn1 = sb("bn1", [P, 2, 2, 6])
        mv1 = sb("mv1", [P, 2, 2, 2])
        ve1 = sb("ve1", [P, 2, 2])
        rs1 = sb("rs1", [P, 2, 2])
        nm1 = sb("nm1", [P, 2, 2])
        bn2 = sb("bn2", [P, 2, 2, 6])
        mv2 = sb("mv2", [P, 2, 2, 2])
        ve2 = sb("ve2", [P, 2, 2])
        rs2 = sb("rs2", [P, 2, 2])
        ghsum = sb("ghsum", [P, NB])
        gT = sb("gT", [E, NB])
        grep = sb("grep", [P, NB])
        gdiag_hi, gdiag_lo = onehot[:, 0, :], onehot[:, 1, :]
        gdiag = sb("gdiag", [P, NB, X])
        b1m = sb("b1m", [P, FCH, NB])

        bank = [ctx.enter_context(nc.psum_tensor(f"bank{i}", [P, 512], F32)) for i in range(8)]

        ld_ids = [sem(f"ld_ids{k}") for k in range(4)]
        ld_const, ld_codes, ld_tok, ld_tok2, ld_rows, ld_ffn, ld_attn, ld_later, ld_tv = (
            sem(n) for n in ("ld_const", "ld_codes", "ld_tok", "ld_tok2", "ld_rows", "ld_ffn", "ld_attn",
                             "ld_later", "ld_tv"))
        prep_pe, prep_act, prep_dve, prep_pool, onehot_ready = (
            sem(n) for n in ("prep_pe", "prep_act", "prep_dve", "prep_pool", "onehot_ready"))
        qk_gathered, xv_gathered, qk_copied, xv_copied = (
            sem(n) for n in ("qk_gathered", "xv_gathered", "qk_copied", "xv_copied"))
        scores_ready, rmax_ready, nmax_ready, probs_ready = (
            sem(n) for n in ("scores_ready", "rmax_ready", "nmax_ready", "probs_ready"))
        probs_turned, probT_ready, av_ready, rsum_ready, x13_ready = (
            sem(n) for n in ("probs_turned", "probT_ready", "av_ready", "rsum_ready", "x13_ready"))
        stat_dve, stat_own, bn_global_ready, stat_pe, stat_pool, affine_ready, pool_const = (
            sem(n) for n in ("stat_dve", "stat_own", "bn_global_ready", "stat_pe", "stat_pool", "affine_ready",
                             "pool_const"))
        x13_turned, x13T_copied, x_hi_ready, x_lo_ready, bparts_pe, bparts_dve = (
            sem(n) for n in ("x13_turned", "x13T_copied", "x_hi_ready", "x_lo_ready", "bparts_pe",
                             "bparts_dve"))
        hid_ready, relu_act, hi_act, lo_pool, hi_dve, lo_dve, hid_used, z_ready = (
            sem(n) for n in ("hid_ready", "relu_act", "hi_act", "lo_pool", "hi_dve", "lo_dve", "hid_used",
                             "z_ready"))
        hT_ready, h_turned, bn1_ready, aggr1_ready, var1_ready, rstd1_ready = (
            sem(n) for n in ("hT_ready", "h_turned", "bn1_ready", "aggr1_ready", "var1_ready",
                             "rstd1_ready"))
        shift1_ready, n_ready, hn_ready, n_turned, nT_ready = (
            sem(n) for n in ("shift1_ready", "n_ready", "hn_ready", "n_turned", "nT_ready"))
        qkv_ready, qk2_copied, v_copied, logits_ready = (
            sem(n) for n in ("qkv_ready", "qk2_copied", "v_copied", "logits_ready"))
        cmax_ready, ncmax_ready, cprobs_ready, csum_ready, vp_ready, read_ready = (
            sem(n) for n in ("cmax_ready", "ncmax_ready", "cprobs_ready", "csum_ready", "vp_ready",
                             "read_ready"))
        h2_ready, bn2_ready, aggr2_ready, var2_ready, rstd2_ready = (
            sem(n) for n in ("h2_ready", "bn2_ready", "aggr2_ready", "var2_ready", "rstd2_ready"))
        m_ready, m_kept, m_turned, mT_ready, gate_ready, gate_summed = (
            sem(n) for n in ("m_ready", "m_kept", "m_turned", "mT_ready", "gate_ready", "gate_summed"))
        tv2_rounded, tv2_split, gdiag_split = (sem(n) for n in ("tv2_rounded", "tv2_split", "gdiag_split"))
        g_pe, gates_ready, biases_pe, biases_ready, merged_pe, merged_dve = (
            sem(n) for n in ("g_pe", "gates_ready", "biases_pe", "biases_ready", "merged_pe", "merged_dve"))
        hid2_ready, hi_ready, split_ready, relu2_act, relu2_dve, out_ready, mb_ready, hlb_ready = (
            sem(n) for n in ("hid2_ready", "hi_ready", "split_ready", "relu2_act", "relu2_dve",
                             "out_ready", "mb_ready",
                             "hlb_ready"))
        res_ready, bn3_ready, aggr3_ready, var3_ready, rstd3_ready, scaled_ready, o_ready = (
            sem(n) for n in ("res_ready", "bn3_ready", "aggr3_ready", "var3_ready", "rstd3_ready",
                             "scaled_ready", "o_ready"))
        stored = [sem("stored_even"), sem("stored_odd")]

        pe_code, peT, ident, avg, diag, merge_c = (
            columns(cst, "const", n) for n in ("pe", "peT", "ident", "avg", "diag", "merge"))
        ids = z_all[:].bitcast(I32)
        ID_ENDS = (0, 2, 4, 8, NB)

        def x13c(c):
            return x13[:].rearrange("p b t -> p (b t)")[:, bass.ds(c * CH, CH)]

        def pipeline(eng, stages, n, in_tail=None, tail=0, unroll=2):
            depth = max(lag for _, lag in stages)
            head = -(-(depth + 2) // unroll) * unroll

            def edge(i):
                for stage, lag in stages:
                    if 0 <= i - lag < n:
                        stage(i - lag, (i - lag) % 2)

            for i in range(head):
                edge(i)
            if head < n:
                with eng.Fori(head // unroll, n // unroll) as turn:
                    for j in range(unroll):
                        for stage, lag in stages:
                            stage(turn * unroll + (j - lag), (j - lag) % 2)
            for i in range(max(head, n), n + max(depth, tail)):
                edge(i)
                if in_tail:
                    in_tail(i)

        BEFORE_BIASES = 4

        def merge_bank(c):
            return c % 2 if c < 8 else c % 4

        IN_TAIL = {4: (0,), 5: (1,), 6: (2, 3), 7: (4, 5), 8: (6,), 9: (7,)}

        def after(eng, s, count):
            if not isinstance(count, int) or count > 0:
                eng.wait_ge(s, count)

        def held_until(eng, s, count):
            after(eng, s, count)
            eng.nop(nofuse=True)

        def skip(k, stage):
            return lambda b, u: None if isinstance(b, int) and b < k else stage(b, u)

        block = ctx.enter_context(nc.Block())

        @block.sync
        def _(sp):
            def load(tile, pack, sem):
                sp.dma_start(tile[:], a[pack]).then_inc(sem, 16)

            def load_rows(tile, pack, sem):
                sp.dma_start(tile[:], a[pack].broadcast_to([P, width(pack)])).then_inc(sem, 16)

            def load_ids(k):
                lo, hi = ID_ENDS[k] * T, ID_ENDS[k + 1] * T
                row = a["x"].rearrange("b t -> (b t)")[lo:hi].rearrange("(o d) -> o d", o=1)
                sp.dma_start(ids[:, lo:hi], row.broadcast_to([P, hi - lo])).then_inc(ld_ids[k], 16)

            half = 2 * P
            sp.dma_start(tables_in[:, 0:half], a["tables"][:, 0:half]).then_inc(ld_tok, 16)
            sp.dma_start(tables_in[:, half:], a["tables"][:, half:]).then_inc(ld_tok2, 16)
            codes = 2 * T
            sp.dma_start(cst[:, 0:codes], a["const"][:, 0:codes]).then_inc(ld_codes, 16)
            load_ids(0)
            sp.dma_start(cst[:, codes:], a["const"][:, codes:]).then_inc(ld_const, 16)
            load_rows(rows_early, "rows_early", ld_rows)
            for k in range(1, 4):
                load_ids(k)
            load(ffn_in, "ffn", ld_ffn)
            load(attn_in, "attn", ld_attn)
            load_rows(rows_late, "rows_late", ld_attn)
            load(later_in, "later", ld_later)
            load(tasks_in, "tasks", ld_later)
            sp.dma_start(tv1[:], a["tv_W1"]).then_inc(ld_tv, 16)
            sp.dma_start(tv2[:], a["tv_W2"]).then_inc(ld_tv, 16)

            def store(b, par):
                after(sp, o_ready, b + 1)
                sp.dma_start(out[b].rearrange("(k p) d -> p k d", p=P),
                             o_s[:, par, :].rearrange("p (k d) -> p k d", k=2)).then_inc(stored[par], 16)

            with sp.Fori(0, NB // 2) as pair:
                store(pair * 2, 0)
                store(pair * 2 + 1, 1)
            for par in range(2):
                sp.wait_ge(stored[par], 8 * NB)

        @block.tensor
        def _(pe):
            pe.wait_ge(ld_tok, 16)
            pe.matmul(bank[1][:, 0:D], wvT, wo, start=True, stop=True).then_inc(prep_pe, 1)
            pe.wait_ge(ld_tok2, 16)
            pe.matmul(bank[2][:, 0:2 * D], embT, of_tables("Wq", "Wk"), start=True, stop=True)\
                .then_inc(prep_pe, 1)
            pe.wait_ge(prep_dve, 1)
            pe.matmul(bank[5][:, 0:D], embT, wvo, start=True, stop=False)
            pe.matmul(bank[5][:, 0:D], bvbc, wo, start=False, stop=True).then_inc(prep_pe, 1)

            pe.wait_ge(ld_codes, 16)
            for k, w in enumerate(("Wq", "Wk")):
                mm = pe.matmul(bank[3][:, k * T:(k + 1) * T], of_tables(w), peT, start=True, stop=True)
            mm.then_inc(prep_pe, 1)
            for k in range(2):
                mm = pe.matmul(bank[4][:, k * D:(k + 1) * D], peT[:, k * P:(k + 1) * P], wvo,
                               start=True, stop=True)
            mm.then_inc(prep_pe, 1)
            pe.wait_ge(prep_dve, 4)

            qk_b, xv_b, s_b, t_b, av_b, xt_b = bank[0:2], bank[2], bank[4:6], bank[6], bank[7], bank[3]

            def gather(b, u):
                after(pe, onehot_ready, b + 1)
                after(pe, qk_copied, b - 1)
                for k in range(2):
                    pe.matmul(qk_b[u][:, k * T:(k + 1) * T], tab_hi[:, k, :], onehot[:, u, :],
                              start=True, stop=False)
                    mm = pe.matmul(qk_b[u][:, k * T:(k + 1) * T], tab_lo[:, k, :], onehot[:, u, :],
                                   start=False, stop=True)
                mm.then_inc(qk_gathered, 1)
                after(pe, xv_copied, b)
                for k in range(2):
                    for part in (tab_hi, tab_lo):
                        mm = pe.matmul(xv_b[:, k * T:(k + 1) * T], onehot[:, u, k * P:(k + 1) * P],
                                       part[:, 2:4, :].rearrange("p k d -> p (k d)"),
                                       start=(part is tab_hi), stop=(part is tab_lo))
                mm.then_inc(xv_gathered, 1)

            def scores(b, u):
                after(pe, qk_copied, b + 1)
                after(pe, probs_ready, b - 1)
                for q in range(2):
                    mm = pe.matmul(s_b[u][:, q * T:(q + 1) * T], qk_s[:, u, 0, q * P:(q + 1) * P],
                                   qk_s[:, u, 1, :], start=True, stop=True)
                mm.then_inc(scores_ready, 1)

            def turn_probs(b, u):
                after(pe, probs_ready, b + 1)
                after(pe, probT_ready, b)
                for k in range(2):
                    for q in range(2):
                        mm = pe.transpose(t_b[:, (2 * k + q) * P:(2 * k + q + 1) * P],
                                          prob[:, u, q, k * P:(k + 1) * P], ident)
                mm.then_inc(probs_turned, 1)

            def probs_by_values(b, u):
                after(pe, probT_ready, b + 1)
                after(pe, x13_ready, b)
                for q in range(2):
                    for k in range(2):
                        mm = pe.matmul(av_b[:, q * P:(q + 1) * P], probT[:, u, k, q * P:(q + 1) * P],
                                       xv_all[:, b, k * T + P:k * T + 2 * P], start=(k == 0), stop=(k == 1))
                mm.then_inc(av_ready, 1)

            def turn_x13(b, u):
                after(pe, x13_ready, b + 1)
                after(pe, x13T_copied, b)
                for k in range(2):
                    mm = pe.transpose(xt_b[:, k * P:(k + 1) * P], x13_s[:, u, k * P:(k + 1) * P], ident)
                mm.then_inc(x13_turned, 1)

            pe.wait_ge(ld_const, 16)
            pipeline(pe, [(scores, 2), (gather, 0), (turn_probs, 3), (probs_by_values, 4),
                          (turn_x13, 5)], NB)
            pe.wait_ge(ld_ffn, 16)
            pe.wait_ge(probs_ready, NB)
            for f in range(FCH):
                mm = pe.matmul(bank[4][:, 2 * f:2 * f + 2], w1s[:, f * P:(f + 1) * P], tcol[:, 4:6],
                               start=True, stop=True)
            mm.then_inc(bparts_pe, 1)

            def partition_mean(r, k):
                pe.wait_ge(stat_dve, 3 * r + 1 + k)
                pe.matmul(bank[7][:, k:k + 1], avg, gstat[:, 4 * k:4 * k + 1], start=True, stop=True)\
                    .then_inc(stat_pe, 1)

            partition_mean(0, 0)

            h_b, x4_b = bank[2:6], bank[6:8]

            def hidden_chunk(c, par, f):
                after(pe, (lo_dve, relu_act)[f % 2], 2 * c - 1 + f // 2)
                w = slice(f * P, (f + 1) * P)
                pe.matmul(h_b[f][:], w1_hi[:, w], x_hi[:, par, :], start=True, stop=False)
                pe.matmul(h_b[f][:], w1_lo[:, w], x_hi[:, par, :], start=False, stop=False)
                pe.matmul(h_b[f][:], w1_hi[:, w], x_lo[:, par, :], start=False, stop=True)\
                    .then_inc(hid_ready, 1)

            def hidden_b(c, par):
                if isinstance(c, int) and c == 0:
                    return
                pe.wait_ge(x_lo_ready, c + 1)
                for f in range(FCH):
                    hidden_chunk(c, par, f)

            def project_b(c, par):
                after(pe, z_ready, c - 1)
                for f in range(FCH):
                    pe.wait_ge((lo_dve, lo_pool)[f % 2], 2 * c + 1 + f // 2)
                    w = slice(f * P, (f + 1) * P)
                    pe.matmul(x4_b[par][:], w2_hi[:, w], hid_hi[:, f, :], start=(f == 0), stop=False)
                    pe.matmul(x4_b[par][:], w2_lo[:, w], hid_hi[:, f, :], start=False, stop=False)
                    pe.matmul(x4_b[par][:], w2_hi[:, w], hid_lo[:, f, :], start=False, stop=(f == FCH - 1))\
                        .then_inc(hid_used, 1)

            partition_mean(0, 1)
            pe.wait_ge(prep_pool, 5)
            pe.wait_ge(x_lo_ready, 1)
            pe.wait_ge(x13T_copied, NB)
            pe.wait_ge(bparts_dve, 1)
            for f in (0, 2):
                pe.matmul(bank[5][:, 0:2], w2s[:, f, :], bparts[:, :, f], start=(f == 0), stop=(f == 2))
            pe.matmul(bank[5][:, 2 * D:4 * D], merge_c[0:E, :],
                      tvd.rearrange("e k d -> e (k d)"), start=True, stop=True).then_inc(bparts_pe, 1)
            hidden_chunk(0, 0, 0)
            hidden_chunk(0, 0, 1)
            hidden_chunk(0, 0, 2)
            pe.wait_ge(bparts_dve, 2)
            hidden_chunk(0, 0, 3)
            pe.wait_ge(probT_ready, NB)
            pipeline(pe, [(hidden_b, 0), (project_b, 1)], NCH)
            partition_mean(1, 0)
            partition_mean(1, 1)
            pe.wait_ge(ld_attn, 16 * 2)

            h_b, t_b, qk_b, v_b, l_b, r_b, g_b = bank[0:2], bank[2], bank[3], bank[4], bank[5], bank[6], bank[7]

            def turn_h(b, u):
                after(pe, hT_ready, b + 1)
                after(pe, hn_ready, b - 1)
                for k in range(2):
                    mm = pe.transpose(h_b[u][:, k * P:(k + 1) * P], hT[:, u, k * P:(k + 1) * P], ident)
                mm.then_inc(h_turned, 1)

            def turn_n(b, u):
                after(pe, n_ready, b + 1)
                after(pe, nT_ready, b)
                after(pe, mT_ready, b - (L_TM - L_TN))
                for k in range(2):
                    mm = pe.transpose(t_b[:, k * P:(k + 1) * P], n_s[:, u, k * P:(k + 1) * P], ident)
                mm.then_inc(n_turned, 1)

            def turn_m(b, u):
                after(pe, m_ready, b + 1)
                after(pe, mT_ready, b)
                for k in range(2):
                    mm = pe.transpose(t_b[:, T + k * P:T + (k + 1) * P], x13_s[:, u, k * P:(k + 1) * P], ident)
                mm.then_inc(m_turned, 1)

            def project(b, u):
                after(pe, nT_ready, b + 1)
                after(pe, qk2_copied, b)
                after(pe, v_copied, b)
                for k in range(2):
                    pe.matmul(qk_b[:, k * T:(k + 1) * T], aw[:, k, :], nT[:, u, :], start=True, stop=True)
                for k in range(2):
                    mm = pe.matmul(v_b[:, k * P:(k + 1) * P], nT[:, u, k * P:(k + 1) * P], aw[:, 2, :],
                                   start=True, stop=True)
                mm.then_inc(qkv_ready, 1)

            def logits(b, u):
                after(pe, qk2_copied, b + 1)
                after(pe, cprobs_ready, b)
                pe.matmul(l_b[:, 0:T], qk_s[:, u, 1, 0:P], qk_s[:, u, 0, :], start=True, stop=False,
                          skip_group_check=True)
                pe.matmul(l_b[:, T:T + P], qk_s[:, u, 1, P:T], qk_s[:, u, 0, P:T],
                          start=False, stop=False, skip_group_check=True)
                pe.matmul(l_b[:, 0:P], ident_b[:], maskT[:], start=False, stop=False,
                          skip_group_check=True)
                pe.matmul(l_b[:, T:T + P], ident_b[:], maskT[:], start=False, stop=True,
                          skip_group_check=True).then_inc(logits_ready, 1)

            def read(b, u):
                after(pe, vp_ready, b + 1)
                after(pe, h2_ready, b)
                pr = prob[:, u].rearrange("p k t -> p (k t)")
                pe.matmul(r_b[:, 0:P], pr[:, 0:P], vp_s[:, u, 0:P], start=True, stop=True)
                pe.matmul(r_b[:, P:T], pr[:, P:T], vp_s[:, u, 0:P], start=True, stop=False)
                pe.matmul(r_b[:, P:T], pr[:, T:T + P], vp_s[:, u, P:T], start=False, stop=True)\
                    .then_inc(read_ready, 1)

            def gate(b, u):
                after(pe, mT_ready, b + 1)
                after(pe, gate_summed, b)
                pe.matmul(g_b[:, 0:T], gw1T, mT[:, b, :], start=True, stop=True).then_inc(gate_ready, 1)

            def gates_pe(g, where):
                pe.wait_ge(gate_summed, 8 * (g + 1))
                pe.matmul(where[:, 0:8], gw2x, ghsum[:, 8 * g:8 * g + 8], start=True, stop=True)
                pe.matmul(where[0:E, 8:16], gw2T, ghsum[:, 8 * g:8 * g + 8], start=True, stop=True)\
                    .then_inc(g_pe, 1)

            def merge_w1(c):
                after(pe, merged_dve, c - 1 if c < 10 else c - 3)
                g, blk = c // 8, c % 8 * 4
                for j in range(4):
                    mm = pe.matmul(bank[merge_bank(c)][:, j * P:(j + 1) * P], tv1[:, blk + j, :],
                                   gdiag[:, 8 * g:8 * g + 8, :].rearrange("p b x -> p (b x)"),
                                   start=True, stop=True)
                mm.then_inc(merged_pe, 1)

            def merge_w2(c):
                after(pe, merged_dve, c - 3)
                for j in range(2):
                    dc, f = divmod(2 * (c - 16) + j, FCH)
                    dst, w = bank[merge_bank(c)][:, j * T:(j + 1) * T], slice(f * P, (f + 1) * P)
                    pe.matmul(dst, tv2_hi[dc][:, w], gdiag_hi, start=True, stop=False)
                    pe.matmul(dst, tv2_lo[:, dc, w], gdiag_hi, start=False, stop=False)
                    mm = pe.matmul(dst, tv2_hi[dc][:, w], gdiag_lo, start=False, stop=True)
                mm.then_inc(merged_pe, 1)

            def merge_in_tail(i):
                if i == NB + 2:
                    pe.wait_ge(hn_ready, NB)
                    gates_pe(0, bank[0])
                if i == NB + 3:
                    pe.wait_ge(gates_ready, 3)
                    pe.wait_ge(ld_tv, 16 * 2)
                for c in IN_TAIL.get(i - NB, ()):
                    merge_w1(c)

            pipeline(pe, [(turn_h, 1), (turn_n, L_TN), (turn_m, L_TM), (logits, 5), (project, 4),
                          (gate, L_GATE), (read, 6)], NB, in_tail=merge_in_tail)

            gates_pe(1, bank[5])
            pe.wait_ge(gates_ready, 6)
            for c in range(8, 8 + BEFORE_BIASES):
                merge_w1(c)
            pe.wait_ge(gates_ready, 7)
            for c in range(FCH):
                mm = pe.matmul(bank[6][:, c * NB:(c + 1) * NB], tvb1[:, c * P:(c + 1) * P], gT[:],
                               start=True, stop=True)
            mm.then_inc(biases_pe, 1)
            for q in range(4):
                after(pe, biases_ready, q)
                for b in range(4):
                    mm = pe.matmul(bank[4 + q % 2][:, b * P:(b + 1) * P], gbc[:, 4 * q + b, :], tvb2,
                                   start=True, stop=True)
                mm.then_inc(biases_pe, 1)
            for c in range(8 + BEFORE_BIASES, 16):
                merge_w1(c)
            pe.wait_ge(mT_ready, NB)
            pe.wait_ge(tv2_split, 8)
            pe.wait_ge(gdiag_split, 2)
            for c in range(16, 32):
                merge_w2(c)

            h_b, o_b = bank[0:4], bank[6:8]
            pe.wait_ge(merged_dve, 32)
            pe.wait_ge(biases_ready, 5)

            def hidden(b, u):
                after(pe, split_ready, b + 1)
                for f in range(FCH):
                    after(pe, (relu2_act, relu2_dve)[f // 2], 2 * (b - 1))
                    dst = h_b[2 * u + f // 2][:, (f % 2) * T:(f % 2 + 1) * T]
                    w = slice(f * P, (f + 1) * P)
                    pe.matmul(dst, w1b_hi[:, u, w], mTb_hi[:, u, :], start=True, stop=False)
                    pe.matmul(dst, w1b_lo[:, u, w], mTb_hi[:, u, :], start=False, stop=False)
                    mm = pe.matmul(dst, w1b_hi[:, u, w], mTb_lo[:, u, :], start=False, stop=True)
                    if f % 2 == 1:
                        mm.then_inc(hid2_ready, 1)

            def project_out(b, u):
                after(pe, res_ready, b - 1)
                after(pe, relu2_act, 2 * (b + 1))
                after(pe, relu2_dve, 2 * (b + 1))
                for k in range(2):
                    for f in range(FCH):
                        mm = pe.matmul(o_b[u][:, k * P:(k + 1) * P], hid2[:, u, f, k * P:(k + 1) * P],
                                       w2m[:, b, f, :], start=(f == 0), stop=(f == FCH - 1))
                mm.then_inc(out_ready, 1)

            pipeline(pe, [(hidden, 0), (project_out, 1)], NB, unroll=4)

        @block.scalar
        def _(act):
            act.wait_ge(prep_pe, 2)
            act.activation(tab_hi[:, 0:2, :].rearrange("p k d -> p (k d)"), bank[2][:, 0:2 * D], ACT.Copy)\
                .then_inc(prep_act, 1)
            act.wait_ge(prep_pe, 3)
            act.activation(tab_hi[:, 3, :], bank[5][:, 0:D], ACT.Copy).then_inc(prep_act, 1)

            def exponentials(b, u):
                after(act, nmax_ready, b + 1)
                after(act, probs_turned, b - 1)
                for q in range(2):
                    ins = act.activation(prob[:, u, q, :], bank[4 + u][:, q * T:(q + 1) * T], ACT.Exp,
                                         bias=nmax[:, u, q:q + 1], scale=TOK_SCALE,
                                         accum_out=psums[:, u, q:q + 1])
                ins.then_inc(probs_ready, 1)

            def copy_probT(b, u):
                after(act, probs_turned, b + 1)
                after(act, av_ready, b - 1)
                act.activation(probT[:, u].rearrange("p k q -> p (k q)"), bank[6][:], ACT.Copy)\
                    .then_inc(probT_ready, 1)

            def copy_x13T(b, u):
                after(act, x13_turned, b + 1)
                act.activation(x13[:, b, :], bank[3][:, 0:T], ACT.Identity, scale=tcol[:, 4:5])\
                    .then_inc(x13T_copied, 1)

            def round_x(c, par):
                after(act, x13T_copied, 2 * (c + 1))
                after(act, hid_ready, 4 * (c - 1))
                act.activation(x_hi[:, par, :], x13c(c), ACT.Copy).then_inc(x_hi_ready, 1)

            pipeline(act, [(copy_probT, 3), (exponentials, 2), (copy_x13T, 5)], NB,
                     in_tail=lambda i: round_x(0, 0) if i == NB + 2 else None)
            round_x(1, 1)

            def relu_b(c, par):
                for k, f in enumerate((1, 3)):
                    after(act, hid_ready, 4 * c + f + 1)
                    after(act, lo_pool, 2 * c - 1 + k)
                    act.activation(hid_act[:, k, :], bank[2 + f][:], ACT.Relu, bias=bvec[:, f:f + 1])\
                        .then_inc(relu_act, 1)
                    after(act, relu_act, 2 * c + 1 + k)
                    after(act, hid_used, 4 * (c - 1) + f + 1)
                    act.activation(hid_hi[:, f, :], hid_act[:, k, :], ACT.Copy).then_inc(hi_act, 1)

            act.wait_ge(affine_ready, 1)
            pipeline(act, [(relu_b, 2), (skip(2, round_x), 0)], NCH)

            act.wait_ge(ld_tv, 16 * 2)
            act.wait_ge(hid_ready, FCH * NCH)
            for k, part in enumerate(tv2_hi):
                act.activation(part, tv2[:, k, :], ACT.Copy).then_inc(tv2_rounded, 1)
            act.wait_ge(affine_ready, 2)
            act.wait_ge(ld_attn, 16 * 2)
            act.wait_ge(ld_later, 16 * 2)
            h_b, t_b, qk_b, v_b, l_b, r_b, g_b = bank[0:2], bank[2], bank[3], bank[4], bank[5], bank[6], bank[7]

            def norm_h(b, u):
                after(act, h_turned, b - 1)
                act.activation(hT[:, u, :], z_all[:, bass.ds(b * T, T)], ACT.Identity,
                               bias=gaff[:, 1:2], scale=gaff[:, 0:1]).then_inc(hT_ready, 1)

            def norm_n(b, u):
                after(act, shift1_ready, b + 1)
                after(act, n_turned, b - 1)
                for k in range(2):
                    ins = act.activation(n_s[:, u, k * P:(k + 1) * P], h_b[u][:, k * P:(k + 1) * P],
                                         ACT.Identity, bias=nm1[:, u, k:k + 1], scale=rs1[:, u, k:k + 1])
                ins.then_inc(n_ready, 1)

            def copy_nT(b, u):
                after(act, n_turned, b + 1)
                after(act, m_turned, b + 1 - (L_TM - L_TN))
                after(act, qkv_ready, b - 1)
                act.activation(nT[:, u, :], t_b[:, 0:T], ACT.Copy).then_inc(nT_ready, 1)

            def bias_qk(b, u):
                after(act, qkv_ready, b + 1)
                after(act, logits_ready, b - 1)
                for k in range(2):
                    ins = act.activation(qk_s[:, u, k, :], qk_b[:, k * T:(k + 1) * T], ACT.Identity,
                                         bias=acol[:, k:k + 1])
                ins.then_inc(qk2_copied, 1)

            def exponentials_c(b, u):
                after(act, ncmax_ready, b + 1)
                after(act, read_ready, b - 1)
                pr = prob[:, u].rearrange("p k t -> p (k t)")
                act.activation(pr[:, 0:T], l_b[:, 0:T], ACT.Exp, bias=nmax[:, u, 0:1],
                               accum_out=psums[:, u, 0:1])
                act.activation(pr[:, T:T + P], l_b[:, T:T + P], ACT.Exp, bias=nmax[:, u, 1:2],
                               accum_out=psums[:, u, 1:2]).then_inc(cprobs_ready, 1)

            def copy_mT(b, u):
                after(act, m_turned, b + 1)
                act.activation(mT[:, b, :], t_b[:, T:2 * T], ACT.Copy).then_inc(mT_ready, 1)

            def relu_gate(b, u):
                after(act, gate_ready, b + 1)
                act.activation(gjunk[:], g_b[:, 0:T], ACT.Relu, bias=gcol[:, 0:1],
                               accum_out=ghsum[:, bass.ds(b, 1)]).then_inc(gate_summed, 1)

            pipeline(act, [(norm_h, 0), (norm_n, 2), (copy_nT, 3), (copy_mT, 9), (exponentials_c, 5),
                           (bias_qk, 4), (relu_gate, 10)], NB)

            act.wait_ge(biases_ready, 1)

            def round_d(b, u):
                after(act, hid2_ready, 2 * (b - 1))
                if isinstance(b, int) and b < 2:
                    act.wait_ge(merged_pe, 24 + 4 * b)
                act.activation(mTb_hi[:, u, :], mT[:, b, :], ACT.Copy).then_inc(hi_ready, 1)
                act.activation(w1b_hi[:, u, :], w1m[:, b, :], ACT.Copy).then_inc(hi_ready, 1)

            def relu_d(b, u):
                for f in range(2):
                    after(act, hid2_ready, 2 * b + 1)
                    after(act, out_ready, b - 1)
                    act.activation(hid2[:, u, f, :], bank[2 * u][:, f * T:(f + 1) * T], ACT.Relu,
                                   bias=b1m[:, f, bass.ds(b, 1)]).then_inc(relu2_act, 1)

            act.wait_ge(merged_dve, 16)
            pipeline(act, [(round_d, 0), (relu_d, 1)], NB, unroll=4)

        @block.vector
        def _(dve):
            add, mult, sub = ALU.add, ALU.mult, ALU.subtract
            flat = lambda t: t.rearrange("p k d -> p (k d)")
            dve.wait_ge(ld_tok2, 16)
            dve.tensor_copy(bvbc, tcol[:, 2:3].to_broadcast([P, P]))
            dve.wait_ge(prep_pe, 1)
            dve.tensor_copy(wvo, bank[1][:, 0:D]).then_inc(prep_dve, 1)
            dve.tensor_copy(tab_hi[:, 2, :], emb).then_inc(prep_dve, 1)
            dve.wait_ge(prep_act, 1)
            dve.tensor_tensor(tab_lo[:, 0:2, :].rearrange("p k d -> p (k d)"), bank[2][:, 0:2 * D],
                              tab_hi[:, 0:2, :].rearrange("p k d -> p (k d)").bitcast(F32), sub)
            dve.wait_ge(prep_dve, 2)
            dve.tensor_tensor(tab_lo[:, 2, :], emb, tab_hi[:, 2, :].bitcast(F32), sub).then_inc(prep_dve, 1)
            dve.wait_ge(prep_act, 2)
            dve.tensor_tensor(tab_lo[:, 3, :], bank[5][:, 0:D], tab_hi[:, 3, :].bitcast(F32), sub)\
                .then_inc(prep_dve, 1)
            dve.wait_ge(prep_pe, 4)
            for k in range(2):
                dve.tensor_scalar(c_qk[:, k, :], bank[3][:, k * T:(k + 1) * T], tcol[:, k:k + 1], None, add)
            dve.wait_ge(ld_rows, 16)
            dve.wait_ge(ld_codes, 16)
            for k in range(2):
                dve.tensor_tensor(c_xv[:, k, 0, :], pe_code[:, k * P:(k + 1) * P], bo_bc, add)
            dve.wait_ge(prep_pe, 5)
            for k in range(2):
                ins = dve.tensor_copy(c_xv[:, k, 1, :], bank[4][:, k * D:(k + 1) * D])
            ins.then_inc(prep_dve, 1)

            dve.wait_ge(prep_dve, 5)

            def copy_qk(b, u):
                after(dve, qk_gathered, b + 1)
                after(dve, scores_ready, b - 1)
                dve.tensor_tensor(qk_s[:, u].rearrange("p k t -> p (k t)"), bank[u][:],
                                  flat(c_qk), add).then_inc(qk_copied, 1)

            def copy_xv(b, u):
                after(dve, xv_gathered, b + 1)
                dve.tensor_tensor(xv_all[:, b, :], bank[2][:],
                                  c_xv.rearrange("p k j d -> p (k j d)"), add).then_inc(xv_copied, 1)

            def row_max(b, u):
                after(dve, scores_ready, b + 1)
                after(dve, nmax_ready, b - 1)
                dve.tensor_reduce(rmax[:, u, :], bank[4 + u][:].rearrange("p (q k) -> p q k", q=2),
                                  AX.X, ALU.max).then_inc(rmax_ready, 1)

            def scaled_max(b, u):
                after(dve, rmax_ready, b + 1)
                after(dve, probs_ready, b - 1)
                dve.tensor_scalar(nmax[:, u, :], rmax[:, u, :], -TOK_SCALE, None, mult)\
                    .then_inc(nmax_ready, 1)

            def invert_sums(b, u):
                after(dve, probs_ready, b + 1)
                after(dve, x13_ready, b - 1)
                dve.reciprocal(rsum[:, u, :], psums[:, u, :]).then_inc(rsum_ready, 1)

            def residual_a(b, u):
                after(dve, rsum_ready, b + 1)
                after(dve, xv_copied, b + 1)
                after(dve, av_ready, b + 1)
                after(dve, x13_turned, b - 1)
                for q in range(2):
                    ins = dve.scalar_tensor_tensor(x13_s[:, u, q * P:(q + 1) * P], bank[7][:, q * P:(q + 1) * P],
                                                   rsum[:, u, q:q + 1], xv_all[:, b, q * T:q * T + P],
                                                   mult, add)
                ins.then_inc(x13_ready, 1)

            def stats_a(b, u):
                held_until(dve, x13_ready, b + 1)
                dve.bn_stats(stats[:, b, :], x13_s[:, u, :]).then_inc(bn_global_ready, 1)

            def hidden_parts():
                dve.wait_ge(bparts_pe, 1)
                src = bank[4][:, 0:2 * FCH].rearrange("p (f k) -> p k f", k=2)
                dve.tensor_copy(bparts[:, 0, 0:FCH], src[:, 0, :])
                dve.tensor_tensor(bparts[:, 1, 0:FCH], src[:, 1, :], tb1[:], add)
                dve.tensor_copy(obase[:, 0:1], tcol[:, 4:5])
                dve.tensor_tensor(obase[:, 1:2], tcol[:, 5:6], tcol[:, 3:4], add).then_inc(bparts_dve, 1)

            pipeline(dve, [(invert_sums, 3), (row_max, 2), (scaled_max, 2), (stats_a, 5), (copy_xv, 0),
                           (residual_a, 4), (copy_qk, 0)], NB)

            def global_std(r, n, eps, meanwhile=(lambda: None, lambda: None)):
                dve.wait_ge(bn_global_ready, NB * r + n)
                dve.bn_aggr(gstat[:, 0:2], stats[:, 0:n, :].rearrange("p b s -> p (b s)")).then_inc(stat_dve, 1)
                meanwhile[0]()
                dve.wait_ge(stat_dve, 3 * r + 1)
                dve.wait_ge(stat_pe, 2 * r + 1)
                dve.tensor_tensor(gstat[:, 3:4], gstat[:, 0:1], bank[7][:, 0:1], sub).then_inc(stat_own, 1)
                dve.wait_ge(stat_own, 3 * r + 1)
                dve.scalar_tensor_tensor(gstat[:, 4:5], gstat[:, 3:4], gstat[:, 3:4], gstat[:, 1:2], mult, add)\
                    .then_inc(stat_dve, 1)
                dve.tensor_tensor(gstat[:, 2:3], gstat[:, 3:4], gstat[:, 0:1], sub).then_inc(stat_own, 1)
                dve.wait_ge(stat_pe, 2 * r + 2)
                dve.tensor_scalar(gstat[:, 5:6], bank[7][:, 1:2], COUNT / (COUNT - 1.0), None, mult)\
                    .then_inc(stat_dve, 1)
                meanwhile[1]()
                dve.wait_ge(stat_pool, r + 1)
                dve.tensor_scalar(gstat[:, 7:8], gstat[:, 6:7], eps, None, add).then_inc(stat_own, 1)
                dve.wait_ge(stat_own, 3 * r + 3)

            def prepare_later():
                dve.wait_ge(bparts_pe, 2)
                dve.tensor_tensor(bparts[:, :, FCH], bank[5][:, 0:2], obase[:], add)
                dve.tensor_tensor(flat(lng), flat(lnp), bank[5][:, 2 * D:4 * D], add).then_inc(bparts_dve, 1)

            global_std(0, NB, STD_EPS, (hidden_parts, prepare_later))
            dve.wait_ge(bparts_dve, 2)
            dve.tensor_scalar(bvec[:], bparts[:, 1, :], gstat[:, 7:8], None, mult).then_inc(bparts_dve, 1)
            dve.wait_ge(bparts_dve, 3)
            dve.scalar_tensor_tensor(bvec[:], bparts[:, 0, :], gstat[:, 2:3], bvec[:], mult, add)\
                .then_inc(affine_ready, 1)
            dve.wait_ge(affine_ready, 1)
            dve.tensor_scalar(nbvec[:], bvec[:, 0:FCH], -1.0, None, mult).then_inc(bparts_dve, 1)
            dve.tensor_scalar(gaff[:, 2:3], gstat[:, 7:8], STD_EPS, None, mult).then_inc(bparts_dve, 1)
            dve.wait_ge(bparts_dve, 5)

            def relu_b(c, par):
                for k, f in enumerate((0, 2)):
                    after(dve, hid_ready, 4 * c + f + 1)
                    after(dve, hid_used, 4 * (c - 1) + f + 1)
                    dve.tensor_scalar(hid_hi[:, f, :], bank[2 + f][:], nbvec[:, f:f + 1], None, ALU.max)\
                        .then_inc(hi_dve, 1)
                    after(dve, hi_dve, 2 * c + 1 + k)
                    dve.scalar_tensor_tensor(hid_lo[:, f, :], bank[2 + f][:], nbvec[:, f:f + 1],
                                             hid_hi[:, f, :].bitcast(F32), ALU.max, sub).then_inc(lo_dve, 1)

            def residual_b(c, par):
                after(dve, hid_used, 4 * (c + 1))
                dve.scalar_tensor_tensor(z_all[:, bass.ds(c * CH, CH)], bank[6 + par][:], bvec[:, FCH:FCH + 1],
                                         x13c(c), add, add).then_inc(z_ready, 1)

            def stats_b(c, par):
                held_until(dve, z_ready, c + 1)
                dve.bn_stats(stats[:, c, :], z_all[:, bass.ds(c * CH, CH)]).then_inc(bn_global_ready, 1)

            pipeline(dve, [(relu_b, 0), (residual_b, 1), (stats_b, 1)], NCH)
            global_std(1, NCH, gaff[:, 2:3])
            dve.reciprocal(gstat[:, 8:9], gstat[:, 7:8]).then_inc(bparts_dve, 1)
            dve.wait_ge(bparts_dve, 6)
            dve.tensor_scalar(gaff[:, 0:1], tcol[:, 4:5], gstat[:, 8:9], None, mult).then_inc(bparts_dve, 1)
            dve.wait_ge(bparts_dve, 7)
            dve.scalar_tensor_tensor(gaff[:, 1:2], gstat[:, 2:3], gaff[:, 0:1], tcol[:, 5:6], mult, add)\
                .then_inc(affine_ready, 1)

            dve.wait_ge(ld_attn, 16 * 2)
            h_b, t_b, qk_b, v_b, l_b, r_b, g_b = bank[0:2], bank[2], bank[3], bank[4], bank[5], bank[6], bank[7]

            def row_stats(src, bn, u, done):
                dve.nop(nofuse=True)
                for k in range(2):
                    ins = dve.bn_stats(bn[:, u, k, :], src[k])
                ins.then_inc(done, 1)

            def row_aggregate(bn, mv, u, b, started, done):
                held_until(dve, started, b + 1)
                for k in range(2):
                    ins = dve.bn_aggr(mv[:, u, k, :], bn[:, u, k, :])
                ins.then_inc(done, 1)

            def stats_h(b, u):
                after(dve, h_turned, b + 1)
                row_stats([h_b[u][:, 0:P], h_b[u][:, P:T]], bn1, u, bn1_ready)

            def aggregate_h(b, u):
                after(dve, shift1_ready, b - 1)
                row_aggregate(bn1, mv1, u, b, bn1_ready, aggr1_ready)

            def shift_h(b, u):
                after(dve, rstd1_ready, b + 1)
                after(dve, n_ready, b - 1)
                dve.scalar_tensor_tensor(nm1[:, u, :], mv1[:, u, :, 0], -1.0, rs1[:, u, :],
                                         mult, mult).then_inc(shift1_ready, 1)

            def add_hn(b, u):
                after(dve, n_ready, b + 1)
                dve.tensor_tensor(res2[:, b, :], h_b[u][:, 0:T], n_s[:, u, :], add).then_inc(hn_ready, 1)

            def bias_v(b, u):
                after(dve, qkv_ready, b + 1)
                after(dve, vp_ready, b - 1)
                dve.tensor_tensor(v_s[:, u, :], v_b[:, 0:T], abv, add).then_inc(v_copied, 1)

            def column_max(b, u):
                after(dve, logits_ready, b + 1)
                after(dve, ncmax_ready, b - 1)
                dve.tensor_reduce(rmax[:, u, 0:1], l_b[:, 0:T], AX.X, ALU.max)
                dve.tensor_reduce(rmax[:, u, 1:2], l_b[:, T:T + P], AX.X, ALU.max).then_inc(cmax_ready, 1)

            def negate_max(b, u):
                after(dve, cmax_ready, b + 1)
                after(dve, cprobs_ready, b - 1)
                dve.tensor_scalar(nmax[:, u, :], rmax[:, u, :], -1.0, None, mult).then_inc(ncmax_ready, 1)

            def invert_sums_c(b, u):
                after(dve, cprobs_ready, b + 1)
                after(dve, vp_ready, b - 1)
                dve.reciprocal(rsum[:, u, :], psums[:, u, :]).then_inc(csum_ready, 1)

            def scale_v(b, u):
                after(dve, csum_ready, b + 1)
                after(dve, v_copied, b + 1)
                after(dve, read_ready, b - 1)
                for k in range(2):
                    ins = dve.tensor_scalar(vp_s[:, u, k * P:(k + 1) * P], v_s[:, u, k * P:(k + 1) * P],
                                            rsum[:, u, k:k + 1], INV_SQRT_K, mult, mult)
                ins.then_inc(vp_ready, 1)

            def residual_c(b, u):
                after(dve, read_ready, b + 1)
                after(dve, hn_ready, b + 1)
                dve.tensor_tensor(res2[:, b, :], r_b[:, 0:T], res2[:, b, :], add).then_inc(h2_ready, 1)

            def stats_h2(b, u):
                after(dve, h2_ready, b + 1)
                row_stats([res2[:, b, 0:P], res2[:, b, P:T]], bn2, u, bn2_ready)

            def aggregate_h2(b, u):
                row_aggregate(bn2, mv2, u, b, bn2_ready, aggr2_ready)

            def norm_m(b, u):
                after(dve, rstd2_ready, b + 1)
                after(dve, m_turned, b - 1)
                after(dve, m_kept, b - 1)
                for k in range(2):
                    ins = dve.tensor_scalar(x13_s[:, u, k * P:(k + 1) * P], res2[:, b, k * P:(k + 1) * P],
                                            mv2[:, u, k, 0:1], rs2[:, u, k:k + 1], sub, mult)
                ins.then_inc(m_ready, 1)

            def gates_dve(g, src):
                b = slice(8 * g, 8 * g + 8)
                dve.wait_ge(g_pe, g + 1)
                dve.tensor_scalar(grep[:, b], src[:, 0:8], 1.0 / T, gcol[:, 1:2], mult, add)\
                    .then_inc(gates_ready, 1)
                dve.tensor_scalar(gT[:, b], src[0:E, 8:16], 1.0 / T, gb2[:, 0:1], mult, add)\
                    .then_inc(gates_ready, 1)
                dve.wait_ge(gates_ready, 3 * g + 2)
                dve.tensor_tensor(gdiag[:, b, :], grep[:, b].unsqueeze(2).to_broadcast([P, 8, X]),
                                  diag.unsqueeze(1).to_broadcast([P, 8, X]), mult).then_inc(gates_ready, 1)

            def merged(c):
                dve.wait_ge(merged_pe, c + 1)
                if c < 16:
                    b, f0 = slice(c // 8 * 8, c // 8 * 8 + 8), c % 8 * 4 * X
                    src = bank[merge_bank(c)][:].rearrange("p (j b x) -> p j b x", j=4, b=8)
                    dst = w1m[:, b, f0:f0 + 4 * X].rearrange("p b (j x) -> p j b x", j=4)
                    base = fw1T[:, f0:f0 + 4 * X].rearrange("p (j x) -> p j x", j=4)
                    base = base.unsqueeze(2).to_broadcast([P, 4, 8, X])
                else:
                    dc, f = 2 * (c - 16) // FCH, 2 * (c - 16) % FCH
                    src = bank[merge_bank(c)][:].rearrange("p (j b x) -> p j b x", j=2, b=NB)
                    dst = w2m[:, :, f:f + 2, dc * X:(dc + 1) * X].rearrange("p b j x -> p j b x")
                    base = fw2T[:, f:f + 2, dc * X:(dc + 1) * X].unsqueeze(2).to_broadcast([P, 2, NB, X])
                dve.tensor_tensor(dst, src, base, add).then_inc(merged_dve, 1)

            def merge_in_tail(i):
                if i == NB + 2:
                    gates_dve(0, bank[0])
                for c in IN_TAIL.get(i - NB, ()):
                    merged(c)

            pipeline(dve, [(residual_c, 7), (shift_h, 2), (invert_sums_c, 6), (stats_h, 1), (scale_v, 6),
                           (aggregate_h, 1), (column_max, 5), (stats_h2, 7), (negate_max, 5),
                           (aggregate_h2, 7), (add_hn, 2), (norm_m, 8),
                           (bias_v, 4)], NB, in_tail=merge_in_tail, tail=L_GATE)

            gates_dve(1, bank[5])
            dve.tensor_copy(gbc, gT[:].unsqueeze(2).to_broadcast([E, NB, P])).then_inc(gates_ready, 1)
            for c in range(8, 8 + BEFORE_BIASES):
                merged(c)
            dve.wait_ge(biases_pe, 1)
            dve.tensor_tensor(b1m[:], bank[6][:, 0:FCH * NB].rearrange("p (c b) -> p c b", c=FCH),
                              fb1.unsqueeze(2).to_broadcast([P, FCH, NB]), add).then_inc(biases_ready, 1)
            for q in range(4):
                dve.wait_ge(biases_pe, 2 + q)
                dve.tensor_tensor(b2m[:, 4 * q:4 * q + 4, :], bank[4 + q % 2][:].rearrange("p (b d) -> p b d", b=4),
                                  fb2.unsqueeze(1).to_broadcast([P, 4, D]), add).then_inc(biases_ready, 1)
            dve.wait_ge(gates_ready, 6)
            dve.tensor_copy(gdiag_hi, gdiag[:].rearrange("p b x -> p (b x)")).then_inc(gdiag_split, 1)
            dve.wait_ge(gdiag_split, 1)
            dve.tensor_tensor(gdiag_lo, gdiag[:].rearrange("p b x -> p (b x)"), gdiag_hi.bitcast(F32), sub)\
                .then_inc(gdiag_split, 1)
            for c in range(8 + BEFORE_BIASES, 32):
                merged(c)

            def relu_d(b, u):
                for f in range(2, 4):
                    after(dve, hid2_ready, 2 * b + 2)
                    after(dve, out_ready, b - 1)
                    dve.tensor_scalar(hid2[:, u, f, :], bank[2 * u + 1][:, (f - 2) * T:(f - 1) * T],
                                      b1m[:, f, bass.ds(b, 1)], 0.0, add, ALU.max).then_inc(relu2_dve, 1)

            def residual_d(b, u):
                if isinstance(b, int) and b == 0:
                    dve.wait_ge(mb_ready, NB)
                    dve.wait_ge(hlb_ready, NB)
                after(dve, out_ready, b + 1)
                dve.tensor_tensor(r_s[:, u, :], bank[6 + u][:, 0:T], x13[:, b, :], add).then_inc(res_ready, 1)

            def stats_d(b, u):
                after(dve, res_ready, b + 1)
                row_stats([r_s[:, u, 0:P], r_s[:, u, P:T]], bn1, u, bn3_ready)

            def aggregate_d(b, u):
                row_aggregate(bn1, mv1, u, b, bn3_ready, aggr3_ready)

            def center(b, u):
                after(dve, aggr3_ready, b + 1)
                for k in range(2):
                    ins = dve.scalar_tensor_tensor(ln_s[:, u, k * P:(k + 1) * P], r_s[:, u, k * P:(k + 1) * P],
                                                   mv1[:, u, k, 0:1], lng[:, 0, :], sub, mult)
                ins.then_inc(scaled_ready, 1)

            def finish(b, u):
                after(dve, scaled_ready, b + 1)
                after(dve, rstd3_ready, b + 1)
                after(dve, stored[u], 8 * (b - u))
                for k in range(2):
                    ins = dve.scalar_tensor_tensor(o_s[:, u, k * P:(k + 1) * P], ln_s[:, u, k * P:(k + 1) * P],
                                                   rs1[:, u, k:k + 1], res2[:, b, k * P:(k + 1) * P],
                                                   mult, add)
                ins.then_inc(o_ready, 1)

            pipeline(dve, [(relu_d, 0), (residual_d, 1), (center, 2), (stats_d, 1), (finish, 2),
                           (aggregate_d, 1)], NB, unroll=4)

        @block.gpsimd
        def _(pool):
            pool.memset(nhalf[:, 0:2], -0.5)
            pool.memset(nhalf[:, 2:4], 0.5).then_inc(pool_const, 1)
            pool.wait_ge(ld_tok2, 16)

            def one_hot(b, u):
                after(pool, xv_gathered, b - 1)
                pool.tensor_scalar(onehot[:, u, :], ids[:, b * T:(b + 1) * T],
                                   of_tables("iota"), None, ALU.is_equal).then_inc(onehot_ready, 1)

            for b in range(NB):
                if b in ID_ENDS:
                    pool.wait_ge(ld_ids[ID_ENDS.index(b)], 16)
                one_hot(b, b % 2)
            pool.wait_ge(ld_ffn, 16)
            pool.tensor_copy(w1_hi[:], w1s).then_inc(prep_pool, 1)
            pool.wait_ge(prep_pool, 1)
            pool.tensor_tensor(w1_lo[:], w1s, w1_hi[:].bitcast(F32), ALU.subtract).then_inc(prep_pool, 1)
            pool.tensor_copy(w2_hi[:], w2f).then_inc(prep_pool, 1)
            pool.wait_ge(prep_pool, 3)
            pool.tensor_tensor(w2_lo[:], w2f, w2_hi[:].bitcast(F32), ALU.subtract).then_inc(prep_pool, 1)
            pool.wait_ge(ld_later, 16 * 2)
            pool.wait_ge(ld_rows, 16)
            pool.tensor_tensor(tvd, tvln, lnp[0:E, :, :], ALU.subtract).then_inc(prep_pool, 1)
            pool.wait_ge(ld_const, 16)
            pool.tensor_copy(ident_b[:], ident)
            pool.memset(maskT[:], 0.0).then_inc(pool_const, 1)
            pool.wait_ge(pool_const, 2)
            pool.affine_select(out=maskT[:], in_=maskT[:], compare_op=ALU.is_ge, fill=MASKED, base=0,
                               pattern=[[1, P]], channel_multiplier=-1).then_inc(pool_const, 1)

            def root(r):
                pool.wait_ge(stat_dve, 3 * r + 3)
                pool.tensor_tensor(gstat[:, 6:7], gstat[:, 5:6], nhalf[:, 2:3], ALU.pow).then_inc(stat_pool, 1)

            def split_x(c, par):
                after(pool, x_hi_ready, c + 1)
                after(pool, hid_ready, 4 * (c - 1))
                pool.tensor_tensor(x_lo[:, par, :], x13c(c), x_hi[:, par, :].bitcast(F32),
                                   ALU.subtract).then_inc(x_lo_ready, 1)

            def split_hidden(c, par):
                for k, f in enumerate((1, 3)):
                    after(pool, hi_act, 2 * c + 1 + k)
                    after(pool, hid_used, 4 * (c - 1) + f + 1)
                    pool.tensor_tensor(hid_lo[:, f, :], hid_act[:, k, :], hid_hi[:, f, :].bitcast(F32),
                                       ALU.subtract).then_inc(lo_pool, 1)

            split_x(0, 0)
            split_x(1, 1)
            root(0)
            pipeline(pool, [(split_hidden, 2), (skip(2, split_x), 0)], NCH)
            def split_tv2(k):
                pool.wait_ge(tv2_rounded, k + 1)
                pool.tensor_tensor(tv2_lo[:, k, :], tv2[:, k, :], tv2_hi[k].bitcast(F32), ALU.subtract)\
                    .then_inc(tv2_split, 1)

            split_tv2(0)
            split_tv2(1)
            root(1)
            split_tv2(2)
            split_tv2(3)

            def split_more(b, u):
                if isinstance(b, int) and b in (1, 3, 5, 7):
                    split_tv2(4 + b // 2)

            def rstd_h(b, u):
                held_until(pool, aggr1_ready, b + 1)
                pool.tensor_scalar(ve1[:, u, :], mv1[:, u, :, 1], LN_EPS, None, ALU.add).then_inc(var1_ready, 1)
                after(pool, var1_ready, b + 1)
                after(pool, n_ready, b - 1)
                pool.tensor_tensor(rs1[:, u, :], ve1[:, u, :], nhalf[:, 0:2], ALU.pow).then_inc(rstd1_ready, 1)

            def rstd_h2(b, u):
                held_until(pool, aggr2_ready, b + 1)
                pool.tensor_scalar(ve2[:, u, :], mv2[:, u, :, 1], LN_EPS, None, ALU.add).then_inc(var2_ready, 1)
                after(pool, var2_ready, b + 1)
                after(pool, m_ready, b - 1)
                pool.tensor_tensor(rs2[:, u, :], ve2[:, u, :], nhalf[:, 0:2], ALU.pow).then_inc(rstd2_ready, 1)

            def keep_m(b, u):
                after(pool, m_ready, b + 1)
                pool.tensor_copy(x13[:, b, :], x13_s[:, u, :]).then_inc(m_kept, 1)

            pipeline(pool, [(rstd_h2, 7), (keep_m, 8), (rstd_h, 0), (split_more, 0)], NB)

            pool.wait_ge(bparts_dve, 2)
            pool.wait_ge(h2_ready, NB)
            pool.wait_ge(m_ready, NB)
            twice = lambda t: t.rearrange("p (k d) -> p k d", k=2)
            with pool.Fori(0, NB) as b:
                pool.tensor_tensor(twice(res2[:, b, :]), twice(res2[:, b, :]),
                                   lng[:, 1, :].unsqueeze(1).to_broadcast([P, 2, D]), ALU.add).then_inc(hlb_ready, 1)
            pool.wait_ge(m_kept, NB)
            pool.wait_ge(biases_ready, 5)
            with pool.Fori(0, NB) as b:
                pool.tensor_tensor(twice(x13[:, b, :]), twice(x13[:, b, :]),
                                   b2m[:, b, :].unsqueeze(1).to_broadcast([P, 2, D]), ALU.add).then_inc(mb_ready, 1)

            def split_d(b, u):
                after(pool, hi_ready, 2 * b + 1)
                after(pool, hid2_ready, 2 * (b - 1))
                pool.tensor_tensor(mTb_lo[:, u, :], mT[:, b, :], mTb_hi[:, u, :].bitcast(F32), ALU.subtract)
                after(pool, hi_ready, 2 * b + 2)
                pool.tensor_tensor(w1b_lo[:, u, :], w1m[:, b, :], w1b_hi[:, u, :].bitcast(F32),
                                   ALU.subtract).then_inc(split_ready, 1)

            def rstd_d(b, u):
                held_until(pool, aggr3_ready, b + 1)
                pool.tensor_scalar(ve1[:, u, :], mv1[:, u, :, 1], LN_EPS, None, ALU.add).then_inc(var3_ready, 1)
                after(pool, var3_ready, b + 1)
                after(pool, o_ready, b - 1)
                pool.tensor_tensor(rs1[:, u, :], ve1[:, u, :], nhalf[:, 0:2], ALU.pow).then_inc(rstd3_ready, 1)

            pipeline(pool, [(split_d, 0), (rstd_d, 3)], NB, unroll=4)


def kernel(**inputs):
    import concourse.bacc as bacc
    from concourse.bass_utils import run_bass_kernel_spmd

    nc = bacc.Bacc("TRN2", target_bir_lowering=False, num_devices=1)
    arrays = lay_out({n: np.asarray(v) for n, v in inputs.items()})
    args = {n: nc.dram_tensor(f"in_{n}", v.shape, mybir.dt.from_np(v.dtype), kind="ExternalInput").ap()
            for n, v in arrays.items()}
    features = inputs["L0_tok_emb"].shape[1]
    out = nc.dram_tensor("out", (*inputs["x"].shape, features), F32, kind="ExternalOutput").ap()
    build(nc, args, out)
    r = run_bass_kernel_spmd(nc, [{f"in_{n}": v for n, v in arrays.items()}], core_ids=[0])
    return r.results[0]["out"]
```
